# Optimizing a Trainium2 kernel written in Bass

```python
import numpy as np
import jax
import jax.numpy as jnp

def _softmax(x, axis=-1):
    return jax.nn.softmax(x, axis=axis)

def _gelu(x):
    return jax.nn.gelu(x, approximate=True)

def _silu(x):
    return jax.nn.silu(x)

def _sigmoid(x):
    return jax.nn.sigmoid(x)

def _layernorm(x, axis=-1, eps=1e-05):
    m = jnp.mean(x, axis=axis, keepdims=True)
    v = jnp.var(x, axis=axis, keepdims=True)
    return (x - m) / jnp.sqrt(v + eps)

def _scatter_add(tgt, idx, src, axis=0):
    return tgt.at[idx].add(src)

def _segment_sum(src, seg, n):
    return jax.ops.segment_sum(src, seg, n)
kernel_name = 'mk_prb_d2_jaxref_r8_1d0697'

def setup_inputs(seed: int=0):
    np.random.seed(seed)
    _w = jnp.asarray

    def _L0_attn_setup():
        import jax, jax.numpy as jnp
        import numpy as np
        import math
        DIM, DIM_QK, DIM_V = (128, 128, 128)
        NUM_BUCKETS, MAX_DISTANCE = (32, 128)

        def silu(x):
            return x * jax.nn.sigmoid(x)

        def laplacian_attn_fn(x):
            mu = math.sqrt(0.5)
            std = math.sqrt(0.25 * math.pi)
            return (1.0 + jax.lax.erf((x - mu) / (std * math.sqrt(2.0)))) * 0.5

        def rel_pos_bias(seq_len, table, scale):
            q_pos = jnp.arange(seq_len)
            k_pos = jnp.arange(seq_len)
            rel_pos = k_pos[None, :] - q_pos[:, None]
            n = jnp.maximum(-rel_pos, 0)
            max_exact = NUM_BUCKETS // 2
            is_small = n < max_exact
            n_safe = jnp.maximum(n, 1).astype(jnp.float32)
            val_if_large = max_exact + (jnp.log(n_safe / max_exact) / math.log(MAX_DISTANCE / max_exact) * (NUM_BUCKETS - max_exact)).astype(jnp.int32)
            val_if_large = jnp.minimum(val_if_large, NUM_BUCKETS - 1)
            bucket = jnp.where(is_small, n, val_if_large)
            return table[bucket] * scale
        key = jax.random.key(seed)
        ks = jax.random.split(key, 8)
        B, S = (4, 256)
        lin_std_qk = 1.0 / math.sqrt(DIM)
        return {'x': jax.random.normal(ks[0], (B, S, DIM), dtype=jnp.float32), 'wqk': jax.random.uniform(ks[1], (DIM, DIM_QK), minval=-lin_std_qk, maxval=lin_std_qk, dtype=jnp.float32), 'bqk': jnp.zeros((DIM_QK,), dtype=jnp.float32), 'gamma': 1.0 + 0.02 * jax.random.normal(ks[2], (2, DIM_QK), dtype=jnp.float32), 'beta': jnp.zeros((2, DIM_QK), dtype=jnp.float32), 'wv': jax.random.uniform(ks[3], (DIM, DIM_V), minval=-lin_std_qk, maxval=lin_std_qk, dtype=jnp.float32), 'bv': jnp.zeros((DIM_V,), dtype=jnp.float32), 'rel_bias': jax.random.normal(ks[4], (NUM_BUCKETS,), dtype=jnp.float32)}
    _L0_attn_in = _L0_attn_setup()

    def _L0_ffn_setup():
        import jax, jax.numpy as jnp
        import numpy as np
        DIM = 128
        LATENT = 64
        INTER = 64
        SHARED = 512
        E = 8
        TOPK = 2
        NGROUP = 2
        TOPKG = 1
        NORM_TOPK = True
        SCALE = 1.0
        B, S = (2, 128)

        def relu2(x):
            r = jnp.maximum(x, 0.0)
            return r * r
        key = jax.random.key(seed)
        ks = jax.random.split(key, 8)

        def w(k, shape, std=0.02):
            return jax.random.normal(k, shape, dtype=jnp.float32) * std
        return {'x': jax.random.normal(ks[0], (B, S, DIM), dtype=jnp.float32), 'gate': w(ks[1], (E, DIM)), 'corr_bias': jnp.zeros((E,), jnp.float32), 'w1': w(ks[2], (E, INTER, LATENT)), 'w2': w(ks[3], (E, LATENT, INTER)), 'fc1_w': w(ks[4], (LATENT, DIM)), 'fc2_w': w(ks[5], (DIM, LATENT)), 'up_w': w(ks[6], (SHARED, DIM)), 'down_w': w(ks[7], (DIM, SHARED))}
    _L0_ffn_in = _L0_ffn_setup()

    def _L1_attn_setup():
        import jax, jax.numpy as jnp
        import numpy as np
        D_MODEL = 128
        N_HEADS = 16
        HEAD_DIM = D_MODEL // N_HEADS
        ROPE_BASE = 10000.0

        def _rope_tables(T, dtype=jnp.float32):
            half = HEAD_DIM // 2
            inv_freq = 1.0 / ROPE_BASE ** (jnp.arange(0, HEAD_DIM, 2, dtype=jnp.float32) / HEAD_DIM)
            t = jnp.arange(T, dtype=jnp.float32)
            freqs = jnp.einsum('i,j->ij', t, inv_freq)
            return (jnp.cos(freqs).astype(dtype), jnp.sin(freqs).astype(dtype))

        def _apply_rotary(x, cos, sin):
            B, T, H, D = x.shape
            xr = x.reshape(B, T, H, D // 2, 2)
            x0, x1 = (xr[..., 0], xr[..., 1])
            c = cos[None, :, None, :]
            s = sin[None, :, None, :]
            out = jnp.stack([x0 * c - x1 * s, x0 * s + x1 * c], axis=-1)
            return out.reshape(B, T, H, D)
        key = jax.random.key(seed)
        ks = jax.random.split(key, 5)
        x = jax.random.normal(ks[0], (4, 128, D_MODEL), dtype=jnp.float32)
        init = 1.0 / np.sqrt(D_MODEL)
        Wq = jax.random.uniform(ks[1], (D_MODEL, D_MODEL), jnp.float32, -init, init)
        Wk = jax.random.uniform(ks[2], (D_MODEL, D_MODEL), jnp.float32, -init, init)
        Wv = jax.random.uniform(ks[3], (D_MODEL, D_MODEL), jnp.float32, -init, init)
        Wo = jax.random.uniform(ks[4], (D_MODEL, D_MODEL), jnp.float32, -init, init)
        return {'x': x, 'Wq': Wq, 'Wk': Wk, 'Wv': Wv, 'Wo': Wo}
    _L1_attn_in = _L1_attn_setup()

    def _L1_ffn_setup():
        import jax, jax.numpy as jnp
        import numpy as np
        B, S, D, F, E, R = (4, 256, 128, 512, 8, 4)
        key = jax.random.key(seed)
        ks = jax.random.split(key, 8)
        s_in = 1.0 / np.sqrt(D)
        s_ff = 1.0 / np.sqrt(F)
        return {'hidden_states': jax.random.normal(ks[0], (B, S, D), jnp.float32), 'gate_W': jax.random.normal(ks[1], (E, D), jnp.float32) * s_in, 'gate_b': jnp.zeros((E,), jnp.float32), 'wi_W': jax.random.normal(ks[2], (F, D), jnp.float32) * s_in, 'wi_b': jnp.zeros((F,), jnp.float32), 'wo_W': jax.random.normal(ks[3], (D, F), jnp.float32) * s_ff, 'wo_b': jnp.zeros((D,), jnp.float32), 'lora_A': jax.random.normal(ks[4], (E, R, D), jnp.float32) * s_in, 'lora_B': jax.random.normal(ks[5], (E, F, R), jnp.float32) * 0.02}
    _L1_ffn_in = _L1_ffn_setup()
    _d = {'L0_attn_x': _L0_attn_in['x'], 'L0_attn_wqk': _L0_attn_in['wqk'], 'L0_attn_bqk': _L0_attn_in['bqk'], 'L0_attn_gamma': _L0_attn_in['gamma'], 'L0_attn_beta': _L0_attn_in['beta'], 'L0_attn_wv': _L0_attn_in['wv'], 'L0_attn_bv': _L0_attn_in['bv'], 'L0_attn_rel_bias': _L0_attn_in['rel_bias'], 'L0_ffn_gate': _L0_ffn_in['gate'], 'L0_ffn_corr_bias': _L0_ffn_in['corr_bias'], 'L0_ffn_w1': _L0_ffn_in['w1'], 'L0_ffn_w2': _L0_ffn_in['w2'], 'L0_ffn_fc1_w': _L0_ffn_in['fc1_w'], 'L0_ffn_fc2_w': _L0_ffn_in['fc2_w'], 'L0_ffn_up_w': _L0_ffn_in['up_w'], 'L0_ffn_down_w': _L0_ffn_in['down_w'], 'L1_attn_Wq': _L1_attn_in['Wq'], 'L1_attn_Wk': _L1_attn_in['Wk'], 'L1_attn_Wv': _L1_attn_in['Wv'], 'L1_attn_Wo': _L1_attn_in['Wo'], 'L1_ffn_gate_W': _L1_ffn_in['gate_W'], 'L1_ffn_gate_b': _L1_ffn_in['gate_b'], 'L1_ffn_wi_W': _L1_ffn_in['wi_W'], 'L1_ffn_wi_b': _L1_ffn_in['wi_b'], 'L1_ffn_wo_W': _L1_ffn_in['wo_W'], 'L1_ffn_wo_b': _L1_ffn_in['wo_b'], 'L1_ffn_lora_A': _L1_ffn_in['lora_A'], 'L1_ffn_lora_B': _L1_ffn_in['lora_B']}
    _x0 = _d['L0_attn_x']
    _d['L0_attn_x'] = jax.random.normal(jax.random.fold_in(jax.random.key(seed), 1), (16, 512, 128), dtype=_x0.dtype)
    del _x0
    return _d

def reference(L0_attn_x, L0_attn_wqk, L0_attn_bqk, L0_attn_gamma, L0_attn_beta, L0_attn_wv, L0_attn_bv, L0_attn_rel_bias, L0_ffn_gate, L0_ffn_corr_bias, L0_ffn_w1, L0_ffn_w2, L0_ffn_fc1_w, L0_ffn_fc2_w, L0_ffn_up_w, L0_ffn_down_w, L1_attn_Wq, L1_attn_Wk, L1_attn_Wv, L1_attn_Wo, L1_ffn_gate_W, L1_ffn_gate_b, L1_ffn_wi_W, L1_ffn_wi_b, L1_ffn_wo_W, L1_ffn_wo_b, L1_ffn_lora_A, L1_ffn_lora_B):

    def _L0_attn_ref(x, wqk, bqk, gamma, beta, wv, bv, rel_bias):
        import jax, jax.numpy as jnp
        import numpy as np
        import math
        DIM, DIM_QK, DIM_V = (128, 128, 128)
        NUM_BUCKETS, MAX_DISTANCE = (32, 128)

        def silu(x):
            return x * jax.nn.sigmoid(x)

        def laplacian_attn_fn(x):
            mu = math.sqrt(0.5)
            std = math.sqrt(0.25 * math.pi)
            return (1.0 + jax.lax.erf((x - mu) / (std * math.sqrt(2.0)))) * 0.5

        def rel_pos_bias(seq_len, table, scale):
            q_pos = jnp.arange(seq_len)
            k_pos = jnp.arange(seq_len)
            rel_pos = k_pos[None, :] - q_pos[:, None]
            n = jnp.maximum(-rel_pos, 0)
            max_exact = NUM_BUCKETS // 2
            is_small = n < max_exact
            n_safe = jnp.maximum(n, 1).astype(jnp.float32)
            val_if_large = max_exact + (jnp.log(n_safe / max_exact) / math.log(MAX_DISTANCE / max_exact) * (NUM_BUCKETS - max_exact)).astype(jnp.int32)
            val_if_large = jnp.minimum(val_if_large, NUM_BUCKETS - 1)
            bucket = jnp.where(is_small, n, val_if_large)
            return table[bucket] * scale
        B, S, _ = x.shape
        qk = silu(x @ wqk + bqk)
        q = qk * gamma[0] + beta[0]
        k = qk * gamma[1] + beta[1]
        v = silu(x @ wv + bv)
        scale = 1.0 / S
        sim = jnp.einsum('bid,bjd->bij', q, k) * scale
        sim = sim + rel_pos_bias(S, rel_bias, DIM_QK ** 0.5)[None, :, :]
        attn = laplacian_attn_fn(sim)
        causal_mask = jnp.triu(jnp.ones((S, S), dtype=bool), k=1)
        attn = jnp.where(causal_mask[None, :, :], 0.0, attn)
        return jnp.einsum('bij,bjd->bid', attn, v)

    def _L0_ffn_ref(x, gate, corr_bias, w1, w2, fc1_w, fc2_w, up_w, down_w):
        import jax, jax.numpy as jnp
        import numpy as np
        DIM = 128
        LATENT = 64
        INTER = 64
        SHARED = 512
        E = 8
        TOPK = 2
        NGROUP = 2
        TOPKG = 1
        NORM_TOPK = True
        SCALE = 1.0
        B, S = (2, 128)

        def relu2(x):
            r = jnp.maximum(x, 0.0)
            return r * r
        Bv, Sv, D = x.shape
        xf = x.reshape(-1, D)
        N = xf.shape[0]
        scores = jax.nn.sigmoid(xf.astype(jnp.float32) @ gate.T)
        sfc = scores + corr_bias
        gs = E // NGROUP
        if NGROUP > 1:
            group_scores = jax.lax.top_k(sfc.reshape(N, NGROUP, gs), 2)[0].sum(-1)
            gidx = jax.lax.top_k(group_scores, TOPKG)[1]
            gmask = jnp.zeros((N, NGROUP), sfc.dtype).at[jnp.arange(N)[:, None], gidx].set(1.0)
            smask = jnp.repeat(gmask, gs, axis=1)
            sfc = jnp.where(smask > 0, sfc, 0.0)
        sel = jax.lax.top_k(sfc, TOPK)[1]
        top_scores = jnp.take_along_axis(scores, sel, axis=1)
        if NORM_TOPK:
            top_scores = top_scores / (top_scores.sum(-1, keepdims=True) + 1e-20)
        flat = sel.reshape(-1)
        perm = jnp.argsort(flat, stable=True)
        sorted_eid = flat[perm]
        scores_sorted = top_scores.reshape(-1)[perm]
        tok = perm // TOPK
        lat = xf @ fc1_w.T
        xs = lat[tok]
        out = jnp.zeros_like(xs)
        for e in range(E):
            he = relu2(xs @ w1[e].T) @ w2[e].T
            out = jnp.where((sorted_eid == e)[:, None], he, out)
        out = out * scores_sorted[:, None]
        comb = jnp.zeros((N, LATENT), out.dtype).at[tok].add(out)
        routed = comb @ fc2_w.T * SCALE
        shared = relu2(xf @ up_w.T) @ down_w.T
        return (routed + shared).reshape(Bv, Sv, D)

    def _L1_attn_ref(x, Wq, Wk, Wv, Wo):
        import jax, jax.numpy as jnp
        import numpy as np
        D_MODEL = 128
        N_HEADS = 16
        HEAD_DIM = D_MODEL // N_HEADS
        ROPE_BASE = 10000.0

        def _rope_tables(T, dtype=jnp.float32):
            half = HEAD_DIM // 2
            inv_freq = 1.0 / ROPE_BASE ** (jnp.arange(0, HEAD_DIM, 2, dtype=jnp.float32) / HEAD_DIM)
            t = jnp.arange(T, dtype=jnp.float32)
            freqs = jnp.einsum('i,j->ij', t, inv_freq)
            return (jnp.cos(freqs).astype(dtype), jnp.sin(freqs).astype(dtype))

        def _apply_rotary(x, cos, sin):
            B, T, H, D = x.shape
            xr = x.reshape(B, T, H, D // 2, 2)
            x0, x1 = (xr[..., 0], xr[..., 1])
            c = cos[None, :, None, :]
            s = sin[None, :, None, :]
            out = jnp.stack([x0 * c - x1 * s, x0 * s + x1 * c], axis=-1)
            return out.reshape(B, T, H, D)
        B, T, C = x.shape
        H, Dh = (N_HEADS, HEAD_DIM)
        scale = Dh ** (-0.5)
        q = (x @ Wq.T).reshape(B, T, H, Dh)
        k = (x @ Wk.T).reshape(B, T, H, Dh)
        v = (x @ Wv.T).reshape(B, T, H, Dh)
        cos, sin = _rope_tables(T, x.dtype)
        q = _apply_rotary(q, cos, sin)
        k = _apply_rotary(k, cos, sin)
        q = q.transpose(0, 2, 1, 3).astype(jnp.float32)
        k = k.transpose(0, 2, 1, 3).astype(jnp.float32)
        v = v.transpose(0, 2, 1, 3)
        scores = jnp.einsum('bhqd,bhkd->bhqk', q, k) * scale
        causal = jnp.triu(jnp.ones((T, T), dtype=bool), k=1)
        scores = jnp.where(causal[None, None], -jnp.inf, scores)
        attn = jax.nn.softmax(scores, axis=-1).astype(v.dtype)
        out = jnp.einsum('bhqk,bhkd->bhqd', attn, v)
        out = out.transpose(0, 2, 1, 3).reshape(B, T, C)
        return out @ Wo.T

    def _L1_ffn_ref(hidden_states, gate_W, gate_b, wi_W, wi_b, wo_W, wo_b, lora_A, lora_B):
        import jax, jax.numpy as jnp
        import numpy as np
        B, S, D, F, E, R = (4, 256, 128, 512, 8, 4)
        x = hidden_states
        logits = jnp.einsum('bsd,ed->bse', x, gate_W) + gate_b
        top1 = jnp.argmax(jax.nn.softmax(logits, axis=-1), axis=-1)
        base = jnp.einsum('bsd,fd->bsf', x, wi_W) + wi_b
        out = jnp.zeros_like(x)
        for i in range(lora_A.shape[0]):
            lora = jnp.einsum('bsr,fr->bsf', jnp.einsum('bsd,rd->bsr', x, lora_A[i]), lora_B[i])
            inter = jax.nn.relu(base + lora)
            expert_out = jnp.einsum('bsf,df->bsd', inter, wo_W) + wo_b
            mask = (top1 == i).astype(x.dtype)[..., None]
            out = out + mask * expert_out
        return out
    x = L0_attn_x
    xn = _layernorm(x, axis=-1)
    x = x + _L0_attn_ref(xn, L0_attn_wqk, L0_attn_bqk, L0_attn_gamma, L0_attn_beta, L0_attn_wv, L0_attn_bv, L0_attn_rel_bias) + _L0_ffn_ref(xn, L0_ffn_gate, L0_ffn_corr_bias, L0_ffn_w1, L0_ffn_w2, L0_ffn_fc1_w, L0_ffn_fc2_w, L0_ffn_up_w, L0_ffn_down_w)
    xn = _layernorm(x, axis=-1)
    x = x + _L1_attn_ref(xn, L1_attn_Wq, L1_attn_Wk, L1_attn_Wv, L1_attn_Wo) + _L1_ffn_ref(xn, L1_ffn_gate_W, L1_ffn_gate_b, L1_ffn_wi_W, L1_ffn_wi_b, L1_ffn_wo_W, L1_ffn_wo_b, L1_ffn_lora_A, L1_ffn_lora_B)
    return x

_drawn_inputs = setup_inputs


def setup_inputs(seed=0):
    import zlib

    import numpy as np

    out = dict(_drawn_inputs(seed))
    spreads = {'L0_attn_bqk': (0.0, 2.0),
     'L0_attn_beta': (0.0, 2.0),
     'L0_attn_bv': (0.0, 0.1),
     'L0_ffn_corr_bias': (0.0, 0.8),
     'L1_ffn_gate_b': (0.0, 2.0),
     'L1_ffn_wi_b': (0.0, 2.0),
     'L1_ffn_wo_b': (0.0, 2.0)}
    factors = {'L0_attn_wqk': 56.686,
     'L0_attn_gamma': 64.0,
     'L0_ffn_gate': 8.0,
     'L0_ffn_w1': 8.0,
     'L0_ffn_w2': 8.0,
     'L0_ffn_fc1_w': 8.0,
     'L0_ffn_fc2_w': 8.0,
     'L0_ffn_up_w': 8.0,
     'L0_ffn_down_w': 8.0,
     'L1_attn_Wq': 8.0,
     'L1_attn_Wk': 8.0,
     'L1_attn_Wv': 4.854,
     'L1_attn_Wo': 4.484,
     'L1_ffn_gate_W': 8.0,
     'L1_ffn_lora_A': 8.0,
     'L1_ffn_lora_B': 8.0,
     'L1_ffn_wi_W': 2.736}
    for name, (base, spread) in spreads.items():
        noise = np.random.default_rng([zlib.crc32(name.encode()), seed]).standard_normal(out[name].shape)
        drawn = base * np.exp(spread * noise) if base else spread * noise
        out[name] = jnp.asarray(drawn.astype(out[name].dtype))
    for name, factor in factors.items():
        out[name] = (out[name] * factor).astype(out[name].dtype)
    return out
```

```python
from contextlib import ExitStack

import concourse.bass as bass
from concourse import mybir

F32 = mybir.dt.float32
BF16 = mybir.dt.bfloat16
ACT = mybir.ActivationFunctionType
ALU = mybir.AluOpType
AX = mybir.AxisListType

P = 128
NSEQ, S, D = 16, 512, 128
NT = S // P
EPS = 1e-5
MASKED = -1e30

E0 = 8
HID = 512
NC = HID // P
LAT = 64
BUCKETS = 32
BIASW = P + S
MU = 0.5 ** 0.5
STD2 = (0.25 * 3.141592653589793) ** 0.5 * 2.0 ** 0.5
ERF_TANH = (1.589504771458711e-07, -5.985556253211403e-06, 8.97119297438412e-05, -0.0006257181651408853,
            -0.00018438501376509347, 0.10276548192955917, 1.1283797054270408)
ERF_END = 4.3

NH, DH = 16, 8
E1, RANK = 8, 4

PARAMS0 = [
    ("wqk", D), ("wv", D), ("bqk", 1), ("gamma0", 1), ("gamma1", 1), ("beta0", 1), ("beta1", 1),
    ("bv", S), ("gate", E0), ("corr", NT * E0), ("up", HID), ("down", HID),
    ("fc1", D), ("w1", HID), ("w2", HID), ("fc2", D), ("table", 1),
]
PARAMS1 = [
    ("wq", D), ("wqs", D), ("wk", D), ("wks", D), ("wv", D), ("wo", D),
    ("ga", E1 + E1 * RANK), ("gate_b", NT * E1), ("wi", HID), ("wi_b", NC), ("wof", HID),
    ("wo_b", S), ("lora_b", HID),
]
CONSTS0 = [("hot", BIASW), ("sel", HID), ("ones", P)]
CONSTS1 = [("cos", S), ("sin", S), ("mask_qk", P), ("mask_kq", P)]
CONSTS = [("ident", P), ("order", NT * E0)]


def offsets(fields):
    at, out = 0, {}
    for name, width in fields:
        out[name] = (at, width)
        at += width
    return out, at


def past(value):
    return not isinstance(value, int) or value > 0


class Seq:

    def __init__(self, quo, par, n):
        self.quo, self.par, self.n = quo, par, n
        self.i = quo * n + par

    def back(self, k):
        m = self.par - k
        return Seq(self.quo + m // self.n, m % self.n, self.n)


class Chain:

    def __init__(self, sem, steps, passed):
        self.sem, self.steps, self.passed = sem, steps, passed

    def begin(self, eng, s):
        self.eng, self.base, self.n = eng, s.i * self.steps, 0

    def step(self, ins):
        self.n += 1
        ins.then_inc(self.sem, 1)
        self.eng.wait_ge(self.sem, self.base + self.n)
        if not isinstance(self.base, int):
            self.eng.sem_inc(self.passed, 1)

    def last(self, ins):
        self.n += 1
        ins.then_inc(self.sem, 1)

    def end(self):
        assert self.n == self.steps, (self.n, self.steps)


def over_sequences(eng, turn, n, stages):
    last = NSEQ + stages - 1
    lead = stages - 1 + n
    loops = (NSEQ - lead) // n

    def peeled(i):
        turn(eng, Seq(i // n, i % n, n), [0 <= i - k < NSEQ for k in range(stages)])

    for i in range(lead):
        peeled(i)
    with eng.Fori(0, loops) as r:
        for j in range(lead, lead + n):
            turn(eng, Seq(r + j // n, j % n, n), [True] * stages)
    for i in range(lead + loops * n, last):
        peeled(i)


def layer0(nc, resid, x_d, prm0_d, cst0_d, cst, skew_d, for_layer1, passed):
    with ExitStack() as ctx:
        sem = lambda n: ctx.enter_context(nc.semaphore(n))
        sb = lambda n, shape, dt=F32: ctx.enter_context(nc.sbuf_tensor("l0_" + n, shape, dt))
        at0, w0 = offsets(PARAMS0)
        atc, wc = offsets(CONSTS0)
        prm_t, cst_t = sb("params0", [P, w0]), sb("consts0", [P, wc])
        prm = lambda n: prm_t[:, at0[n][0]:at0[n][0] + at0[n][1]]
        cst0 = lambda n: cst_t[:, atc[n][0]:atc[n][0] + atc[n][1]]
        identf = cst("ident")
        identb, selb = sb("identb0", [P, P], BF16), sb("selb", [64, HID], BF16)
        w1f, w2f = sb("w1f", [P, HID]), sb("w2f", [P, NC, D])
        bias, rows, tab = sb("bias", [P, S]), sb("bias_rows", [P, BIASW]), sb("table_cols", [BUCKETS, P])

        with ExitStack() as sctx:
            ssem = lambda n: sctx.enter_context(nc.semaphore(n))
            params_in, folded, scaled, tab_ok = ssem("params_in"), ssem("folded"), ssem("scaled"), ssem("tab_ok")
            later_in = ssem("later_in")
            skew_out, skew_in, made, bias_ok = ssem("skew_out"), ssem("skew_in"), ssem("made"), ssem("bias_ok")
            ps = sctx.enter_context(nc.psum_tensor("fold_ps", [P, 4, 512], F32))
            block = sctx.enter_context(nc.Block())

            @block.sync
            def _(sp):
                sp.dma_start(cst_t[:, :], cst0_d).then_inc(params_in, 16)
                sp.wait_ge(scaled, 2)
                sp.dma_start(skew_d[:, :], rows[:, :]).then_inc(skew_out, 16)
                sp.wait_ge(skew_out, 16)
                sp.dma_start(bias[:, :], bass.AP(tensor=skew_d, offset=P - 1, ap=[[BIASW - 1, P], [1, S]])
                             ).then_inc(skew_in, 16)

            @block.scalar
            def _(act):
                act.dma_start(prm_t[:, :], prm0_d).then_inc(params_in, 16)
                act.dma_start(cst.tile[:, :], cst.dram).then_inc(params_in, 16)
                for f in for_layer1:
                    act.dma_start(f.tile[:, :], f.dram).then_inc(later_in, 16)
                act.wait_ge(later_in, 16 * len(for_layer1))

            @block.gpsimd
            def _(pool):
                pool.wait_ge(skew_in, 16)
                nc.gpsimd.affine_select(out=bias[:, :], in_=bias[:, :], compare_op=ALU.is_ge, fill=MASKED,
                                        base=0, pattern=[[1, S]], channel_multiplier=-1).then_inc(bias_ok, 1)
                pool.wait_ge(bias_ok, 1)

            @block.tensor
            def _(pe):
                pe.wait_ge(params_in, 48)
                pe.matmul(ps[:, 0, :], prm("fc1")[0:LAT], prm("w1")[0:LAT], start=True, stop=True).then_inc(folded, 1)
                for c in range(NC):
                    mm = pe.matmul(ps[:, 1, c * P:(c + 1) * P], prm("w2")[0:LAT, c * P:(c + 1) * P],
                                   prm("fc2")[0:LAT], start=True, stop=True)
                mm.then_inc(folded, 1)
                pe.wait_ge(tab_ok, 1)
                pe.matmul(ps[:, 2, :], tab[:, :], cst0("hot")[0:BUCKETS, 0:S], start=True, stop=True).then_inc(folded, 1)
                pe.matmul(ps[:, 3, 0:BIASW - S], tab[:, :], cst0("hot")[0:BUCKETS, S:BIASW],
                          start=True, stop=True).then_inc(folded, 1)

            @block.vector
            def _(dve):
                dve.wait_ge(params_in, 48)
                nc.vector.tensor_scalar(tab[:, :], cst0("ones")[0:BUCKETS], prm("table")[0:BUCKETS], None, ALU.mult
                                        ).then_inc(tab_ok, 1)
                nc.vector.tensor_copy(identb[:, :], identf).then_inc(made, 1)
                nc.vector.tensor_copy(selb[:, :], cst0("sel")[0:64]).then_inc(made, 1)
                dve.wait_ge(folded, 4)
                nc.vector.tensor_scalar(rows[:, 0:S], ps[:, 2, :], float(D) ** 0.5 / STD2, -MU / STD2, ALU.mult, ALU.add
                                        ).then_inc(scaled, 1)
                nc.vector.tensor_scalar(rows[:, S:BIASW], ps[:, 3, 0:BIASW - S], float(D) ** 0.5 / STD2, -MU / STD2,
                                        ALU.mult, ALU.add).then_inc(scaled, 1)
                nc.vector.tensor_copy(w1f[:, :], ps[:, 0, :]).then_inc(made, 1)
                nc.vector.tensor_copy(w2f[:, :, :].rearrange("p c d -> p (c d)"), ps[:, 1, :]).then_inc(made, 1)
                dve.wait_ge(made, 4)

        xn, xnT = sb("xn", [P, 2, NT, D]), sb("xnT", [P, 2, S])
        sigq, uq, qT, kT = sb("sigq", [P, S]), sb("uq", [P, S]), sb("qT", [P, S]), sb("kT", [P, S])
        vt, sigv, v = sb("vt", [P, S]), sb("sigv", [P, S]), sb("v", [P, 2, NT, D])
        wsc, wsq, att = sb("wsc", [P, 1280]), sb("wsq", [P, 1280]), sb("att", [P, 2, 1280])
        hr, hs = sb("hr", [P, 2, 512]), sb("hs", [P, 2, NC, S])
        rr, rw, rh = sb("rr", [P, 2, NC, S]), sb("rw", [P, 2, S]), sb("rh", [P, NC, S])
        st6, mv, rstd = sb("st6", [P, NT, 6]), sb("mv", [P, NT, 2]), sb("rstd", [P, NT])
        halfneg = sb("halfneg", [P, NT])
        gts = sb("gts", [P, 2, NT, E0])
        gw = sb("gw", [P, 20, NT * E0])
        w3 = sb("w3", [P, NT, 64], BF16)
        wT = sb("wT", [64, 2, S], BF16)

        psum = lambda n: ctx.enter_context(nc.psum_tensor(n, [P, 512], F32))
        X, Y = psum("X"), psum("Y")
        G = [psum("G0"), psum("G1")]
        Z = [psum("Z0"), psum("Z1")]
        BC = [psum("BC0"), psum("BC1")]

        x_in = [sem("x_in0"), sem("x_in1")]
        const_ok, rstd_ok, xn_ok = sem("const_ok"), sem("rstd_ok"), sem("xn_ok")
        xT_ps, xT_ok, qk_ps, sigq_ok, uq_ok = sem("xT_ps"), sem("xT_ok"), sem("qk_ps"), sem("sigq_ok"), sem("uq_ok")
        q_ok, k_ok, sim_ps, z_ok, erf_ok, p_ok = sem("q_ok"), sem("k_ok"), sem("sim_ps"), sem("z_ok"), sem("erf_ok"), sem("p_ok")
        v_ps, vt_ok, sigv_ok, v_ok = sem("v_ps"), sem("vt_ok"), sem("sigv_ok"), sem("v_ok")
        gate_ps, gate_ok, hid_ps, relu_ok, hs_ok = sem("gate_ps"), sem("gate_ok"), sem("hid_ps"), sem("relu_ok"), sem("hs_ok")
        wT_ps, wT_ok, bc_ps, rw_ok, rh_ok = sem("wT_ps"), sem("wT_ok"), sem("bc_ps"), sem("rw_ok"), sem("rh_ok")
        y_ps, x1_ok, clamp_ok, sq_ok = sem("y_ps"), sem("x1_ok"), sem("clamp_ok"), sem("sq_ok")
        poly_chain = Chain(sem("poly_chain"), 6, passed)
        ln_chain = Chain(sem("ln_chain"), 2, passed)
        pool_chain = Chain(sem("pool_chain"), 1, passed)
        gate_chain = Chain(sem("gate_chain"), 32, passed)

        KB = [(0, 0, 512), (1, 512, 384), (2, 1024, 256), (3, 896, 128)]
        UNITS = [(0, 512), (512, 512), (1024, 256)]
        block = ctx.enter_context(nc.Block())

        @block.sync
        def _(sp):
            def turn(sp, s, on):
                if past(2 * (s.i - 1)):
                    sp.wait_ge(ln_chain.sem, 2 * (s.i - 1))
                sp.dma_start(resid[:, bass.ds(s.i * S, S)].rearrange("p (t d) -> p t d", d=D),
                             x_d[bass.ds(s.i, 1), :, :].rearrange("s (t p) d -> p (s t) d", p=P)
                             ).then_inc(x_in[s.par], 16)
            over_sequences(sp, turn, 2, 1)

        @block.gpsimd
        def _(pool):
            nc.gpsimd.memset(halfneg[:, :], -0.5).then_inc(const_ok, 1)
            nc.gpsimd.memset(w3[:, :, :], 0.0).then_inc(const_ok, 1)
            pool.wait_ge(const_ok, 2)

            def turn(pool, s, on):
                a, b = s.back(1), s.back(2)
                if on[0]:
                    pool.wait_ge(ln_chain.sem, 2 * (s.i + 1))
                    pool.sem_inc(passed, 1)
                    pool_chain.begin(pool, s)
                    pool_chain.step(nc.gpsimd.tensor_scalar(rstd[:, :], mv[:, :, 1], EPS, None, ALU.add))
                    nc.gpsimd.tensor_tensor(rstd[:, :], rstd[:, :], halfneg[:, :], ALU.pow).then_inc(rstd_ok, 1)
                    pool_chain.end()
                if on[2]:
                    pool.wait_ge(erf_ok, b.i + 1)
                    pool.sem_inc(passed, 1)
                    nc.gpsimd.tensor_scalar(att[:, b.par, :], att[:, b.par, :], 0.5, 0.5, ALU.mult, ALU.add
                                            ).then_inc(p_ok, 1)
                    if past(b.i):
                        pool.wait_ge(y_ps, b.i)
                    for c in range(NC):
                        pool.wait_ge(rw_ok, NC * b.i + c + 1)
                        nc.gpsimd.tensor_tensor(rh[:, c, :], rw[:, c % 2, :], rr[:, b.par, c, :], ALU.mult
                                                ).then_inc(rh_ok, 1)
                if on[1]:
                    pool.wait_ge(uq_ok, a.i + 1)
                    pool.sem_inc(passed, 1)
                    if past(4 * a.i):
                        pool.wait_ge(sim_ps, 4 * a.i)
                        pool.sem_inc(passed, 1)
                    nc.gpsimd.tensor_scalar(kT[:, :], uq[:, :], prm("gamma1"), prm("beta1"), ALU.mult, ALU.add
                                            ).then_inc(k_ok, 1)
                    pool.wait_ge(sigv_ok, a.i + 1)
                    pool.sem_inc(passed, 1)
                    pool.wait_ge(vt_ok, a.i + 1)
                    pool.sem_inc(passed, 1)
                    if past(a.i - 1):
                        pool.wait_ge(y_ps, a.i - 1)
                    nc.gpsimd.tensor_tensor(v[:, a.par, :, :].rearrange("p t d -> p (t d)"), vt[:, :], sigv[:, :],
                                            ALU.mult).then_inc(v_ok, 1)
                    for u, (c, w) in enumerate(UNITS):
                        pool.wait_ge(z_ok, 3 * a.i + u + 1)
                        pool.sem_inc(passed, 1)
                        nc.gpsimd.tensor_scalar(wsc[:, c:c + w], wsc[:, c:c + w], ERF_END, -ERF_END, ALU.min, ALU.max
                                                ).then_inc(clamp_ok, 1)
            over_sequences(pool, turn, 2, 3)

        @block.scalar
        def _(act):
            def relu(a, g):
                act.wait_ge(hid_ps, 8 * a.i + g)
                src = G[(9 * a.par + g) % 2][:, :]
                if g <= NC:
                    nc.scalar.activation(hr[:, g % 2, :], src, ACT.Relu).then_inc(relu_ok, 1)
                else:
                    if past(NC * (a.i - 1)):
                        act.wait_ge(rh_ok, NC * (a.i - 1))
                    nc.scalar.activation(rr[:, a.par, g - 5, :], src, ACT.Relu).then_inc(relu_ok, 1)

            def square(a, g):
                act.wait_ge(relu_ok, 8 * a.i + g)
                if g == 1:
                    if past(a.i - 1):
                        act.wait_ge(y_ps, a.i - 1)
                nc.scalar.activation(hs[:, a.par, g - 1, :], hr[:, g % 2, :], ACT.Square).then_inc(hs_ok, 1)

            def turn(act, s, on):
                a, b = s.back(1), s.back(2)
                if on[2]:
                    act.wait_ge(poly_chain.sem, poly_chain.steps * (b.i + 1))
                    nc.scalar.activation(att[:, b.par, :], att[:, b.par, :], ACT.Tanh, scale=ERF_TANH[0]
                                         ).then_inc(erf_ok, 1)
                if on[1]:
                    act.wait_ge(qk_ps, a.i + 1)
                    if past(a.i):
                        act.wait_ge(uq_ok, a.i)
                    nc.scalar.activation(sigq[:, :], G[(9 * a.par) % 2][:, :], ACT.Sigmoid, bias=prm("bqk")
                                         ).then_inc(sigq_ok, 1)
                    act.wait_ge(gate_ps, a.i + 1)
                    nc.scalar.activation(gts[:, a.par, :, :], BC[0][:, 0:NT * E0].rearrange("p (t e) -> p t e", e=E0),
                                         ACT.Sigmoid).then_inc(gate_ok, 1)
                    act.wait_ge(vt_ok, a.i + 1)
                    if past(a.i):
                        act.wait_ge(v_ok, a.i)
                    nc.scalar.activation(sigv[:, :], vt[:, :], ACT.Sigmoid).then_inc(sigv_ok, 1)
                    for g in range(1, NC + 1):
                        relu(a, g)
                        square(a, g)
                    for u, (c, w) in enumerate(UNITS):
                        act.wait_ge(clamp_ok, 3 * a.i + u + 1)
                        if past(poly_chain.steps * a.i):
                            act.wait_ge(poly_chain.sem, poly_chain.steps * a.i)
                        nc.scalar.activation(wsq[:, c:c + w], wsc[:, c:c + w], ACT.Square).then_inc(sq_ok, 1)
                    for g in range(NC + 1, 2 * NC + 1):
                        relu(a, g)
                    act.wait_ge(wT_ps, a.i + 1)
                    if past(NC * (a.i - 1)):
                        act.wait_ge(bc_ps, NC * (a.i - 1))
                    nc.scalar.activation(wT[:, a.par, :], X[0:64, 0:S // 2].bitcast(BF16), ACT.Copy).then_inc(wT_ok, 1)
            over_sequences(act, turn, 2, 3)

        @block.tensor
        def _(pe):
            def hidden(a, g):
                bank = G[(9 * a.par + g) % 2]
                if g == 1:
                    if past(8 * a.i):
                        pe.wait_ge(relu_ok, 8 * a.i)
                elif g == 2:
                    pe.wait_ge(uq_ok, a.i + 1)
                else:
                    if past(8 * a.i + g - 2):
                        pe.wait_ge(relu_ok, 8 * a.i + g - 2)
                w = prm("up")[:, (g - 1) * P:g * P] if g <= NC else w1f[:, (g - 5) * P:(g - 4) * P]
                pe.matmul(bank[:, :], w, xnT[:, a.par, :], start=True, stop=True).then_inc(hid_ps, 1)

            def scores(a, kb, bank, lo):
                w = S - kb * P
                pe.matmul(bank[:, lo:lo + w], kT[:, kb * P:(kb + 1) * P], qT[:, kb * P:S], start=True, stop=True
                          ).then_inc(sim_ps, 1)

            def spread(b, c):
                if c == 0:
                    pe.wait_ge(wT_ok, b.i + 1)
                    pe.wait_ge(gate_ok, b.i + 1)
                if past(NC * b.i + c - 1):
                    pe.wait_ge(rw_ok, NC * b.i + c - 1)
                pe.matmul(BC[c % 2][:, :], selb[:, c * P:(c + 1) * P], wT[:, b.par, :], start=True, stop=True
                          ).then_inc(bc_ps, 1)

            def output(b, t):
                if t == 0:
                    if past(b.i):
                        pe.wait_ge(x1_ok, b.i)
                    pe.wait_ge(p_ok, b.i + 1)
                    pe.wait_ge(v_ok, b.i + 1)
                    pe.wait_ge(hs_ok, NC * (b.i + 1))
                out, q = Y[:, t * P:(t + 1) * P], slice(t * P, (t + 1) * P)
                for kb, c, w in KB[:t + 1]:
                    lo = c + (t - kb) * P
                    pe.matmul(out, att[:, b.par, lo:lo + P], v[:, b.par, kb, :], start=(kb == 0), stop=False)
                for c in range(NC):
                    pe.matmul(out, hs[:, b.par, c, q], prm("down")[:, c * D:(c + 1) * D], start=False, stop=False)
                if t == 0:
                    pe.wait_ge(rh_ok, NC * (b.i + 1))
                for c in range(NC):
                    mm = pe.matmul(out, rh[:, c, q], w2f[:, c, :], start=False, stop=(c == NC - 1))
                if t == NT - 1:
                    mm.then_inc(y_ps, 1)

            def turn(pe, s, on):
                a, b = s.back(1), s.back(2)
                if on[1]:
                    pe.wait_ge(xn_ok, a.i + 1)
                    if past(a.i):
                        pe.wait_ge(wT_ok, a.i)
                    for t in range(NT):
                        mm = pe.transpose(X[:, t * P:(t + 1) * P], xn[:, a.par, t, :], identf)
                    mm.then_inc(xT_ps, 1)
                if on[2]:
                    spread(b, 0)
                    spread(b, 1)
                if on[1]:
                    pe.wait_ge(xT_ok, a.i + 1)
                    if past(8 * a.i - 1):
                        pe.wait_ge(relu_ok, 8 * a.i - 1)
                    pe.matmul(G[(9 * a.par) % 2][:, :], prm("wqk"), xnT[:, a.par, :], start=True, stop=True
                              ).then_inc(qk_ps, 1)
                    hidden(a, 1)
                if on[2]:
                    spread(b, 2)
                    spread(b, 3)
                if on[1]:
                    for t in range(NT):
                        mm = pe.matmul(X[:, t * P:(t + 1) * P], xnT[:, a.par, t * P:(t + 1) * P], prm("wv"),
                                       start=True, stop=True)
                    mm.then_inc(v_ps, 1)
                    hidden(a, 2)
                    if past(NC * a.i - 1):
                        pe.wait_ge(rw_ok, NC * a.i - 1)
                    for t in range(NT):
                        mm = pe.matmul(BC[0][:, t * E0:(t + 1) * E0], xnT[:, a.par, t * P:(t + 1) * P], prm("gate"),
                                       start=True, stop=True)
                    mm.then_inc(gate_ps, 1)
                    hidden(a, 3)
                    pe.wait_ge(q_ok, a.i + 1)
                    pe.wait_ge(k_ok, a.i + 1)
                    if past(3 * a.i):
                        pe.wait_ge(z_ok, 3 * a.i)
                    scores(a, 0, Z[0], 0)
                    scores(a, 1, Z[1], 0)
                    scores(a, 3, Z[1], 384)
                    hidden(a, 4)
                    pe.wait_ge(z_ok, 3 * a.i + 1)
                    scores(a, 2, Z[0], 0)
                for t in range(NT):
                    if on[1]:
                        hidden(a, NC + 1 + t)
                    if on[2]:
                        output(b, t)
                if on[1]:
                    pe.wait_ge(gate_chain.sem, gate_chain.steps * (a.i + 1))
                    pe.wait_ge(vt_ok, a.i + 1)
                    pe.sem_inc(passed, 1)
                    for t in range(NT):
                        mm = pe.transpose(X[0:64, 0:S // 2].bitcast(BF16)[:, t * P:(t + 1) * P], w3[:, t, :], identb[:, :])
                    mm.then_inc(wT_ps, 1)
            over_sequences(pe, turn, 2, 3)

        @block.vector
        def _(dve):
            dve.wait_ge(const_ok, 2)

            def gating(a):
                ch = gate_chain
                ch.begin(dve, a)
                tt, tsc, red = nc.vector.tensor_tensor, nc.vector.tensor_scalar, nc.vector.tensor_reduce
                row = lambda k, n=NT * E0: gw[:, k, 0:n]
                te = lambda k: row(k).rearrange("p (t e) -> p t e", e=E0)
                grp = lambda k: row(k).rearrange("p (g e) -> p g e", e=E0 // 2)
                per_t = lambda k: row(k, NT).unsqueeze(2).to_broadcast([P, NT, E0])
                score = gts[:, a.par, :, :]
                ch.step(tt(te(0), score, prm("corr").rearrange("p (t e) -> p t e", e=E0), ALU.add))
                hi, lo = row(1, 16).rearrange("p (g e) -> p g e", e=2), row(2, 16).rearrange("p (g e) -> p g e", e=2)
                ch.step(tt(hi, grp(0)[:, :, 0:2], grp(0)[:, :, 2:4], ALU.max))
                ch.step(tt(lo, grp(0)[:, :, 0:2], grp(0)[:, :, 2:4], ALU.min))
                g1 = lambda k: row(k, 8).unsqueeze(2)
                ch.step(tt(g1(3), hi[:, :, 0:1], hi[:, :, 1:2], ALU.max))
                ch.step(tt(g1(4), hi[:, :, 0:1], hi[:, :, 1:2], ALU.min))
                ch.step(tt(g1(5), lo[:, :, 0:1], lo[:, :, 1:2], ALU.max))
                ch.step(tt(row(4, 8), row(4, 8), row(5, 8), ALU.max))
                ch.step(tt(row(3, 8), row(3, 8), row(4, 8), ALU.add))
                gs = row(3, 8).rearrange("p (t g) -> p t g", g=2)
                gm = row(5, 8).rearrange("p (t g) -> p t g", g=2)
                ch.step(tt(gm[:, :, 0:1], gs[:, :, 0:1], gs[:, :, 1:2], ALU.is_ge))
                ch.step(tt(gm[:, :, 1:2], gs[:, :, 0:1], gs[:, :, 1:2], ALU.is_lt))
                ch.step(tt(grp(6), grp(0), row(5, 8).unsqueeze(2).to_broadcast([P, 8, 4]), ALU.mult))
                order = cst("order").rearrange("p (t e) -> p t e", e=E0)
                for k in range(2):
                    ch.step(red(row(7, NT), te(6), AX.X, ALU.max))
                    ch.step(tt(te(8), te(6), per_t(7), ALU.is_equal))
                    ch.step(tt(te(8), te(8), order, ALU.mult))
                    ch.step(red(row(7, NT), te(8), AX.X, ALU.max))
                    ch.step(tt(te(9 + k), te(8), per_t(7), ALU.is_equal))
                    if k == 0:
                        ch.step(nc.vector.scalar_tensor_tensor(out=row(6), in0=row(9), scalar=MASKED, in1=row(6),
                                                               op0=ALU.mult, op1=ALU.add))
                ch.step(tt(te(9), te(9), te(10), ALU.add))
                ch.step(tt(te(9), te(9), score, ALU.mult))
                ch.step(red(row(7, NT), te(9), AX.X, ALU.add))
                ch.step(tsc(row(7, NT), row(7, NT), 1e-20, None, ALU.add))
                ch.step(nc.vector.reciprocal(row(7, NT), row(7, NT)))
                ch.step(tt(te(9), te(9), per_t(7), ALU.mult))
                if past(a.i):
                    dve.wait_ge(wT_ps, a.i)
                ch.step(nc.vector.tensor_copy(w3[:, :, 0:E0], te(9)))
                ch.step(tt(te(9), te(9), w3[:, :, 0:E0], ALU.subtract))
                ch.step(nc.vector.tensor_copy(w3[:, :, E0:2 * E0], te(9)))
                ch.last(tt(w3[:, :, 2 * E0:3 * E0], te(9), w3[:, :, E0:2 * E0], ALU.subtract))
                ch.end()

            def scaled(b, c):
                dve.wait_ge(bc_ps, NC * b.i + c + 1)
                if past(NC * b.i + c - 1):
                    dve.wait_ge(rh_ok, NC * b.i + c - 1)
                nc.vector.tensor_tensor(rw[:, c % 2, :], rr[:, b.par, c, :], BC[c % 2][:, :], ALU.mult
                                        ).then_inc(rw_ok, 1)

            def biased(a, u):
                for kb, c, w in KB:
                    if UNITS[u][0] <= c < UNITS[u][0] + UNITS[u][1]:
                        dve.wait_ge(sim_ps, 4 * a.i + (1, 3, 4)[u])
                        last = nc.vector.scalar_tensor_tensor(
                            out=wsc[:, c:c + w], in0=Z[u % 2][:, c - UNITS[u][0]:c - UNITS[u][0] + w],
                            scalar=1.0 / (S * STD2), in1=bias[:, 0:w], op0=ALU.mult, op1=ALU.add)
                last.then_inc(z_ok, 1)

            def turn(dve, s, on):
                a, b = s.back(1), s.back(2)
                if on[0]:
                    x = resid[:, bass.ds(s.i * S, S)].rearrange("p (t d) -> p t d", d=D)
                if on[1]:
                    dve.wait_ge(xT_ps, a.i + 1)
                    if past(8 * (a.i - 1)):
                        dve.wait_ge(hid_ps, 8 * (a.i - 1))
                    nc.vector.tensor_copy(xnT[:, a.par, :], X[:, :]).then_inc(xT_ok, 1)
                if on[0]:
                    dve.wait_ge(x_in[s.par], 16 * (s.quo + 1))
                    ln_chain.begin(dve, s)
                    for t in range(NT):
                        last = nc.vector.bn_stats(st6[:, t, :], x[:, t, :])
                    ln_chain.step(last)
                    if past(s.i):
                        dve.wait_ge(rstd_ok, s.i)
                        dve.sem_inc(passed, 1)
                    for t in range(NT):
                        last = nc.vector.bn_aggr(mv[:, t, :], st6[:, t, :])
                    ln_chain.last(last)
                    ln_chain.end()
                if on[2]:
                    scaled(b, 0)
                    scaled(b, 1)
                if on[1]:
                    dve.wait_ge(sigq_ok, a.i + 1)
                    if past(a.i):
                        dve.wait_ge(k_ok, a.i)
                    nc.vector.scalar_tensor_tensor(out=uq[:, :], in0=G[(9 * a.par) % 2][:, :], scalar=prm("bqk"),
                                                   in1=sigq[:, :], op0=ALU.add, op1=ALU.mult).then_inc(uq_ok, 1)
                    dve.wait_ge(uq_ok, a.i + 1)
                    if past(4 * a.i):
                        dve.wait_ge(sim_ps, 4 * a.i)
                    nc.vector.tensor_scalar(qT[:, :], uq[:, :], prm("gamma0"), prm("beta0"), ALU.mult, ALU.add
                                            ).then_inc(q_ok, 1)
                if on[2]:
                    scaled(b, 2)
                    scaled(b, 3)
                if on[1]:
                    dve.wait_ge(v_ps, a.i + 1)
                    if past(a.i):
                        dve.wait_ge(v_ok, a.i)
                    nc.vector.tensor_tensor(vt[:, :], X[:, :], prm("bv"), ALU.add).then_inc(vt_ok, 1)
                    for u in range(3):
                        biased(a, u)
                    dve.wait_ge(gate_ok, a.i + 1)
                    gating(a)
                    poly_chain.begin(dve, a)
                    dve.wait_ge(sq_ok, 3 * (a.i + 1))
                    if past(a.i - 1):
                        dve.wait_ge(y_ps, a.i - 1)
                    t = att[:, a.par, :]
                    for k in range(1, 7):
                        op = nc.vector.scalar_tensor_tensor(
                            out=t, in0=(wsq[:, :] if k == 1 else t), scalar=ERF_TANH[k] / ERF_TANH[0],
                            in1=(wsq[:, :] if k < 6 else wsc[:, :]), op0=ALU.add, op1=ALU.mult)
                        (poly_chain.step if k < 6 else poly_chain.last)(op)
                    poly_chain.end()
                if on[0]:
                    dve.wait_ge(rstd_ok, s.i + 1)
                    if past(s.i - 1):
                        dve.wait_ge(xT_ps, s.i - 1)
                    for t in range(NT):
                        last = nc.vector.tensor_scalar(xn[:, s.par, t, :], x[:, t, :], mv[:, t, 0:1], rstd[:, t:t + 1],
                                                       ALU.subtract, ALU.mult)
                    last.then_inc(xn_ok, 1)
                if on[2]:
                    dve.wait_ge(y_ps, b.i + 1)
                    xb = resid[:, bass.ds(b.i * S, S)]
                    nc.vector.tensor_tensor(xb, xb, Y[:, :], ALU.add).then_inc(x1_ok, 1)
            over_sequences(dve, turn, 2, 3)
            dve.wait_ge(x1_ok, NSEQ)


def layer1(nc, resid, cst, prm, cst1, out_d, scratch, passed):
    QPART, KPART = (0, 0, 0, 1, 1, 2), (0, 1, 2, 0, 1, 0)
    ROWS = 6 * DH
    SCALE = DH ** -0.5
    qk_d, m_d, o_d, r_d = scratch
    with ExitStack() as ctx:
        sem = lambda n: ctx.enter_context(nc.semaphore("b_" + n))
        sb = lambda n, shape, dt=F32: ctx.enter_context(nc.sbuf_tensor("l1_" + n, shape, dt))
        identf = cst("ident")
        identb = sb("identb", [P, P], BF16)
        mask_qk, mask_kq = sb("mask_qk", [P, P], BF16), sb("mask_kq", [P, P], BF16)
        Q, K = sb("Q", [P, 3, NH // 2, S], BF16), sb("K", [P, 3, NH // 2, S], BF16)
        V = sb("V", [P, 3, NT, NH, 32])
        E = sb("E", [P, 2, 5120])
        xn, xnT = sb("xn", [P, NT, D]), sb("xnT", [P, S])
        rope = sb("rope", [P, 2, 2, S])
        parts = sb("parts", [P, 2, 3, S], BF16)
        hid = sb("hid", [P, NC, S])
        low, lowT = sb("low", [P, NT, P]), sb("lowT", [P, S])
        gl = sb("gl", [P, 4, NT * E1])
        st6, mv, rstd, halfneg = sb("st6", [P, NT, 6]), sb("mv", [P, NT, 2]), sb("rstd", [P, NT]), sb("halfneg", [P, NT])
        negmax, mparts, mT = sb("negmax", [P, NT, NH]), sb("mparts", [P, NT, 3 * NH], BF16), sb("mT", [3 * NH, S], BF16)
        avs = sb("avs", [P, 2, S])
        heads, denom, recip, spread, normed = (sb("heads", [P, S]), sb("denom", [P, S // 8]), sb("recip", [P, S // 8]),
                                               sb("spread", [P, S]), sb("normed", [P, S]))

        psum = lambda n, shape: ctx.enter_context(nc.psum_tensor("l1_" + n, shape, F32))
        MB, TB = psum("MB", [P, 2, 512]), psum("TB", [P, 2, 512])
        AVB, X, G = psum("AVB", [P, 512]), psum("X", [P, 512]), [psum("G0", [P, 512]), psum("G1", [P, 512])]

        set_ok, dset_ok, rstd_ok, xn_ok = sem("set_ok"), sem("dset_ok"), sem("rstd_ok"), sem("xn_ok")
        xT_ps, xT_ok, q_ps, k_ps, rope_ok, v_ps, v_ok = (sem("xT_ps"), sem("xT_ok"), sem("q_ps"), sem("k_ps"),
                                                         sem("rope_ok"), sem("v_ps"), sem("v_ok"))
        ga_ps, low_ps, lowT_ok, hid_ps, hid_ok, ffn_ps, ffn_ok = (sem("ga_ps"), sem("low_ps"), sem("lowT_ok"), sem("hid_ps"),
                                                                  sem("hid_ok"), sem("ffn_ps"), sem("ffn_ok"))
        biased_ok = sem("biased_ok")
        m_ps, max_ok, mT_ps, mT_ok, m_out, m_in = (sem("m_ps"), sem("max_ok"), sem("mT_ps"), sem("mT_ok"), sem("m_out"),
                                                   sem("m_in"))
        t_ps, exp_ok, av_ps, avs_ok = sem("t_ps"), sem("exp_ok"), sem("av_ps"), sem("avs_ok")
        parts_out, stack_in = [sem("q_parts_out"), sem("k_parts_out")], sem("stack_in")
        o_out, o_in, rec_ok, r_out, r_in, normed_ok, wo_ps, x2_ok, stored = (
            [sem("even_o_out"), sem("odd_o_out")], sem("o_in"), sem("rec_ok"), sem("r_out"), sem("r_in"), sem("normed_ok"), sem("wo_ps"),
            sem("x2_ok"), sem("stored"))
        ln_chain, pool_chain = Chain(sem("ln_chain"), 2, passed), Chain(sem("pool_chain"), 1, passed)
        part_chain, top_chain = Chain(sem("part_chain"), 10, passed), Chain(sem("top_chain"), 7, passed)
        max_chain = Chain(sem("max_chain"), 4, passed)

        def head(h):
            return slice(64 * (h % 2), 64 * (h % 2) + ROWS), slice(64 * (h % 2), 64 * (h % 2) + ROWS + 3), h // 2

        MUNITS = [[(0, 3, 0, 0), (1, 3, 1, 0)], [(2, 3, 0, 0), (3, 3, 1, 0)],
                  [(0, 2, 0, 0), (0, 0, 0, 384), (1, 2, 1, 0), (1, 0, 1, 384)],
                  [(2, 2, 0, 0), (2, 0, 0, 384), (3, 2, 1, 0), (3, 0, 1, 384)],
                  [(h, 1, h % 2, 256 * (h // 2)) for h in range(4)]]
        TUNITS = [[(h, 0, 0, 0), (h, 1, 1, 0), (h, 3, 1, 384)] for h in range(4)]
        TUNITS.append([(h, 2, h % 2, 256 * (h // 2)) for h in range(4)])
        UN = len(TUNITS)
        ECOL = {(h, kb): unit * 1024 + bank * 512 + col
                for unit, blocks in enumerate(TUNITS) for h, kb, bank, col in blocks}

        LAG = 5

        def quad_of(j, t, u, on):
            return (t, j - 1, on[3]) if j else (u, 3, on[4])

        def value_quad_of(j, t, u, on):
            return [(u, 2, on[4]), (u, 3, on[4]), (t, 0, on[3]), (t, 1, on[3])][j]

        block = ctx.enter_context(nc.Block())

        @block.sync
        def _(sp):
            def turn(sp, s, on):
                a, t, u, v = s.back(1), s.back(3), s.back(4), s.back(5)
                if on[5]:
                    sp.wait_ge(x2_ok, v.i + 1)
                    sp.sem_inc(passed, 1)
                    sp.dma_start(out_d[bass.ds(v.i, 1), :, :].rearrange("s (t p) d -> p (s t) d", p=P),
                                 resid[:, bass.ds(v.i * S, S)].rearrange("p (t d) -> p t d", d=D)).then_inc(stored, 16)
                if on[3]:
                    sp.wait_ge(mT_ok, t.i + 1)
                    sp.sem_inc(passed, 1)
                    if past(32 * t.i):
                        sp.wait_ge(m_in, 32 * t.i)
                        sp.sem_inc(passed, 1)
                    sp.dma_start(m_d[t.par], mT[:, :]).then_inc(m_out, 16)
                    sp.wait_ge(m_out, 16 * (t.i + 1))
                    sp.sem_inc(passed, 1)
                    for half in range(2):
                        rows = m_d[t.par].rearrange("(m g f) n -> f m g n", m=3, f=2)[half]
                        sp.dma_start(Q[64 * half + ROWS:64 * half + ROWS + 3, t.par, :, :], rows).then_inc(m_in, 16)
                if on[4]:
                    store_heads(sp, u, 2)
                if on[1]:
                    for side in range(2):
                        sp.wait_ge(part_chain.sem, part_chain.steps * a.i + 5 * (side + 1))
                        sp.sem_inc(passed, 1)
                        sp.dma_start(qk_d[a.par, side].rearrange("m p n -> p m n"), parts[:, side, :, :]
                                     ).then_inc(parts_out[side], 16)
                    for side in range(2):
                        sp.wait_ge(parts_out[side], 16 * (a.i + 1))
                        sp.sem_inc(passed, 1)
                    if past(UN * 4 * (a.i - 2)):
                        sp.wait_ge(t_ps, UN * 4 * (a.i - 2))
                        sp.sem_inc(passed, 1)
                    if past(16 * 24 * a.i):
                        sp.wait_ge(stack_in, 16 * 24 * a.i)
                        sp.sem_inc(passed, 1)
                    for side, (stack, order) in enumerate(((Q, QPART), (K, KPART))):
                        for slot, part in enumerate(order):
                            for half in range(2):
                                lo = 64 * half + slot * DH
                                rows = qk_d[a.par, side, part].rearrange("(g f d) n -> f d g n", f=2, d=DH)[half]
                                sp.dma_start(stack[lo:lo + DH, a.par, :, :], rows).then_inc(stack_in, 16)
                if on[4]:
                    store_heads(sp, u, 3)
                    for r in range(2):
                        sp.wait_ge(o_out[r], 16 * 2 * (u.i + 1))
                        sp.sem_inc(passed, 1)
                    if past(u.i):
                        sp.wait_ge(normed_ok, u.i)
                        sp.sem_inc(passed, 1)
                    if past(u.i):
                        sp.wait_ge(rec_ok, u.i)
                        sp.sem_inc(passed, 1)
                    o = o_d[u.par].rearrange("(h r) n -> h r n", r=32)
                    sp.dma_start(heads[:, :], o[:, 0:DH, :]).then_inc(o_in, 16)
                    sp.dma_start(denom[:, :], o[:, DH, :].rearrange("h (b n) -> h b n", b=8)).then_inc(o_in, 16)
                    sp.wait_ge(rec_ok, u.i + 1)
                    sp.sem_inc(passed, 1)
                    sp.dma_start(r_d[u.par].rearrange("h (b n) -> (h b) n", b=8), recip[:, :]).then_inc(r_out, 16)
                    sp.wait_ge(r_out, 16 * (u.i + 1))
                    sp.sem_inc(passed, 1)
                    sp.dma_start(spread[:, :], bass.AP(tensor=r_d.tensor, offset=u.par * NH * S,
                                                       ap=[[S, NH], [0, DH], [1, S]])).then_inc(r_in, 16)
                if on[3]:
                    store_heads(sp, t, 0)
                    store_heads(sp, t, 1)

            def store_heads(sp, seq, q):
                sp.wait_ge(avs_ok, 4 * seq.i + q + 1)
                sp.sem_inc(passed, 1)
                sp.dma_start(o_d[seq.par, q * P:(q + 1) * P, :], avs[:, q % 2, :]).then_inc(o_out[q % 2], 16)

            over_sequences(sp, turn, 3, LAG + 1)
            sp.wait_ge(stored, 16 * NSEQ)

        @block.gpsimd
        def _(pool):
            nc.gpsimd.memset(halfneg[:, :], -0.5).then_inc(set_ok, 1)
            nc.gpsimd.memset(low[:, :, :], 0.0).then_inc(set_ok, 1)
            nc.gpsimd.memset(V[:, :, :, :, :], 0.0).then_inc(set_ok, 1)
            pool.wait_ge(set_ok, 3)
            nc.gpsimd.memset(V[:, :, :, :, DH:DH + 1], 1.0).then_inc(set_ok, 1)
            pool.wait_ge(set_ok, 4)

            def split(pool, a, side):
                x, part = rope[:, side, 0, :], lambda k: parts[:, side, k, :]
                pool.wait_ge(rope_ok, 2 * a.i + side + 1)
                pool.sem_inc(passed, 1)
                if past(16 * a.i):
                    pool.wait_ge(parts_out[side], 16 * a.i)
                ch = part_chain
                ch.step(nc.gpsimd.tensor_tensor(x, x, rope[:, side, 1, :], ALU.add))
                ch.step(nc.gpsimd.tensor_scalar(part(0), x, 1.0, None, ALU.mult))
                ch.step(nc.gpsimd.tensor_tensor(x, x, part(0), ALU.subtract))
                ch.step(nc.gpsimd.tensor_scalar(part(1), x, 1.0, None, ALU.mult))
                ch.last(nc.gpsimd.tensor_tensor(part(2), x, part(1), ALU.subtract))

            def turn(pool, s, on):
                a, u = s.back(1), s.back(4)
                if on[1]:
                    part_chain.begin(pool, a)
                    split(pool, a, 0)
                    split(pool, a, 1)
                    part_chain.end()
                if on[0]:
                    pool.wait_ge(ln_chain.sem, 2 * (s.i + 1))
                    pool.sem_inc(passed, 1)
                    pool_chain.begin(pool, s)
                    pool_chain.step(nc.gpsimd.tensor_scalar(rstd[:, :], mv[:, :, 1], EPS, None, ALU.add))
                    nc.gpsimd.tensor_tensor(rstd[:, :], rstd[:, :], halfneg[:, :], ALU.pow).then_inc(rstd_ok, 1)
                    pool_chain.end()
                if on[4]:
                    pool.wait_ge(o_in, 32 * (u.i + 1))
                    pool.wait_ge(r_in, 16 * (u.i + 1))
                    if past(u.i):
                        pool.wait_ge(wo_ps, u.i)
                    nc.gpsimd.tensor_tensor(normed[:, :], heads[:, :], spread[:, :], ALU.mult).then_inc(normed_ok, 1)
                if on[1]:
                    x = resid[:, bass.ds(a.i * S, S)]
                    pool.wait_ge(xn_ok, a.i + 1)
                    nc.gpsimd.tensor_tensor(x, x, prm("wo_b"), ALU.add).then_inc(biased_ok, 1)
            over_sequences(pool, turn, 3, LAG)

        @block.scalar
        def _(act):
            def turn(act, s, on):
                a, t, u = s.back(1), s.back(3), s.back(4)
                for k in range(4 * UN):
                    j, n = divmod(k, UN)
                    seq, q, live = quad_of(j, t, u, on)
                    if live:
                        act.wait_ge(t_ps, UN * (4 * seq.i + q) + n + 1)
                        if n == 0:
                            if past(4 * seq.i + q - 1):
                                act.wait_ge(av_ps, 4 * seq.i + q - 1)
                        nc.scalar.activation(E[:, j % 2, 1024 * n:1024 * (n + 1)],
                                             TB[:, :, :].rearrange("p b n -> p (b n)"), ACT.Exp, scale=SCALE
                                             ).then_inc(exp_ok, 1)
                    if k == 0 and on[1]:
                        act.wait_ge(xT_ps, a.i + 1)
                        if past(NC * a.i):
                            act.wait_ge(hid_ps, NC * a.i)
                        nc.scalar.activation(xnT[:, :], X[:, :], ACT.Copy).then_inc(xT_ok, 1)
                    if k == 2 and on[3]:
                        act.wait_ge(mT_ps, t.i + 1)
                        if past(16 * t.i):
                            act.wait_ge(m_out, 16 * t.i)
                        nc.scalar.activation(mT[:, :], X[0:3 * NH, 0:S // 2].bitcast(BF16), ACT.Copy).then_inc(mT_ok, 1)
                    if k == 8 and on[1]:
                        act.wait_ge(low_ps, a.i + 1)
                        nc.scalar.activation(lowT[:, :], X[:, :], ACT.Copy).then_inc(lowT_ok, 1)
                    if 10 <= k < 10 + NC and on[1]:
                        c = k - 10
                        act.wait_ge(hid_ps, NC * a.i + c + 1)
                        if past(a.i):
                            act.wait_ge(ffn_ps, a.i)
                        nc.scalar.activation(hid[:, c, :], G[c % 2][:, :], ACT.Relu, bias=prm("wi_b")[:, c:c + 1]
                                             ).then_inc(hid_ok, 1)
                    if n == 4:
                        seq, q, live = value_quad_of(j, t, u, on)
                        if live:
                            act.wait_ge(av_ps, 4 * seq.i + q + 1)
                            if past(16 * (2 * seq.i + q // 2)):
                                act.wait_ge(o_out[q % 2], 16 * (2 * seq.i + q // 2))
                            nc.scalar.activation(avs[:, q % 2, :], AVB[:, :], ACT.Copy).then_inc(avs_ok, 1)
            over_sequences(act, turn, 3, LAG)

        @block.tensor
        def _(pe):
            pe.wait_ge(set_ok, 4)
            pe.wait_ge(dset_ok, 5)

            def maxima(m, j, n):
                if j == 0 and n == 0:
                    pe.wait_ge(stack_in, 16 * 24 * (m.i + 1))
                if past(UN * (4 * m.i + j) + n):
                    pe.wait_ge(max_ok, UN * (4 * m.i + j) + n)
                for h, qt, bank, lo in MUNITS[n]:
                    rows, _, g = head(4 * j + h)
                    w = (qt + 1) * P
                    pe.matmul(MB[:, bank, lo:lo + w], Q[rows, m.par, g, qt * P:w], K[rows, m.par, g, 0:w],
                              start=True, stop=False)
                    mm = pe.matmul(MB[:, bank, lo + qt * P:lo + w], identb[:, :], mask_qk[:, :], start=False, stop=True)
                mm.then_inc(m_ps, 1)

            def scores(t, q, n):
                if n == 0:
                    pe.wait_ge(m_in, 32 * (t.i + 1))
                if past(UN * (4 * t.i + q) + n):
                    pe.wait_ge(exp_ok, UN * (4 * t.i + q) + n)
                for h, kb, bank, lo in TUNITS[n]:
                    _, rows, g = head(4 * q + h)
                    w = S - kb * P
                    pe.matmul(TB[:, bank, lo:lo + w], K[rows, t.par, g, kb * P:(kb + 1) * P], Q[rows, t.par, g, kb * P:S],
                              start=True, stop=False)
                    mm = pe.matmul(TB[:, bank, lo:lo + P], identb[:, :], mask_kq[:, :], start=False, stop=True)
                mm.then_inc(t_ps, 1)

            def values(t, q, kb, buf):
                if kb == 0:
                    if past(UN * (4 * t.i + q + 1)):
                        pe.wait_ge(exp_ok, UN * (4 * t.i + q + 1))
                    if past(4 * t.i + q):
                        pe.wait_ge(avs_ok, 4 * t.i + q)
                    pe.wait_ge(v_ok, t.i + 1)
                w = S - kb * P
                for h in range(4):
                    c = ECOL[(h, kb)]
                    mm = pe.matmul(AVB[32 * h:32 * h + 32, kb * P:S], V[:, t.par, kb, 4 * q + h, :], E[:, buf, c:c + w],
                                   start=(kb == 0), stop=(kb == NT - 1))
                if kb == NT - 1:
                    mm.then_inc(av_ps, 1)

            def general(k, a, t, u, on):
                if k == 0 and on[1]:
                    pe.wait_ge(xn_ok, a.i + 1)
                    if past(a.i):
                        pe.wait_ge(ffn_ok, a.i)
                    for i in range(NT):
                        mm = pe.transpose(X[:, i * P:(i + 1) * P], xn[:, i, :], identf)
                    mm.then_inc(xT_ps, 1)
                if k in (1, 3) and on[1]:
                    if k == 1:
                        pe.wait_ge(xT_ok, a.i + 1)
                        if past(NC * a.i):
                            pe.wait_ge(hid_ok, NC * a.i)
                        if past(a.i - 3):
                            pe.wait_ge(x2_ok, a.i - 3)
                    else:
                        pe.wait_ge(rope_ok, 2 * a.i + 1)
                    names = ("wq", "wqs") if k == 1 else ("wk", "wks")
                    for g in range(2):
                        mm = pe.matmul(G[g][:, :], prm(names[g]), xnT[:, :], start=True, stop=True)
                    mm.then_inc(q_ps if k == 1 else k_ps, 1)
                if k == 2 and on[3]:
                    pe.wait_ge(max_chain.sem, max_chain.steps * (t.i + 1))
                    pe.sem_inc(passed, 1)
                    if on[1]:
                        pe.wait_ge(xT_ok, a.i + 1)
                        pe.sem_inc(passed, 1)
                    pe.wait_ge(ffn_ok, 1)
                    pe.sem_inc(passed, 1)
                    for i in range(NT):
                        mm = pe.transpose(X[0:3 * NH, 0:S // 2].bitcast(BF16)[:, i * P:(i + 1) * P], mparts[:, i, :],
                                          identb[:, :])
                    mm.then_inc(mT_ps, 1)
                if k == 5 and on[1]:
                    if on[3]:
                        pe.wait_ge(mT_ok, t.i + 1)
                    for i in range(NT):
                        mm = pe.matmul(X[:, i * 40:(i + 1) * 40], xnT[:, i * P:(i + 1) * P], prm("ga"),
                                       start=True, stop=True)
                    mm.then_inc(ga_ps, 1)
                if k == 8 and on[1]:
                    pe.wait_ge(top_chain.sem, top_chain.steps * (a.i + 1))
                    for i in range(NT):
                        mm = pe.transpose(X[:, i * P:(i + 1) * P], low[:, i, :], identf)
                    mm.then_inc(low_ps, 1)
                if k == 9 and on[1]:
                    pe.wait_ge(lowT_ok, a.i + 1)
                    for i in range(NT):
                        mm = pe.matmul(X[:, i * P:(i + 1) * P], xnT[:, i * P:(i + 1) * P], prm("wv"),
                                       start=True, stop=True)
                    mm.then_inc(v_ps, 1)
                if 10 <= k < 10 + NC and on[1]:
                    c = k - 10
                    if c == 0:
                        pe.wait_ge(lowT_ok, a.i + 1)
                        if past(2 * a.i + 2):
                            pe.wait_ge(rope_ok, 2 * a.i + 2)
                    elif c >= 2:
                        if past(NC * a.i + c - 1):
                            pe.wait_ge(hid_ok, NC * a.i + c - 1)
                    cols = slice(c * P, (c + 1) * P)
                    pe.matmul(G[c % 2][:, :], prm("wi")[:, cols], xnT[:, :], start=True, stop=False)
                    pe.matmul(G[c % 2][:, :], prm("lora_b")[:, cols], lowT[:, :], start=False, stop=True
                              ).then_inc(hid_ps, 1)
                if 14 <= k < 14 + NT and on[1]:
                    i = k - 14
                    if i == 0:
                        pe.wait_ge(hid_ok, NC * (a.i + 1))
                        pe.wait_ge(v_ok, a.i + 1)
                    for c in range(NC):
                        mm = pe.matmul(X[:, i * P:(i + 1) * P], hid[:, c, i * P:(i + 1) * P],
                                       prm("wof")[:, c * D:(c + 1) * D], start=(c == 0), stop=(c == NC - 1))
                    if i == NT - 1:
                        mm.then_inc(ffn_ps, 1)
                if k == 18 and on[4]:
                    pe.wait_ge(normed_ok, u.i + 1)
                    if on[1]:
                        pe.wait_ge(hid_ok, NC * (a.i + 1))
                    for i in range(NT):
                        mm = pe.matmul(G[0][:, i * P:(i + 1) * P], normed[:, i * P:(i + 1) * P], prm("wo"),
                                       start=True, stop=True)
                    mm.then_inc(wo_ps, 1)

            def turn(pe, s, on):
                a, m, t, u = s.back(1), s.back(2), s.back(3), s.back(4)
                for k in range(4 * UN):
                    j, n = divmod(k, UN)
                    if on[2]:
                        maxima(m, j, n)
                    seq, q, live = quad_of(j, t, u, on)
                    if live:
                        scores(seq, q, n)
                    general(k, a, t, u, on)
                    if n < NT:
                        seq, q, live = value_quad_of(j, t, u, on)
                        if live:
                            values(seq, q, n, (j + 1) % 2)
            over_sequences(pe, turn, 3, LAG)

        @block.vector
        def _(dve):
            for i, (dst, src) in enumerate(((identb, identf), (mask_qk, cst1("mask_qk")), (mask_kq, cst1("mask_kq")))):
                nc.vector.tensor_copy(dst[:, :], src).then_inc(dset_ok, 1)
            for half in range(2):
                nc.vector.memset(K[64 * half + 32:64 * half + 64, :, :, :], 1.0).then_inc(dset_ok, 1)
            dve.wait_ge(set_ok, 4)

            def rowmax(m, j, n):
                dve.wait_ge(m_ps, UN * (4 * m.i + j) + n + 1)
                if j == 0 and n == 0:
                    if past(max_chain.steps * m.i):
                        dve.wait_ge(max_chain.sem, max_chain.steps * m.i)
                red = nc.vector.tensor_reduce
                h = 4 * j + 2 * (n % 2)
                if n < 2:
                    last = red(negmax[:, 3, h:h + 2], MB[:, :, :], AX.X, ALU.max, negate=True)
                elif n < 4:
                    red(negmax[:, 2, h:h + 2], MB[:, :, 0:384], AX.X, ALU.max, negate=True)
                    last = red(negmax[:, 0, h:h + 2], MB[:, :, 384:512], AX.X, ALU.max, negate=True)
                else:
                    last = red(negmax[:, 1, 4 * j:4 * j + 4].rearrange("p (h b) -> p b h", b=2),
                               MB[:, :, :].rearrange("p b (h n) -> p b h n", n=256), AX.X, ALU.max, negate=True)
                last.then_inc(max_ok, 1)

            def split_max(m):
                ch = max_chain
                ch.begin(dve, m)
                dve.wait_ge(max_ok, UN * 4 * (m.i + 1))
                dve.sem_inc(passed, 1)
                if past(m.i):
                    dve.wait_ge(mT_ps, m.i)
                    dve.sem_inc(passed, 1)
                ch.step(nc.vector.tensor_copy(mparts[:, :, 0:NH], negmax[:, :, :]))
                ch.step(nc.vector.tensor_tensor(negmax[:, :, :], negmax[:, :, :], mparts[:, :, 0:NH], ALU.subtract))
                ch.step(nc.vector.tensor_copy(mparts[:, :, NH:2 * NH], negmax[:, :, :]))
                ch.last(nc.vector.tensor_tensor(mparts[:, :, 2 * NH:3 * NH], negmax[:, :, :], mparts[:, :, NH:2 * NH],
                                                ALU.subtract))
                ch.end()

            def rotate(a, side):
                dve.wait_ge(k_ps if side else q_ps, a.i + 1)
                if past(part_chain.steps * (a.i - 1) + 5 * (side + 1)):
                    dve.wait_ge(part_chain.sem, part_chain.steps * (a.i - 1) + 5 * (side + 1))
                nc.vector.tensor_tensor(rope[:, side, 0, :], G[0][:, :], cst1("cos"), ALU.mult)
                nc.vector.tensor_tensor(rope[:, side, 1, :], G[1][:, :], cst1("sin"), ALU.mult).then_inc(rope_ok, 1)

            def top1(a):
                ch, tt = top_chain, nc.vector.tensor_tensor
                te = lambda k: gl[:, k, :].rearrange("p (t e) -> p t e", e=E1)
                per_t = gl[:, 3, 0:NT].unsqueeze(2).to_broadcast([P, NT, E1])
                ga = X[:, 0:NT * 40].rearrange("p (t c) -> p t c", c=40)
                ch.begin(dve, a)
                dve.wait_ge(ga_ps, a.i + 1)
                ch.step(tt(te(0), ga[:, :, 0:E1], prm("gate_b").rearrange("p (t e) -> p t e", e=E1), ALU.add))
                ch.step(nc.vector.tensor_reduce(gl[:, 3, 0:NT], te(0), AX.X, ALU.max))
                ch.step(tt(te(1), te(0), per_t, ALU.is_equal))
                ch.step(tt(te(1), te(1), cst("order").rearrange("p (t e) -> p t e", e=E1), ALU.mult))
                ch.step(nc.vector.tensor_reduce(gl[:, 3, 0:NT], te(1), AX.X, ALU.max))
                ch.step(tt(te(2), te(1), per_t, ALU.is_equal))
                if past(a.i):
                    dve.wait_ge(low_ps, a.i)
                ch.last(tt(low[:, :, 0:E1 * RANK].rearrange("p t (e r) -> p t e r", r=RANK),
                           ga[:, :, E1:40].rearrange("p t (e r) -> p t e r", r=RANK),
                           te(2).unsqueeze(3).to_broadcast([P, NT, E1, RANK]), ALU.mult))
                ch.end()

            def turn(dve, s, on):
                a, m, u = s.back(1), s.back(2), s.back(4)
                if on[0]:
                    x = resid[:, bass.ds(s.i * S, S)].rearrange("p (t d) -> p t d", d=D)
                for k in range(4 * UN):
                    if on[2]:
                        rowmax(m, *divmod(k, UN))
                    if k in (1, 3) and on[1]:
                        rotate(a, k // 2)
                    if k == 4 and on[0]:
                        ln_chain.begin(dve, s)
                        for t in range(NT):
                            last = nc.vector.bn_stats(st6[:, t, :], x[:, t, :])
                        ln_chain.step(last)
                        if past(s.i):
                            dve.wait_ge(rstd_ok, s.i)
                            dve.sem_inc(passed, 1)
                        for t in range(NT):
                            last = nc.vector.bn_aggr(mv[:, t, :], st6[:, t, :])
                        ln_chain.last(last)
                        ln_chain.end()
                    if k == 9 and on[1]:
                        dve.wait_ge(v_ps, a.i + 1)
                        if past(4 * (a.i - 2)):
                            dve.wait_ge(av_ps, 4 * (a.i - 2))
                        nc.vector.tensor_copy(V[:, a.par, :, :, 0:DH],
                                              X[:, :].rearrange("p (t h d) -> p t h d", t=NT, d=DH)).then_inc(v_ok, 1)
                    if k == 5 and on[1]:
                        top1(a)
                    if k == 11 and on[4]:
                        dve.wait_ge(o_in, 32 * (u.i + 1))
                        if past(16 * u.i):
                            dve.wait_ge(r_out, 16 * u.i)
                        nc.vector.reciprocal(recip[:, :], denom[:, :]).then_inc(rec_ok, 1)
                    if k == 13 and on[0]:
                        dve.wait_ge(rstd_ok, s.i + 1)
                        if past(s.i):
                            dve.wait_ge(xT_ps, s.i)
                        for t in range(NT):
                            last = nc.vector.tensor_scalar(xn[:, t, :], x[:, t, :], mv[:, t, 0:1], rstd[:, t:t + 1],
                                                           ALU.subtract, ALU.mult)
                        last.then_inc(xn_ok, 1)
                    if k == 18 and on[1]:
                        xa = resid[:, bass.ds(a.i * S, S)]
                        dve.wait_ge(ffn_ps, a.i + 1)
                        dve.wait_ge(biased_ok, a.i + 1)
                        nc.vector.tensor_tensor(xa, xa, X[:, :], ALU.add).then_inc(ffn_ok, 1)
                    if k == 19 and on[4]:
                        xu = resid[:, bass.ds(u.i * S, S)]
                        dve.wait_ge(wo_ps, u.i + 1)
                        dve.wait_ge(ffn_ok, u.i + 1)
                        nc.vector.tensor_tensor(xu, xu, G[0][:, :], ALU.add).then_inc(x2_ok, 1)
                if on[2]:
                    split_max(m)
            over_sequences(dve, turn, 3, LAG)


class Fields:

    def __init__(self, tile, dram, fields):
        self.tile, self.dram = tile, dram
        self.at, _ = offsets(fields)

    def __call__(self, name):
        a, w = self.at[name]
        return self.tile[:, a:a + w]


def program(nc, x_d, prm0_d, cst0_d, cst_d, prm1_d, cst1_d, out_d):
    passed = nc.alloc_semaphore("waits_passed")
    skew_d = nc.dram_tensor("bias_skew", (P, BIASW), F32)
    scratch = (nc.dram_tensor("qk_parts", (3, 2, 3, P, S), BF16).ap(), nc.dram_tensor("max_rows", (3, 3 * NH, S), BF16).ap(),
               nc.dram_tensor("head_rows", (3, NH * 32, S), F32).ap(), nc.dram_tensor("recip_rows", (3, NH, S), F32).ap())
    with ExitStack() as ctx:
        def fields(name, dram, table):
            _, w = offsets(table)
            return Fields(ctx.enter_context(nc.sbuf_tensor(name, [P, w], F32)), dram, table)

        resid = ctx.enter_context(nc.sbuf_tensor("resid", [P, NSEQ * S], F32))
        cst = fields("consts_sb", cst_d, CONSTS)
        prm1, cst1 = fields("params1_sb", prm1_d, PARAMS1), fields("consts1_sb", cst1_d, CONSTS1)
        layer0(nc, resid, x_d, prm0_d, cst0_d, cst, skew_d, (prm1, cst1), passed)
        layer1(nc, resid, cst, prm1, cst1, out_d, scratch, passed)


def pack(np, fields, values, rows=P):
    at, width = offsets(fields)
    out = np.zeros((rows, width), np.float32)
    for name, (a, w) in at.items():
        val = values[name]
        out[0:val.shape[0], a:a + w] = val
    return out


def layout0(np, v):
    col = lambda a: a.reshape(-1, 1)
    tiled = lambda a, n: np.broadcast_to(np.tile(a, n), (P, n * a.size))
    chunks = lambda a: a.reshape(NC, P, -1).transpose(1, 0, 2).reshape(P, -1)
    return pack(np, PARAMS0, {
        "wqk": v["L0_attn_wqk"], "wv": v["L0_attn_wv"], "bqk": col(v["L0_attn_bqk"]),
        "gamma0": col(v["L0_attn_gamma"][0]), "gamma1": col(v["L0_attn_gamma"][1]),
        "beta0": col(v["L0_attn_beta"][0]), "beta1": col(v["L0_attn_beta"][1]),
        "bv": tiled(v["L0_attn_bv"], NT), "gate": v["L0_ffn_gate"].T, "corr": tiled(v["L0_ffn_corr_bias"], NT),
        "up": v["L0_ffn_up_w"].T, "down": chunks(v["L0_ffn_down_w"].T),
        "fc1": v["L0_ffn_fc1_w"], "w1": v["L0_ffn_w1"].transpose(2, 0, 1).reshape(LAT, HID),
        "w2": v["L0_ffn_w2"].transpose(1, 0, 2).reshape(LAT, HID), "fc2": v["L0_ffn_fc2_w"].T,
        "table": col(v["L0_attn_rel_bias"]),
    })


def layout1(np, v):
    col = lambda a: a.reshape(-1, 1)
    tiled = lambda a, n: np.broadcast_to(np.tile(a, n), (P, n * a.size))
    chunks = lambda a: a.reshape(NC, P, -1).transpose(1, 0, 2).reshape(P, -1)
    swap = np.arange(D) ^ 1
    A = v["L1_ffn_lora_A"].reshape(E1 * RANK, D)
    B = v["L1_ffn_lora_B"].transpose(0, 2, 1).reshape(E1 * RANK, HID)
    return pack(np, PARAMS1, {
        "wq": v["L1_attn_Wq"].T, "wqs": v["L1_attn_Wq"][swap].T, "wk": v["L1_attn_Wk"].T, "wks": v["L1_attn_Wk"][swap].T,
        "wv": v["L1_attn_Wv"].T, "wo": v["L1_attn_Wo"].T,
        "ga": np.concatenate([v["L1_ffn_gate_W"], A]).T, "gate_b": tiled(v["L1_ffn_gate_b"], NT),
        "wi": v["L1_ffn_wi_W"].T, "wi_b": v["L1_ffn_wi_b"].reshape(NC, P).T, "wof": chunks(v["L1_ffn_wo_W"].T),
        "wo_b": tiled(v["L1_ffn_wo_b"], NT), "lora_b": B,
    })


def constants(np):
    exact = BUCKETS // 2
    n = np.maximum(np.arange(BIASW) - (P - 1), 0)
    far = exact + (np.log(np.maximum(n, 1).astype(np.float32) / exact) / np.log(P / exact) * (BUCKETS - exact)).astype(np.int32)
    bucket = np.where(n < exact, n, np.minimum(far, BUCKETS - 1))
    hot = (np.arange(BUCKETS)[:, None] == bucket[None, :]).astype(np.float32)
    r, h = np.arange(3 * E0)[:, None], np.arange(HID)[None, :]
    sel = (h // LAT == r % E0).astype(np.float32)
    c0 = pack(np, CONSTS0, {"hot": hot, "sel": sel, "ones": np.ones((P, P), np.float32)})
    c = pack(np, CONSTS, {"ident": np.eye(P, dtype=np.float32),
                          "order": np.broadcast_to(np.tile(np.arange(E0, 0, -1), NT), (P, NT * E0))})
    freq = (1.0 / np.float32(10000.0) ** (np.arange(0, DH, 2, dtype=np.float32) / DH)).astype(np.float32)
    angle = np.tile(np.repeat(freq, 2), NH)[:, None] * np.arange(S, dtype=np.float32)[None, :]
    sign = np.tile(np.array([-1.0, 1.0], np.float32), D // 2)[:, None]
    i = np.arange(P)
    c1 = pack(np, CONSTS1, {"cos": np.cos(angle), "sin": np.sin(angle) * sign,
                            "mask_qk": np.where(i[None, :] > i[:, None], MASKED, 0.0),
                            "mask_kq": np.where(i[None, :] < i[:, None], MASKED, 0.0)})
    return c0, c, c1


def kernel(**inputs):
    import numpy as np
    import concourse.bacc as bacc
    from concourse.bass_utils import run_bass_kernel_spmd

    v = {n: np.asarray(a) for n, a in inputs.items()}
    c0, c, c1 = constants(np)
    arrays = {"x": np.ascontiguousarray(v["L0_attn_x"]), "params0": layout0(np, v), "consts0": c0, "consts": c,
              "params1": layout1(np, v), "consts1": c1}
    nc = bacc.Bacc("TRN2", target_bir_lowering=False, num_devices=1)
    args = [nc.dram_tensor(n, a.shape, F32, kind="ExternalInput").ap() for n, a in arrays.items()]
    out = nc.dram_tensor("out", (NSEQ, S, D), F32, kind="ExternalOutput").ap()
    program(nc, *args, out)
    r = run_bass_kernel_spmd(nc, [arrays], core_ids=[0])
    return r.results[0]["out"]
```

```python
from contextlib import ExitStack

import concourse.bass as bass
from concourse import mybir

F32 = mybir.dt.float32
BF16 = mybir.dt.bfloat16
ACT = mybir.ActivationFunctionType
ALU = mybir.AluOpType
AX = mybir.AxisListType

P = 128
NSEQ, S, D = 16, 512, 128
NT = S // P
EPS = 1e-5
MASKED = -1e30

E0 = 8
HID = 512
NC = HID // P
LAT = 64
BUCKETS = 32
BIASW = P + S
MU = 0.5 ** 0.5
STD2 = (0.25 * 3.141592653589793) ** 0.5 * 2.0 ** 0.5
ERF_LEAD = 1.589504771458711e-07
ERF_FACTORS = ((6.240601629142306, 19.10411456424337), (-5.013595302101354, 235.38095817050322),
               (-20.055374636116174, 67.20108358292511))
ERF_END = 4.3

NH, DH = 16, 8
E1, RANK = 8, 4

PARAMS0 = [
    ("wqk", D), ("wv", D), ("bqk", 1), ("gamma0", 1), ("gamma1", 1), ("beta0", 1), ("beta1", 1),
    ("bv", S), ("gate", E0), ("corr", NT * E0), ("up", HID), ("down", HID),
    ("fc1", D), ("w1", HID), ("w2", HID), ("fc2", D), ("table", 1),
]
PARAMS1 = [
    ("wq", D), ("wqs", D), ("wk", D), ("wks", D), ("wv", D), ("wo", D),
    ("ga", E1 + E1 * RANK), ("gate_b", NT * E1), ("wi", HID), ("wi_b", NC), ("wof", HID),
    ("wo_b", S), ("lora_b", HID),
]
CONSTS0 = [("hot", BIASW), ("sel", HID), ("ones", P), ("before", NT * E0 * E0)]
CONSTS1 = [("cos", S), ("sin", S), ("mask_qk", P), ("mask_kq", P)]
CONSTS = [("ident", P), ("order", NT * E0)]


def offsets(fields):
    at, out = 0, {}
    for name, width in fields:
        out[name] = (at, width)
        at += width
    return out, at


def past(value):
    return not isinstance(value, int) or value > 0


class Seq:

    def __init__(self, quo, par, n):
        self.quo, self.par, self.n = quo, par, n
        self.i = quo * n + par

    def back(self, k):
        m = self.par - k
        return Seq(self.quo + m // self.n, m % self.n, self.n)


class Chain:

    def __init__(self, sem, steps, passed):
        self.sem, self.steps, self.passed = sem, steps, passed

    def begin(self, eng, s):
        self.eng, self.base, self.n = eng, s.i * self.steps, 0

    def step(self, ins):
        self.n += 1
        ins.then_inc(self.sem, 1)
        self.eng.wait_ge(self.sem, self.base + self.n)
        if not isinstance(self.base, int):
            self.eng.sem_inc(self.passed, 1)

    def last(self, ins):
        self.n += 1
        ins.then_inc(self.sem, 1)

    def end(self):
        assert self.n == self.steps, (self.n, self.steps)


def over_sequences(eng, turn, n, stages):
    last = NSEQ + stages - 1
    lead = stages - 1 + n
    loops = (NSEQ - lead) // n

    def peeled(i):
        turn(eng, Seq(i // n, i % n, n), [0 <= i - k < NSEQ for k in range(stages)])

    for i in range(lead):
        peeled(i)
    with eng.Fori(0, loops) as r:
        for j in range(lead, lead + n):
            turn(eng, Seq(r + j // n, j % n, n), [True] * stages)
    for i in range(lead + loops * n, last):
        peeled(i)


def layer0(nc, resid, x_d, prm0_d, cst0_d, cst, skew_d, for_layer1, passed):
    with ExitStack() as ctx:
        sem = lambda n: ctx.enter_context(nc.semaphore(n))
        sb = lambda n, shape, dt=F32: ctx.enter_context(nc.sbuf_tensor("l0_" + n, shape, dt))
        at0, w0 = offsets(PARAMS0)
        atc, wc = offsets(CONSTS0)
        prm_t, cst_t = sb("params0", [P, w0]), sb("consts0", [P, wc])
        prm = lambda n: prm_t[:, at0[n][0]:at0[n][0] + at0[n][1]]
        cst0 = lambda n: cst_t[:, atc[n][0]:atc[n][0] + atc[n][1]]
        identf = cst("ident")
        identb, selb = sb("identb0", [P, P], BF16), sb("selb", [64, HID], BF16)
        w1f, w2f = sb("w1f", [P, HID]), sb("w2f", [P, NC, D])
        bias, rows, tab = sb("bias", [P, S]), sb("bias_rows", [P, BIASW]), sb("table_cols", [BUCKETS, P])

        with ExitStack() as sctx:
            ssem = lambda n: sctx.enter_context(nc.semaphore(n))
            params_in, folded, scaled, tab_ok = ssem("params_in"), ssem("folded"), ssem("scaled"), ssem("tab_ok")
            later_in = ssem("later_in")
            skew_out, skew_in, made, bias_ok = ssem("skew_out"), ssem("skew_in"), ssem("made"), ssem("bias_ok")
            ps = sctx.enter_context(nc.psum_tensor("fold_ps", [P, 4, 512], F32))
            block = sctx.enter_context(nc.Block())

            @block.sync
            def _(sp):
                sp.dma_start(cst_t[:, :], cst0_d).then_inc(params_in, 16)
                sp.wait_ge(scaled, 2)
                sp.dma_start(skew_d[:, :], rows[:, :]).then_inc(skew_out, 16)
                sp.wait_ge(skew_out, 16)
                sp.dma_start(bias[:, :], bass.AP(tensor=skew_d, offset=P - 1, ap=[[BIASW - 1, P], [1, S]])
                             ).then_inc(skew_in, 16)

            @block.scalar
            def _(act):
                act.dma_start(prm_t[:, :], prm0_d).then_inc(params_in, 16)
                act.dma_start(cst.tile[:, :], cst.dram).then_inc(params_in, 16)
                for f in for_layer1:
                    act.dma_start(f.tile[:, :], f.dram).then_inc(later_in, 16)
                act.wait_ge(later_in, 16 * len(for_layer1))

            @block.gpsimd
            def _(pool):
                pool.wait_ge(skew_in, 16)
                nc.gpsimd.affine_select(out=bias[:, :], in_=bias[:, :], compare_op=ALU.is_ge, fill=MASKED,
                                        base=0, pattern=[[1, S]], channel_multiplier=-1).then_inc(bias_ok, 1)
                pool.wait_ge(bias_ok, 1)

            @block.tensor
            def _(pe):
                pe.wait_ge(params_in, 48)
                pe.matmul(ps[:, 0, :], prm("fc1")[0:LAT], prm("w1")[0:LAT], start=True, stop=True).then_inc(folded, 1)
                for c in range(NC):
                    mm = pe.matmul(ps[:, 1, c * P:(c + 1) * P], prm("w2")[0:LAT, c * P:(c + 1) * P],
                                   prm("fc2")[0:LAT], start=True, stop=True)
                mm.then_inc(folded, 1)
                pe.wait_ge(tab_ok, 1)
                pe.matmul(ps[:, 2, :], tab[:, :], cst0("hot")[0:BUCKETS, 0:S], start=True, stop=True).then_inc(folded, 1)
                pe.matmul(ps[:, 3, 0:BIASW - S], tab[:, :], cst0("hot")[0:BUCKETS, S:BIASW],
                          start=True, stop=True).then_inc(folded, 1)

            @block.vector
            def _(dve):
                dve.wait_ge(params_in, 48)
                nc.vector.tensor_scalar(tab[:, :], cst0("ones")[0:BUCKETS], prm("table")[0:BUCKETS], None, ALU.mult
                                        ).then_inc(tab_ok, 1)
                nc.vector.tensor_copy(identb[:, :], identf).then_inc(made, 1)
                nc.vector.tensor_copy(selb[:, :], cst0("sel")[0:64]).then_inc(made, 1)
                dve.wait_ge(folded, 4)
                nc.vector.tensor_scalar(rows[:, 0:S], ps[:, 2, :], float(D) ** 0.5 / STD2, -MU / STD2, ALU.mult, ALU.add
                                        ).then_inc(scaled, 1)
                nc.vector.tensor_scalar(rows[:, S:BIASW], ps[:, 3, 0:BIASW - S], float(D) ** 0.5 / STD2, -MU / STD2,
                                        ALU.mult, ALU.add).then_inc(scaled, 1)
                nc.vector.tensor_copy(w1f[:, :], ps[:, 0, :]).then_inc(made, 1)
                nc.vector.tensor_copy(w2f[:, :, :].rearrange("p c d -> p (c d)"), ps[:, 1, :]).then_inc(made, 1)
                dve.wait_ge(made, 4)

        xn, xnT = sb("xn", [P, 2, NT, D]), sb("xnT", [P, 2, S])
        sigq, uq, qT, kT = sb("sigq", [P, S]), sb("uq", [P, S]), sb("qT", [P, S]), sb("kT", [P, S])
        vt, sigv, v = sb("vt", [P, S]), sb("sigv", [P, S]), sb("v", [P, 2, NT, D])
        wsc, fac, att = sb("wsc", [P, 1280]), sb("fac", [P, 3, 1280]), sb("att", [P, 2, 1280])
        hr, hs = sb("hr", [P, 2, 512]), sb("hs", [P, 2, NC, S])
        rr, rw, rh = sb("rr", [P, 2, NC, S]), sb("rw", [P, 2, S]), sb("rh", [P, NC, S])
        st6, mv, rstd = sb("st6", [P, NT, 6]), sb("mv", [P, NT, 2]), sb("rstd", [P, NT])
        halfneg = sb("halfneg", [P, NT])
        gts = sb("gts", [P, 2, NT, E0])
        shift = sb("shift", [P, 3])
        sfc, top_s, in_group = sb("sfc", [P, NT, E0]), sb("top_s", [P, NT * 2]), sb("in_group", [P, NT, 2])
        pair_sums = sb("pair_sums", [P, NT * 2, 6])
        above, ties = sb("above", [P, NT, E0, E0]), sb("ties", [P, NT, E0, E0])
        rank, gsum, gate_w, gate_r = (sb("rank", [P, NT, E0]), sb("gsum", [P, NT]), sb("gate_w", [P, NT, E0]),
                                      sb("gate_r", [P, NT, E0]))
        picked = sb("picked", [P, NT, E0 + 1])
        w3 = sb("w3", [P, NT, 64], BF16)
        wT = sb("wT", [64, 2, S], BF16)

        psum = lambda n: ctx.enter_context(nc.psum_tensor(n, [P, 512], F32))
        X, Y = psum("X"), psum("Y")
        G = [psum("G0"), psum("G1")]
        Z = [psum("Z0"), psum("Z1")]
        BC = [psum("BC0"), psum("BC1")]

        x_in = [sem("x_in0"), sem("x_in1")]
        const_ok, rstd_ok, xn_ok = sem("const_ok"), sem("rstd_ok"), sem("xn_ok")
        xT_ps, xT_ok, qk_ps, sigq_ok, uq_ok = sem("xT_ps"), sem("xT_ok"), sem("qk_ps"), sem("sigq_ok"), sem("uq_ok")
        q_ok, k_ok, sim_ps, z_ok, erf_ok, p_ok = sem("q_ok"), sem("k_ok"), sem("sim_ps"), sem("z_ok"), sem("erf_ok"), sem("p_ok")
        v_ps, vt_ok, sigv_ok, v_ok = sem("v_ps"), sem("vt_ok"), sem("sigv_ok"), sem("v_ok")
        gate_ps, gate_ok, hid_ps, relu_ok, hs_ok = sem("gate_ps"), sem("gate_ok"), sem("hid_ps"), sem("relu_ok"), sem("hs_ok")
        wT_ps, wT_ok, bc_ps, rw_ok, rh_ok = sem("wT_ps"), sem("wT_ok"), sem("bc_ps"), sem("rw_ok"), sem("rh_ok")
        y_ps, x1_ok, clamp_ok, sq_ok = sem("y_ps"), sem("x1_ok"), sem("clamp_ok"), sem("sq_ok")
        poly_ok, gate_step, w3_ok = sem("poly_ok"), sem("gate_step"), sem("w3_ok")
        POLY, GATING = 9, 14
        ln_chain = Chain(sem("ln_chain"), 2, passed)
        pool_chain = Chain(sem("pool_chain"), 1, passed)

        KB = [(0, 0, 512), (1, 512, 384), (2, 1024, 256), (3, 896, 128)]
        UNITS = [(0, 512), (512, 512), (1024, 256)]
        block = ctx.enter_context(nc.Block())

        @block.sync
        def _(sp):
            def turn(sp, s, on):
                if past(2 * (s.i - 1)):
                    sp.wait_ge(ln_chain.sem, 2 * (s.i - 1))
                sp.dma_start(resid[:, bass.ds(s.i * S, S)].rearrange("p (t d) -> p t d", d=D),
                             x_d[bass.ds(s.i, 1), :, :].rearrange("s (t p) d -> p (s t) d", p=P)
                             ).then_inc(x_in[s.par], 16)
            over_sequences(sp, turn, 2, 1)

        @block.gpsimd
        def _(pool):
            nc.gpsimd.memset(halfneg[:, :], -0.5).then_inc(const_ok, 1)
            nc.gpsimd.memset(w3[:, :, :], 0.0).then_inc(const_ok, 1)
            nc.gpsimd.memset(picked[:, :, :], 1e-20).then_inc(const_ok, 1)
            for i in range(3):
                nc.gpsimd.memset(shift[:, i:i + 1], ERF_FACTORS[i][0]).then_inc(const_ok, 1)
            pool.wait_ge(const_ok, 6)

            def routed(b, c):
                pool.wait_ge(rw_ok, NC * b.i + c + 1)
                nc.gpsimd.tensor_tensor(rh[:, c, :], rw[:, c % 2, :], rr[:, b.par, c, :], ALU.mult).then_inc(rh_ok, 1)

            def turn(pool, s, on):
                a, b = s.back(1), s.back(2)
                if on[0]:
                    pool.wait_ge(ln_chain.sem, 2 * (s.i + 1))
                    pool.sem_inc(passed, 1)
                    pool_chain.begin(pool, s)
                    pool_chain.step(nc.gpsimd.tensor_scalar(rstd[:, :], mv[:, :, 1], EPS, None, ALU.add))
                    nc.gpsimd.tensor_tensor(rstd[:, :], rstd[:, :], halfneg[:, :], ALU.pow).then_inc(rstd_ok, 1)
                    pool_chain.end()
                if on[1]:
                    pool.wait_ge(uq_ok, a.i + 1)
                    pool.sem_inc(passed, 1)
                    if past(4 * a.i):
                        pool.wait_ge(sim_ps, 4 * a.i)
                        pool.sem_inc(passed, 1)
                    nc.gpsimd.tensor_scalar(kT[:, :], uq[:, :], prm("gamma1"), prm("beta1"), ALU.mult, ALU.add
                                            ).then_inc(k_ok, 1)
                if on[2]:
                    pool.wait_ge(erf_ok, b.i + 1)
                    pool.sem_inc(passed, 1)
                    nc.gpsimd.tensor_scalar(att[:, b.par, :], att[:, b.par, :], 0.5, 0.5, ALU.mult, ALU.add
                                            ).then_inc(p_ok, 1)
                    if past(b.i):
                        pool.wait_ge(y_ps, b.i)
                    routed(b, 0)
                if on[1]:
                    pool.wait_ge(sigv_ok, a.i + 1)
                    pool.sem_inc(passed, 1)
                    pool.wait_ge(vt_ok, a.i + 1)
                    pool.sem_inc(passed, 1)
                    if past(a.i - 1):
                        pool.wait_ge(y_ps, a.i - 1)
                    nc.gpsimd.tensor_tensor(v[:, a.par, :, :].rearrange("p t d -> p (t d)"), vt[:, :], sigv[:, :],
                                            ALU.mult).then_inc(v_ok, 1)
                if on[2]:
                    for c in range(1, NC):
                        routed(b, c)
            over_sequences(pool, turn, 2, 3)

        @block.scalar
        def _(act):
            def relu(a, g):
                act.wait_ge(hid_ps, 8 * a.i + g)
                src = G[(9 * a.par + g) % 2][:, :]
                if g <= NC:
                    if past(NC * a.i + g - 2):
                        act.wait_ge(hs_ok, NC * a.i + g - 2)
                    nc.scalar.activation(hr[:, g % 2, :], src, ACT.Relu).then_inc(relu_ok, 1)
                else:
                    if past(NC * (a.i - 1)):
                        act.wait_ge(rh_ok, NC * (a.i - 1))
                    nc.scalar.activation(rr[:, a.par, g - 5, :], src, ACT.Relu).then_inc(relu_ok, 1)

            def square(a, g):
                act.wait_ge(relu_ok, 8 * a.i + g)
                if g == 1:
                    if past(a.i - 1):
                        act.wait_ge(y_ps, a.i - 1)
                nc.scalar.activation(hs[:, a.par, g - 1, :], hr[:, g % 2, :], ACT.Square).then_inc(hs_ok, 1)

            act.wait_ge(const_ok, 6)

            def turn(act, s, on):
                a, b = s.back(1), s.back(2)
                if on[2]:
                    act.wait_ge(wT_ps, b.i + 1)
                    if past(NC * (b.i - 1)):
                        act.wait_ge(bc_ps, NC * (b.i - 1))
                    nc.scalar.activation(wT[:, b.par, :], BC[1][0:64, 0:S // 2].bitcast(BF16), ACT.Copy
                                         ).then_inc(wT_ok, 1)
                if on[1]:
                    act.wait_ge(qk_ps, a.i + 1)
                    if past(a.i):
                        act.wait_ge(uq_ok, a.i)
                    nc.scalar.activation(sigq[:, :], G[(9 * a.par) % 2][:, :], ACT.Sigmoid, bias=prm("bqk")
                                         ).then_inc(sigq_ok, 1)
                    relu(a, 1)
                if on[2]:
                    act.wait_ge(poly_ok, POLY * (b.i + 1))
                    nc.scalar.activation(att[:, b.par, :], att[:, b.par, :], ACT.Tanh, scale=ERF_LEAD
                                         ).then_inc(erf_ok, 1)
                if on[1]:
                    relu(a, 2)
                    act.wait_ge(vt_ok, a.i + 1)
                    if past(a.i):
                        act.wait_ge(v_ok, a.i)
                    nc.scalar.activation(sigv[:, :], vt[:, :], ACT.Sigmoid).then_inc(sigv_ok, 1)
                    square(a, 1)
                    square(a, 2)
                    act.wait_ge(gate_ps, a.i + 1)
                    nc.scalar.activation(gts[:, a.par, :, :], BC[0][:, 0:NT * E0].rearrange("p (t e) -> p t e", e=E0),
                                         ACT.Sigmoid).then_inc(gate_ok, 1)
                    relu(a, 3)
                    relu(a, 4)
                    square(a, 3)
                    square(a, 4)
                    for g in range(NC + 1, 2 * NC + 1):
                        relu(a, g)
                    for u, (c, w) in enumerate(UNITS):
                        act.wait_ge(clamp_ok, 3 * a.i + u + 1)
                        if past(POLY * a.i):
                            act.wait_ge(poly_ok, POLY * a.i)
                        nc.scalar.activation(fac[:, 2, c:c + w], wsc[:, c:c + w], ACT.Square).then_inc(sq_ok, 1)
                    for i in range(3):
                        if past(6 * a.i + (3, 3, 5)[i]):
                            act.wait_ge(sq_ok, 6 * a.i + (3, 3, 5)[i])
                        nc.scalar.activation(fac[:, i, :], fac[:, 2, :], ACT.Square, bias=shift[:, i:i + 1]
                                             ).then_inc(sq_ok, 1)
            over_sequences(act, turn, 2, 3)

        @block.tensor
        def _(pe):
            def hidden(a, g):
                bank = G[(9 * a.par + g) % 2]
                if g == 1:
                    if past(8 * a.i):
                        pe.wait_ge(relu_ok, 8 * a.i)
                elif g == 2:
                    pe.wait_ge(uq_ok, a.i + 1)
                else:
                    if past(8 * a.i + g - 2):
                        pe.wait_ge(relu_ok, 8 * a.i + g - 2)
                w = prm("up")[:, (g - 1) * P:g * P] if g <= NC else w1f[:, (g - 5) * P:(g - 4) * P]
                pe.matmul(bank[:, :], w, xnT[:, a.par, :], start=True, stop=True).then_inc(hid_ps, 1)

            def scores(a, kb, bank, lo):
                w = S - kb * P
                pe.matmul(bank[:, lo:lo + w], kT[:, kb * P:(kb + 1) * P], qT[:, kb * P:S], start=True, stop=True
                          ).then_inc(sim_ps, 1)

            def spread(b, c):
                if c < 2:
                    pe.wait_ge(wT_ok, b.i + 1)
                if past(NC * b.i + c - 1):
                    pe.wait_ge(rw_ok, NC * b.i + c - 1)
                pe.matmul(BC[c % 2][:, :], selb[:, c * P:(c + 1) * P], wT[:, b.par, :], start=True, stop=True
                          ).then_inc(bc_ps, 1)

            def output(b, t):
                if t == 0:
                    if past(b.i):
                        pe.wait_ge(x1_ok, b.i)
                    pe.wait_ge(p_ok, b.i + 1)
                    pe.wait_ge(v_ok, b.i + 1)
                    pe.wait_ge(hs_ok, NC * (b.i + 1))
                out, q = Y[:, t * P:(t + 1) * P], slice(t * P, (t + 1) * P)
                for kb, c, w in KB[:t + 1]:
                    lo = c + (t - kb) * P
                    pe.matmul(out, att[:, b.par, lo:lo + P], v[:, b.par, kb, :], start=(kb == 0), stop=False)
                for c in range(NC):
                    pe.matmul(out, hs[:, b.par, c, q], prm("down")[:, c * D:(c + 1) * D], start=False, stop=False)
                if t == 0:
                    pe.wait_ge(rh_ok, NC * (b.i + 1))
                for c in range(NC):
                    mm = pe.matmul(out, rh[:, c, q], w2f[:, c, :], start=False, stop=(c == NC - 1))
                if t == NT - 1:
                    mm.then_inc(y_ps, 1)

            def turn(pe, s, on):
                a, b = s.back(1), s.back(2)
                if on[2]:
                    pe.wait_ge(w3_ok, b.i + 1)
                    pe.sem_inc(passed, 1)
                    if past(NC * b.i):
                        pe.wait_ge(rw_ok, NC * b.i)
                        pe.sem_inc(passed, 1)
                    for t in range(NT):
                        mm = pe.transpose(BC[1][0:64, 0:S // 2].bitcast(BF16)[:, t * P:(t + 1) * P], w3[:, t, :],
                                          identb[:, :])
                    mm.then_inc(wT_ps, 1)
                if on[1]:
                    pe.wait_ge(xT_ok, a.i + 1)
                    if past(8 * a.i - 1):
                        pe.wait_ge(relu_ok, 8 * a.i - 1)
                    pe.matmul(G[(9 * a.par) % 2][:, :], prm("wqk"), xnT[:, a.par, :], start=True, stop=True
                              ).then_inc(qk_ps, 1)
                    hidden(a, 1)
                if on[2]:
                    spread(b, 0)
                if on[1]:
                    for t in range(NT):
                        mm = pe.matmul(X[:, t * P:(t + 1) * P], xnT[:, a.par, t * P:(t + 1) * P], prm("wv"),
                                       start=True, stop=True)
                    mm.then_inc(v_ps, 1)
                    hidden(a, 2)
                if on[2]:
                    spread(b, 1)
                if on[1]:
                    if past(NC * (a.i - 1) + 1):
                        pe.wait_ge(rw_ok, NC * (a.i - 1) + 1)
                    for t in range(NT):
                        mm = pe.matmul(BC[0][:, t * E0:(t + 1) * E0], xnT[:, a.par, t * P:(t + 1) * P], prm("gate"),
                                       start=True, stop=True)
                    mm.then_inc(gate_ps, 1)
                    hidden(a, 3)
                    pe.wait_ge(q_ok, a.i + 1)
                    pe.wait_ge(k_ok, a.i + 1)
                    if past(3 * a.i):
                        pe.wait_ge(z_ok, 3 * a.i)
                    scores(a, 0, Z[0], 0)
                if on[2]:
                    if on[1]:
                        pe.wait_ge(gate_ok, a.i + 1)
                    spread(b, 2)
                if on[1]:
                    scores(a, 1, Z[1], 0)
                    scores(a, 3, Z[1], 384)
                    hidden(a, 4)
                if on[2]:
                    spread(b, 3)
                if on[1]:
                    pe.wait_ge(z_ok, 3 * a.i + 1)
                    scores(a, 2, Z[0], 0)
                    for g in range(NC + 1, 2 * NC + 1):
                        hidden(a, g)
                for t in range(NT):
                    if on[2]:
                        output(b, t)
                    if t == 0 and on[0]:
                        pe.wait_ge(xn_ok, s.i + 1)
                        if past(s.i):
                            pe.wait_ge(vt_ok, s.i)
                        for i in range(NT):
                            mm = pe.transpose(X[:, i * P:(i + 1) * P], xn[:, s.par, i, :], identf)
                        mm.then_inc(xT_ps, 1)
            over_sequences(pe, turn, 2, 3)

        @block.vector
        def _(dve):
            dve.wait_ge(const_ok, 6)

            def gating(a, k):
                tt, red = nc.vector.tensor_tensor, nc.vector.tensor_reduce
                score, parts = gts[:, a.par, :, :], lambda m: w3[:, :, m * E0:(m + 1) * E0]
                grp = sfc[:, :, :].rearrange("p t (g e) -> p (t g) e", e=E0 // 2)
                if k == 0:
                    dve.wait_ge(gate_ok, a.i + 1)
                    last = tt(sfc[:, :, :], score, prm("corr").rearrange("p (t e) -> p t e", e=E0), ALU.add)
                else:
                    dve.wait_ge(gate_step, GATING * a.i + k)
                if k == 1:
                    tt(pair_sums[:, :, 0:3], grp[:, :, 0:3], grp[:, :, 1:4], ALU.add)
                    tt(pair_sums[:, :, 3:5], grp[:, :, 0:2], grp[:, :, 2:4], ALU.add)
                    last = tt(pair_sums[:, :, 5:6], grp[:, :, 0:1], grp[:, :, 3:4], ALU.add)
                if k == 2:
                    last = red(top_s[:, :], pair_sums[:, :, :], AX.X, ALU.max)
                if k == 3:
                    ts = top_s[:, :].rearrange("p (t g) -> p t g", g=2)
                    tt(in_group[:, :, 0:1], ts[:, :, 0:1], ts[:, :, 1:2], ALU.is_ge)
                    last = tt(in_group[:, :, 1:2], ts[:, :, 0:1], ts[:, :, 1:2], ALU.is_lt)
                if k == 4:
                    last = tt(grp, grp, in_group[:, :, :].rearrange("p t g -> p (t g)").unsqueeze(2)
                              .to_broadcast([P, 2 * NT, E0 // 2]), ALU.mult)
                if k == 5:
                    other = sfc[:, :, :].unsqueeze(2).to_broadcast([P, NT, E0, E0])
                    own = sfc[:, :, :].unsqueeze(3).to_broadcast([P, NT, E0, E0])
                    tt(above[:, :, :, :], other, own, ALU.is_gt)
                    last = tt(ties[:, :, :, :], other, own, ALU.is_ge)
                flat = lambda m: m[:, :, :, :].rearrange("p t e f -> p (t e f)")
                if k == 6:
                    last = tt(flat(ties), flat(ties), cst0("before"), ALU.mult)
                if k == 7:
                    last = tt(flat(above), flat(above), flat(ties), ALU.max)
                if k == 8:
                    last = red(rank[:, :, :], above[:, :, :, :], AX.X, ALU.add)
                if k == 9:
                    last = nc.vector.scalar_tensor_tensor(out=picked[:, :, 0:E0], in0=rank[:, :, :], scalar=1.5,
                                                          in1=score, op0=ALU.is_lt, op1=ALU.mult)
                if k == 10:
                    last = red(gsum[:, :], picked[:, :, :], AX.X, ALU.add)
                if k == 11:
                    last = nc.vector.reciprocal(gsum[:, :], gsum[:, :])
                if k == 12:
                    inverse = gsum[:, :].unsqueeze(2).to_broadcast([P, NT, E0])
                    tt(gate_w[:, :, :], picked[:, :, 0:E0], inverse, ALU.mult)
                    if past(a.i):
                        dve.wait_ge(wT_ps, a.i)
                    last = tt(parts(0), picked[:, :, 0:E0], inverse, ALU.mult)
                if k == 13:
                    tt(gate_r[:, :, :], gate_w[:, :, :], parts(0), ALU.subtract)
                    last = tt(parts(1), gate_w[:, :, :], parts(0), ALU.subtract)
                last.then_inc(gate_step, 1)

            def gating_end(a):
                dve.wait_ge(gate_step, GATING * (a.i + 1))
                nc.vector.tensor_tensor(w3[:, :, 2 * E0:3 * E0], gate_r[:, :, :], w3[:, :, E0:2 * E0], ALU.subtract
                                        ).then_inc(w3_ok, 1)

            def polynomial(a, i, u):
                c, w = UNITS[u]
                t = att[:, a.par, c:c + w]
                if past(6 * a.i + 4 + i):
                    dve.wait_ge(sq_ok, 6 * a.i + 4 + i)
                if i == 0:
                    if past(a.i - 1):
                        dve.wait_ge(y_ps, a.i - 1)
                else:
                    dve.wait_ge(poly_ok, POLY * a.i + 3 * (i - 1) + u + 1)
                nc.vector.scalar_tensor_tensor(out=t, in0=fac[:, i, c:c + w], scalar=ERF_FACTORS[i][1],
                                               in1=(t if i else wsc[:, c:c + w]), op0=ALU.add, op1=ALU.mult
                                               ).then_inc(poly_ok, 1)

            def scaled(b, c):
                dve.wait_ge(bc_ps, NC * b.i + c + 1)
                if past(NC * b.i + c - 1):
                    dve.wait_ge(rh_ok, NC * b.i + c - 1)
                nc.vector.tensor_tensor(rw[:, c % 2, :], rr[:, b.par, c, :], BC[c % 2][:, :], ALU.mult
                                        ).then_inc(rw_ok, 1)

            def biased(a, u):
                for kb, c, w in KB:
                    if UNITS[u][0] <= c < UNITS[u][0] + UNITS[u][1]:
                        dve.wait_ge(sim_ps, 4 * a.i + (1, 3, 4)[u])
                        last = nc.vector.scalar_tensor_tensor(
                            out=wsc[:, c:c + w], in0=Z[u % 2][:, c - UNITS[u][0]:c - UNITS[u][0] + w],
                            scalar=1.0 / (S * STD2), in1=bias[:, 0:w], op0=ALU.mult, op1=ALU.add)
                last.then_inc(z_ok, 1)

            def clamp(a, u):
                c, w = UNITS[u]
                dve.wait_ge(z_ok, 3 * a.i + u + 1)
                nc.vector.tensor_scalar(wsc[:, c:c + w], wsc[:, c:c + w], ERF_END, -ERF_END, ALU.min, ALU.max
                                        ).then_inc(clamp_ok, 1)

            def normalise(s, x, tiles):
                dve.wait_ge(rstd_ok, s.i + 1)
                if past(s.i - 1):
                    dve.wait_ge(xT_ps, s.i - 1)
                for t in tiles:
                    last = nc.vector.tensor_scalar(xn[:, s.par, t, :], x[:, t, :], mv[:, t, 0:1], rstd[:, t:t + 1],
                                                   ALU.subtract, ALU.mult)
                if t == NT - 1:
                    last.then_inc(xn_ok, 1)

            def turn(dve, s, on):
                a, b = s.back(1), s.back(2)
                if on[0]:
                    x = resid[:, bass.ds(s.i * S, S)].rearrange("p (t d) -> p t d", d=D)
                    dve.wait_ge(x_in[s.par], 16 * (s.quo + 1))
                    ln_chain.begin(dve, s)
                    for t in range(NT):
                        last = nc.vector.bn_stats(st6[:, t, :], x[:, t, :])
                    ln_chain.step(last)
                    if past(s.i):
                        dve.wait_ge(rstd_ok, s.i)
                        dve.sem_inc(passed, 1)
                    for t in range(NT):
                        last = nc.vector.bn_aggr(mv[:, t, :], st6[:, t, :])
                    ln_chain.last(last)
                    ln_chain.end()
                if on[1]:
                    dve.wait_ge(sigq_ok, a.i + 1)
                    if past(a.i):
                        dve.wait_ge(k_ok, a.i)
                    nc.vector.scalar_tensor_tensor(out=uq[:, :], in0=G[(9 * a.par) % 2][:, :], scalar=prm("bqk"),
                                                   in1=sigq[:, :], op0=ALU.add, op1=ALU.mult).then_inc(uq_ok, 1)
                if on[2]:
                    scaled(b, 0)
                if on[1]:
                    dve.wait_ge(uq_ok, a.i + 1)
                    if past(4 * a.i):
                        dve.wait_ge(sim_ps, 4 * a.i)
                    nc.vector.tensor_scalar(qT[:, :], uq[:, :], prm("gamma0"), prm("beta0"), ALU.mult, ALU.add
                                            ).then_inc(q_ok, 1)
                    dve.wait_ge(v_ps, a.i + 1)
                    if past(a.i):
                        dve.wait_ge(v_ok, a.i)
                    nc.vector.tensor_tensor(vt[:, :], X[:, :], prm("bv"), ALU.add).then_inc(vt_ok, 1)
                if on[2]:
                    scaled(b, 1)
                if on[1]:
                    gating(a, 0)
                if on[0]:
                    normalise(s, x, (0, 1))
                if on[1]:
                    gating(a, 1)
                if on[0]:
                    normalise(s, x, (2, 3))
                if on[1]:
                    gating(a, 2)
                    biased(a, 0)
                    gating(a, 3)
                if on[2]:
                    scaled(b, 2)
                if on[1]:
                    gating(a, 4)
                    biased(a, 1)
                    gating(a, 5)
                if on[2]:
                    scaled(b, 3)
                if on[1]:
                    clamp(a, 0)
                    gating(a, 6)
                    biased(a, 2)
                    gating(a, 7)
                    clamp(a, 1)
                    gating(a, 8)
                    clamp(a, 2)
                    for k in range(9, GATING):
                        gating(a, k)
                    gating_end(a)
                    for u in range(3):
                        polynomial(a, 0, u)
                if on[0]:
                    dve.wait_ge(xT_ps, s.i + 1)
                    if past(8 * (s.i - 1)):
                        dve.wait_ge(hid_ps, 8 * (s.i - 1))
                    nc.vector.tensor_copy(xnT[:, s.par, :], X[:, :]).then_inc(xT_ok, 1)
                if on[1]:
                    for i in (1, 2):
                        for u in range(3):
                            polynomial(a, i, u)
                if on[2]:
                    dve.wait_ge(y_ps, b.i + 1)
                    xb = resid[:, bass.ds(b.i * S, S)]
                    nc.vector.tensor_tensor(xb, xb, Y[:, :], ALU.add).then_inc(x1_ok, 1)
            over_sequences(dve, turn, 2, 3)
            dve.wait_ge(x1_ok, NSEQ)


def layer1(nc, resid, cst, prm, cst1, out_d, scratch, passed):
    QPART, KPART = (0, 0, 0, 1, 1, 2), (0, 1, 2, 0, 1, 0)
    ROWS = 6 * DH
    SCALE = DH ** -0.5
    qk_d, m_d, o_d, r_d = scratch
    with ExitStack() as ctx:
        sem = lambda n: ctx.enter_context(nc.semaphore("b_" + n))
        sb = lambda n, shape, dt=F32: ctx.enter_context(nc.sbuf_tensor("l1_" + n, shape, dt))
        identf = cst("ident")
        identb = sb("identb", [P, P], BF16)
        mask_qk, mask_kq = sb("mask_qk", [P, P], BF16), sb("mask_kq", [P, P], BF16)
        Q, K = sb("Q", [P, 3, NH // 2, S], BF16), sb("K", [P, 3, NH // 2, S], BF16)
        V = sb("V", [P, 3, NT, NH, 32])
        E = sb("E", [P, 2, 5120])
        xn, xnT = sb("xn", [P, NT, D]), sb("xnT", [P, S])
        rope = sb("rope", [P, 2, 2, S])
        parts = sb("parts", [P, 2, 3, S], BF16)
        hid = sb("hid", [P, NC, S])
        low, lowT = sb("low", [P, NT, P]), sb("lowT", [P, S])
        gl = sb("gl", [P, 4, NT * E1])
        st6, mv, rstd, halfneg = sb("st6", [P, NT, 6]), sb("mv", [P, NT, 2]), sb("rstd", [P, NT]), sb("halfneg", [P, NT])
        negmax, mparts, mT = sb("negmax", [P, NT, NH]), sb("mparts", [P, NT, 3 * NH], BF16), sb("mT", [3 * NH, S], BF16)
        avs = sb("avs", [P, 2, S])
        heads, denom, recip, spread, normed = (sb("heads", [P, S]), sb("denom", [P, S // 8]), sb("recip", [P, S // 8]),
                                               sb("spread", [P, S]), sb("normed", [P, S]))

        psum = lambda n, shape: ctx.enter_context(nc.psum_tensor("l1_" + n, shape, F32))
        MB, TB = psum("MB", [P, 2, 512]), psum("TB", [P, 2, 512])
        AVB, X, G = psum("AVB", [P, 512]), psum("X", [P, 512]), [psum("G0", [P, 512]), psum("G1", [P, 512])]

        set_ok, dset_ok, rstd_ok, xn_ok = sem("set_ok"), sem("dset_ok"), sem("rstd_ok"), sem("xn_ok")
        xT_ps, xT_ok, q_ps, k_ps, rope_ok, v_ps, v_ok = (sem("xT_ps"), sem("xT_ok"), sem("q_ps"), sem("k_ps"),
                                                         sem("rope_ok"), sem("v_ps"), sem("v_ok"))
        ga_ps, low_ps, lowT_ok, hid_ps, hid_ok, ffn_ps, ffn_ok = (sem("ga_ps"), sem("low_ps"), sem("lowT_ok"), sem("hid_ps"),
                                                                  sem("hid_ok"), sem("ffn_ps"), sem("ffn_ok"))
        biased_ok = sem("biased_ok")
        m_ps, max_ok, mT_ps, mT_ok, m_out, m_in = (sem("m_ps"), sem("max_ok"), sem("mT_ps"), sem("mT_ok"), sem("m_out"),
                                                   sem("m_in"))
        t_ps, exp_ok, av_ps, avs_ok = sem("t_ps"), sem("exp_ok"), sem("av_ps"), sem("avs_ok")
        parts_out, stack_in = [sem("q_parts_out"), sem("k_parts_out")], sem("stack_in")
        o_out, o_in, rec_ok, r_out, r_in, normed_ok, wo_ps, x2_ok, stored = (
            [sem("even_o_out"), sem("odd_o_out")], sem("o_in"), sem("rec_ok"), sem("r_out"), sem("r_in"), sem("normed_ok"), sem("wo_ps"),
            sem("x2_ok"), sem("stored"))
        ln_chain, pool_chain = Chain(sem("ln_chain"), 2, passed), Chain(sem("pool_chain"), 1, passed)
        part_chain, top_chain = Chain(sem("part_chain"), 10, passed), Chain(sem("top_chain"), 7, passed)
        max_chain = Chain(sem("max_chain"), 4, passed)

        def head(h):
            return slice(64 * (h % 2), 64 * (h % 2) + ROWS), slice(64 * (h % 2), 64 * (h % 2) + ROWS + 3), h // 2

        MUNITS = [[(0, 3, 0, 0), (1, 3, 1, 0)], [(2, 3, 0, 0), (3, 3, 1, 0)],
                  [(0, 2, 0, 0), (0, 0, 0, 384), (1, 2, 1, 0), (1, 0, 1, 384)],
                  [(2, 2, 0, 0), (2, 0, 0, 384), (3, 2, 1, 0), (3, 0, 1, 384)],
                  [(h, 1, h % 2, 256 * (h // 2)) for h in range(4)]]
        TUNITS = [[(h, 0, 0, 0), (h, 1, 1, 0), (h, 3, 1, 384)] for h in range(4)]
        TUNITS.append([(h, 2, h % 2, 256 * (h // 2)) for h in range(4)])
        UN = len(TUNITS)
        ECOL = {(h, kb): unit * 1024 + bank * 512 + col
                for unit, blocks in enumerate(TUNITS) for h, kb, bank, col in blocks}

        LAG = 5

        def quad_of(j, t, u, on):
            return (t, j - 1, on[3]) if j else (u, 3, on[4])

        def value_quad_of(j, t, u, on):
            return [(u, 2, on[4]), (u, 3, on[4]), (t, 0, on[3]), (t, 1, on[3])][j]

        block = ctx.enter_context(nc.Block())

        @block.sync
        def _(sp):
            def turn(sp, s, on):
                a, t, u, v = s.back(1), s.back(3), s.back(4), s.back(5)
                if on[5]:
                    sp.wait_ge(x2_ok, v.i + 1)
                    sp.sem_inc(passed, 1)
                    sp.dma_start(out_d[bass.ds(v.i, 1), :, :].rearrange("s (t p) d -> p (s t) d", p=P),
                                 resid[:, bass.ds(v.i * S, S)].rearrange("p (t d) -> p t d", d=D)).then_inc(stored, 16)
                if on[3]:
                    sp.wait_ge(mT_ok, t.i + 1)
                    sp.sem_inc(passed, 1)
                    if past(32 * t.i):
                        sp.wait_ge(m_in, 32 * t.i)
                        sp.sem_inc(passed, 1)
                    sp.dma_start(m_d[t.par], mT[:, :]).then_inc(m_out, 16)
                    sp.wait_ge(m_out, 16 * (t.i + 1))
                    sp.sem_inc(passed, 1)
                    for half in range(2):
                        rows = m_d[t.par].rearrange("(m g f) n -> f m g n", m=3, f=2)[half]
                        sp.dma_start(Q[64 * half + ROWS:64 * half + ROWS + 3, t.par, :, :], rows).then_inc(m_in, 16)
                if on[4]:
                    store_heads(sp, u, 2)
                if on[1]:
                    for side in range(2):
                        sp.wait_ge(part_chain.sem, part_chain.steps * a.i + 5 * (side + 1))
                        sp.sem_inc(passed, 1)
                        sp.dma_start(qk_d[a.par, side].rearrange("m p n -> p m n"), parts[:, side, :, :]
                                     ).then_inc(parts_out[side], 16)
                    for side in range(2):
                        sp.wait_ge(parts_out[side], 16 * (a.i + 1))
                        sp.sem_inc(passed, 1)
                    if past(UN * 4 * (a.i - 2)):
                        sp.wait_ge(t_ps, UN * 4 * (a.i - 2))
                        sp.sem_inc(passed, 1)
                    if past(16 * 24 * a.i):
                        sp.wait_ge(stack_in, 16 * 24 * a.i)
                        sp.sem_inc(passed, 1)
                    for side, (stack, order) in enumerate(((Q, QPART), (K, KPART))):
                        for slot, part in enumerate(order):
                            for half in range(2):
                                lo = 64 * half + slot * DH
                                rows = qk_d[a.par, side, part].rearrange("(g f d) n -> f d g n", f=2, d=DH)[half]
                                sp.dma_start(stack[lo:lo + DH, a.par, :, :], rows).then_inc(stack_in, 16)
                if on[4]:
                    store_heads(sp, u, 3)
                    for r in range(2):
                        sp.wait_ge(o_out[r], 16 * 2 * (u.i + 1))
                        sp.sem_inc(passed, 1)
                    if past(u.i):
                        sp.wait_ge(normed_ok, u.i)
                        sp.sem_inc(passed, 1)
                    if past(u.i):
                        sp.wait_ge(rec_ok, u.i)
                        sp.sem_inc(passed, 1)
                    o = o_d[u.par].rearrange("(h r) n -> h r n", r=32)
                    sp.dma_start(heads[:, :], o[:, 0:DH, :]).then_inc(o_in, 16)
                    sp.dma_start(denom[:, :], o[:, DH, :].rearrange("h (b n) -> h b n", b=8)).then_inc(o_in, 16)
                    sp.wait_ge(rec_ok, u.i + 1)
                    sp.sem_inc(passed, 1)
                    sp.dma_start(r_d[u.par].rearrange("h (b n) -> (h b) n", b=8), recip[:, :]).then_inc(r_out, 16)
                    sp.wait_ge(r_out, 16 * (u.i + 1))
                    sp.sem_inc(passed, 1)
                    sp.dma_start(spread[:, :], bass.AP(tensor=r_d.tensor, offset=u.par * NH * S,
                                                       ap=[[S, NH], [0, DH], [1, S]])).then_inc(r_in, 16)
                if on[3]:
                    store_heads(sp, t, 0)
                    store_heads(sp, t, 1)

            def store_heads(sp, seq, q):
                sp.wait_ge(avs_ok, 4 * seq.i + q + 1)
                sp.sem_inc(passed, 1)
                sp.dma_start(o_d[seq.par, q * P:(q + 1) * P, :], avs[:, q % 2, :]).then_inc(o_out[q % 2], 16)

            over_sequences(sp, turn, 3, LAG + 1)
            sp.wait_ge(stored, 16 * NSEQ)

        @block.gpsimd
        def _(pool):
            nc.gpsimd.memset(halfneg[:, :], -0.5).then_inc(set_ok, 1)
            nc.gpsimd.memset(low[:, :, :], 0.0).then_inc(set_ok, 1)
            nc.gpsimd.memset(V[:, :, :, :, :], 0.0).then_inc(set_ok, 1)
            pool.wait_ge(set_ok, 3)
            nc.gpsimd.memset(V[:, :, :, :, DH:DH + 1], 1.0).then_inc(set_ok, 1)
            pool.wait_ge(set_ok, 4)

            def split(pool, a, side):
                x, part = rope[:, side, 0, :], lambda k: parts[:, side, k, :]
                pool.wait_ge(rope_ok, 2 * a.i + side + 1)
                pool.sem_inc(passed, 1)
                if past(16 * a.i):
                    pool.wait_ge(parts_out[side], 16 * a.i)
                ch = part_chain
                ch.step(nc.gpsimd.tensor_tensor(x, x, rope[:, side, 1, :], ALU.add))
                ch.step(nc.gpsimd.tensor_scalar(part(0), x, 1.0, None, ALU.mult))
                ch.step(nc.gpsimd.tensor_tensor(x, x, part(0), ALU.subtract))
                ch.step(nc.gpsimd.tensor_scalar(part(1), x, 1.0, None, ALU.mult))
                ch.last(nc.gpsimd.tensor_tensor(part(2), x, part(1), ALU.subtract))

            def turn(pool, s, on):
                a, u = s.back(1), s.back(4)
                if on[1]:
                    part_chain.begin(pool, a)
                    split(pool, a, 0)
                    split(pool, a, 1)
                    part_chain.end()
                if on[0]:
                    pool.wait_ge(ln_chain.sem, 2 * (s.i + 1))
                    pool.sem_inc(passed, 1)
                    pool_chain.begin(pool, s)
                    pool_chain.step(nc.gpsimd.tensor_scalar(rstd[:, :], mv[:, :, 1], EPS, None, ALU.add))
                    nc.gpsimd.tensor_tensor(rstd[:, :], rstd[:, :], halfneg[:, :], ALU.pow).then_inc(rstd_ok, 1)
                    pool_chain.end()
                if on[4]:
                    pool.wait_ge(o_in, 32 * (u.i + 1))
                    pool.wait_ge(r_in, 16 * (u.i + 1))
                    if past(u.i):
                        pool.wait_ge(wo_ps, u.i)
                    nc.gpsimd.tensor_tensor(normed[:, :], heads[:, :], spread[:, :], ALU.mult).then_inc(normed_ok, 1)
                if on[1]:
                    x = resid[:, bass.ds(a.i * S, S)]
                    pool.wait_ge(xn_ok, a.i + 1)
                    nc.gpsimd.tensor_tensor(x, x, prm("wo_b"), ALU.add).then_inc(biased_ok, 1)
            over_sequences(pool, turn, 3, LAG)

        @block.scalar
        def _(act):
            def turn(act, s, on):
                a, t, u = s.back(1), s.back(3), s.back(4)
                for k in range(4 * UN):
                    j, n = divmod(k, UN)
                    seq, q, live = quad_of(j, t, u, on)
                    if live:
                        act.wait_ge(t_ps, UN * (4 * seq.i + q) + n + 1)
                        if n == 0:
                            if past(4 * seq.i + q - 1):
                                act.wait_ge(av_ps, 4 * seq.i + q - 1)
                        nc.scalar.activation(E[:, j % 2, 1024 * n:1024 * (n + 1)],
                                             TB[:, :, :].rearrange("p b n -> p (b n)"), ACT.Exp, scale=SCALE
                                             ).then_inc(exp_ok, 1)
                    if k == 0 and on[1]:
                        act.wait_ge(xT_ps, a.i + 1)
                        if past(NC * a.i):
                            act.wait_ge(hid_ps, NC * a.i)
                        nc.scalar.activation(xnT[:, :], X[:, :], ACT.Copy).then_inc(xT_ok, 1)
                    if k == 2 and on[3]:
                        act.wait_ge(mT_ps, t.i + 1)
                        if past(16 * t.i):
                            act.wait_ge(m_out, 16 * t.i)
                        nc.scalar.activation(mT[:, :], X[0:3 * NH, 0:S // 2].bitcast(BF16), ACT.Copy).then_inc(mT_ok, 1)
                    if k == 8 and on[1]:
                        act.wait_ge(low_ps, a.i + 1)
                        nc.scalar.activation(lowT[:, :], X[:, :], ACT.Copy).then_inc(lowT_ok, 1)
                    if 10 <= k < 10 + NC and on[1]:
                        c = k - 10
                        act.wait_ge(hid_ps, NC * a.i + c + 1)
                        if past(a.i):
                            act.wait_ge(ffn_ps, a.i)
                        nc.scalar.activation(hid[:, c, :], G[c % 2][:, :], ACT.Relu, bias=prm("wi_b")[:, c:c + 1]
                                             ).then_inc(hid_ok, 1)
                    if n == 4:
                        seq, q, live = value_quad_of(j, t, u, on)
                        if live:
                            act.wait_ge(av_ps, 4 * seq.i + q + 1)
                            if past(16 * (2 * seq.i + q // 2)):
                                act.wait_ge(o_out[q % 2], 16 * (2 * seq.i + q // 2))
                            nc.scalar.activation(avs[:, q % 2, :], AVB[:, :], ACT.Copy).then_inc(avs_ok, 1)
            over_sequences(act, turn, 3, LAG)

        @block.tensor
        def _(pe):
            pe.wait_ge(set_ok, 4)
            pe.wait_ge(dset_ok, 5)

            def maxima(m, j, n):
                if j == 0 and n == 0:
                    pe.wait_ge(stack_in, 16 * 24 * (m.i + 1))
                if past(UN * (4 * m.i + j) + n):
                    pe.wait_ge(max_ok, UN * (4 * m.i + j) + n)
                for h, qt, bank, lo in MUNITS[n]:
                    rows, _, g = head(4 * j + h)
                    w = (qt + 1) * P
                    pe.matmul(MB[:, bank, lo:lo + w], Q[rows, m.par, g, qt * P:w], K[rows, m.par, g, 0:w],
                              start=True, stop=False)
                    mm = pe.matmul(MB[:, bank, lo + qt * P:lo + w], identb[:, :], mask_qk[:, :], start=False, stop=True)
                mm.then_inc(m_ps, 1)

            def scores(t, q, n):
                if n == 0:
                    pe.wait_ge(m_in, 32 * (t.i + 1))
                if past(UN * (4 * t.i + q) + n):
                    pe.wait_ge(exp_ok, UN * (4 * t.i + q) + n)
                for h, kb, bank, lo in TUNITS[n]:
                    _, rows, g = head(4 * q + h)
                    w = S - kb * P
                    pe.matmul(TB[:, bank, lo:lo + w], K[rows, t.par, g, kb * P:(kb + 1) * P], Q[rows, t.par, g, kb * P:S],
                              start=True, stop=False)
                    mm = pe.matmul(TB[:, bank, lo:lo + P], identb[:, :], mask_kq[:, :], start=False, stop=True)
                mm.then_inc(t_ps, 1)

            def values(t, q, kb, buf):
                if kb == 0:
                    if past(UN * (4 * t.i + q + 1)):
                        pe.wait_ge(exp_ok, UN * (4 * t.i + q + 1))
                    if past(4 * t.i + q):
                        pe.wait_ge(avs_ok, 4 * t.i + q)
                    pe.wait_ge(v_ok, t.i + 1)
                w = S - kb * P
                for h in range(4):
                    c = ECOL[(h, kb)]
                    mm = pe.matmul(AVB[32 * h:32 * h + 32, kb * P:S], V[:, t.par, kb, 4 * q + h, :], E[:, buf, c:c + w],
                                   start=(kb == 0), stop=(kb == NT - 1))
                if kb == NT - 1:
                    mm.then_inc(av_ps, 1)

            def general(k, a, t, u, on):
                if k == 0 and on[1]:
                    pe.wait_ge(xn_ok, a.i + 1)
                    if past(a.i):
                        pe.wait_ge(ffn_ok, a.i)
                    for i in range(NT):
                        mm = pe.transpose(X[:, i * P:(i + 1) * P], xn[:, i, :], identf)
                    mm.then_inc(xT_ps, 1)
                if k in (1, 3) and on[1]:
                    if k == 1:
                        pe.wait_ge(xT_ok, a.i + 1)
                        if past(NC * a.i):
                            pe.wait_ge(hid_ok, NC * a.i)
                        if past(a.i - 3):
                            pe.wait_ge(x2_ok, a.i - 3)
                    else:
                        pe.wait_ge(rope_ok, 2 * a.i + 1)
                    names = ("wq", "wqs") if k == 1 else ("wk", "wks")
                    for g in range(2):
                        mm = pe.matmul(G[g][:, :], prm(names[g]), xnT[:, :], start=True, stop=True)
                    mm.then_inc(q_ps if k == 1 else k_ps, 1)
                if k == 2 and on[3]:
                    pe.wait_ge(max_chain.sem, max_chain.steps * (t.i + 1))
                    pe.sem_inc(passed, 1)
                    if on[1]:
                        pe.wait_ge(xT_ok, a.i + 1)
                        pe.sem_inc(passed, 1)
                    pe.wait_ge(ffn_ok, 1)
                    pe.sem_inc(passed, 1)
                    for i in range(NT):
                        mm = pe.transpose(X[0:3 * NH, 0:S // 2].bitcast(BF16)[:, i * P:(i + 1) * P], mparts[:, i, :],
                                          identb[:, :])
                    mm.then_inc(mT_ps, 1)
                if k == 5 and on[1]:
                    if on[3]:
                        pe.wait_ge(mT_ok, t.i + 1)
                    for i in range(NT):
                        mm = pe.matmul(X[:, i * 40:(i + 1) * 40], xnT[:, i * P:(i + 1) * P], prm("ga"),
                                       start=True, stop=True)
                    mm.then_inc(ga_ps, 1)
                if k == 8 and on[1]:
                    pe.wait_ge(top_chain.sem, top_chain.steps * (a.i + 1))
                    for i in range(NT):
                        mm = pe.transpose(X[:, i * P:(i + 1) * P], low[:, i, :], identf)
                    mm.then_inc(low_ps, 1)
                if k == 9 and on[1]:
                    pe.wait_ge(lowT_ok, a.i + 1)
                    for i in range(NT):
                        mm = pe.matmul(X[:, i * P:(i + 1) * P], xnT[:, i * P:(i + 1) * P], prm("wv"),
                                       start=True, stop=True)
                    mm.then_inc(v_ps, 1)
                if 10 <= k < 10 + NC and on[1]:
                    c = k - 10
                    if c == 0:
                        pe.wait_ge(lowT_ok, a.i + 1)
                        if past(2 * a.i + 2):
                            pe.wait_ge(rope_ok, 2 * a.i + 2)
                    elif c >= 2:
                        if past(NC * a.i + c - 1):
                            pe.wait_ge(hid_ok, NC * a.i + c - 1)
                    cols = slice(c * P, (c + 1) * P)
                    pe.matmul(G[c % 2][:, :], prm("wi")[:, cols], xnT[:, :], start=True, stop=False)
                    pe.matmul(G[c % 2][:, :], prm("lora_b")[:, cols], lowT[:, :], start=False, stop=True
                              ).then_inc(hid_ps, 1)
                if 14 <= k < 14 + NT and on[1]:
                    i = k - 14
                    if i == 0:
                        pe.wait_ge(hid_ok, NC * (a.i + 1))
                        pe.wait_ge(v_ok, a.i + 1)
                    for c in range(NC):
                        mm = pe.matmul(X[:, i * P:(i + 1) * P], hid[:, c, i * P:(i + 1) * P],
                                       prm("wof")[:, c * D:(c + 1) * D], start=(c == 0), stop=(c == NC - 1))
                    if i == NT - 1:
                        mm.then_inc(ffn_ps, 1)
                if k == 18 and on[4]:
                    pe.wait_ge(normed_ok, u.i + 1)
                    if on[1]:
                        pe.wait_ge(hid_ok, NC * (a.i + 1))
                    for i in range(NT):
                        mm = pe.matmul(G[0][:, i * P:(i + 1) * P], normed[:, i * P:(i + 1) * P], prm("wo"),
                                       start=True, stop=True)
                    mm.then_inc(wo_ps, 1)

            def turn(pe, s, on):
                a, m, t, u = s.back(1), s.back(2), s.back(3), s.back(4)
                for k in range(4 * UN):
                    j, n = divmod(k, UN)
                    if on[2]:
                        maxima(m, j, n)
                    seq, q, live = quad_of(j, t, u, on)
                    if live:
                        scores(seq, q, n)
                    general(k, a, t, u, on)
                    if n < NT:
                        seq, q, live = value_quad_of(j, t, u, on)
                        if live:
                            values(seq, q, n, (j + 1) % 2)
            over_sequences(pe, turn, 3, LAG)

        @block.vector
        def _(dve):
            for i, (dst, src) in enumerate(((identb, identf), (mask_qk, cst1("mask_qk")), (mask_kq, cst1("mask_kq")))):
                nc.vector.tensor_copy(dst[:, :], src).then_inc(dset_ok, 1)
            for half in range(2):
                nc.vector.memset(K[64 * half + 32:64 * half + 64, :, :, :], 1.0).then_inc(dset_ok, 1)
            dve.wait_ge(set_ok, 4)

            def rowmax(m, j, n):
                dve.wait_ge(m_ps, UN * (4 * m.i + j) + n + 1)
                if j == 0 and n == 0:
                    if past(max_chain.steps * m.i):
                        dve.wait_ge(max_chain.sem, max_chain.steps * m.i)
                red = nc.vector.tensor_reduce
                h = 4 * j + 2 * (n % 2)
                if n < 2:
                    last = red(negmax[:, 3, h:h + 2], MB[:, :, :], AX.X, ALU.max, negate=True)
                elif n < 4:
                    red(negmax[:, 2, h:h + 2], MB[:, :, 0:384], AX.X, ALU.max, negate=True)
                    last = red(negmax[:, 0, h:h + 2], MB[:, :, 384:512], AX.X, ALU.max, negate=True)
                else:
                    last = red(negmax[:, 1, 4 * j:4 * j + 4].rearrange("p (h b) -> p b h", b=2),
                               MB[:, :, :].rearrange("p b (h n) -> p b h n", n=256), AX.X, ALU.max, negate=True)
                last.then_inc(max_ok, 1)

            def split_max(m):
                ch = max_chain
                ch.begin(dve, m)
                dve.wait_ge(max_ok, UN * 4 * (m.i + 1))
                dve.sem_inc(passed, 1)
                if past(m.i):
                    dve.wait_ge(mT_ps, m.i)
                    dve.sem_inc(passed, 1)
                ch.step(nc.vector.tensor_copy(mparts[:, :, 0:NH], negmax[:, :, :]))
                ch.step(nc.vector.tensor_tensor(negmax[:, :, :], negmax[:, :, :], mparts[:, :, 0:NH], ALU.subtract))
                ch.step(nc.vector.tensor_copy(mparts[:, :, NH:2 * NH], negmax[:, :, :]))
                ch.last(nc.vector.tensor_tensor(mparts[:, :, 2 * NH:3 * NH], negmax[:, :, :], mparts[:, :, NH:2 * NH],
                                                ALU.subtract))
                ch.end()

            def rotate(a, side):
                dve.wait_ge(k_ps if side else q_ps, a.i + 1)
                if past(part_chain.steps * (a.i - 1) + 5 * (side + 1)):
                    dve.wait_ge(part_chain.sem, part_chain.steps * (a.i - 1) + 5 * (side + 1))
                nc.vector.tensor_tensor(rope[:, side, 0, :], G[0][:, :], cst1("cos"), ALU.mult)
                nc.vector.tensor_tensor(rope[:, side, 1, :], G[1][:, :], cst1("sin"), ALU.mult).then_inc(rope_ok, 1)

            def top1(a):
                ch, tt = top_chain, nc.vector.tensor_tensor
                te = lambda k: gl[:, k, :].rearrange("p (t e) -> p t e", e=E1)
                per_t = gl[:, 3, 0:NT].unsqueeze(2).to_broadcast([P, NT, E1])
                ga = X[:, 0:NT * 40].rearrange("p (t c) -> p t c", c=40)
                ch.begin(dve, a)
                dve.wait_ge(ga_ps, a.i + 1)
                ch.step(tt(te(0), ga[:, :, 0:E1], prm("gate_b").rearrange("p (t e) -> p t e", e=E1), ALU.add))
                ch.step(nc.vector.tensor_reduce(gl[:, 3, 0:NT], te(0), AX.X, ALU.max))
                ch.step(tt(te(1), te(0), per_t, ALU.is_equal))
                ch.step(tt(te(1), te(1), cst("order").rearrange("p (t e) -> p t e", e=E1), ALU.mult))
                ch.step(nc.vector.tensor_reduce(gl[:, 3, 0:NT], te(1), AX.X, ALU.max))
                ch.step(tt(te(2), te(1), per_t, ALU.is_equal))
                if past(a.i):
                    dve.wait_ge(low_ps, a.i)
                ch.last(tt(low[:, :, 0:E1 * RANK].rearrange("p t (e r) -> p t e r", r=RANK),
                           ga[:, :, E1:40].rearrange("p t (e r) -> p t e r", r=RANK),
                           te(2).unsqueeze(3).to_broadcast([P, NT, E1, RANK]), ALU.mult))
                ch.end()

            def turn(dve, s, on):
                a, m, u = s.back(1), s.back(2), s.back(4)
                if on[0]:
                    x = resid[:, bass.ds(s.i * S, S)].rearrange("p (t d) -> p t d", d=D)
                for k in range(4 * UN):
                    if on[2]:
                        rowmax(m, *divmod(k, UN))
                    if k in (1, 3) and on[1]:
                        rotate(a, k // 2)
                    if k == 4 and on[0]:
                        ln_chain.begin(dve, s)
                        for t in range(NT):
                            last = nc.vector.bn_stats(st6[:, t, :], x[:, t, :])
                        ln_chain.step(last)
                        if past(s.i):
                            dve.wait_ge(rstd_ok, s.i)
                            dve.sem_inc(passed, 1)
                        for t in range(NT):
                            last = nc.vector.bn_aggr(mv[:, t, :], st6[:, t, :])
                        ln_chain.last(last)
                        ln_chain.end()
                    if k == 9 and on[1]:
                        dve.wait_ge(v_ps, a.i + 1)
                        if past(4 * (a.i - 2)):
                            dve.wait_ge(av_ps, 4 * (a.i - 2))
                        nc.vector.tensor_copy(V[:, a.par, :, :, 0:DH],
                                              X[:, :].rearrange("p (t h d) -> p t h d", t=NT, d=DH)).then_inc(v_ok, 1)
                    if k == 5 and on[1]:
                        top1(a)
                    if k == 11 and on[4]:
                        dve.wait_ge(o_in, 32 * (u.i + 1))
                        if past(16 * u.i):
                            dve.wait_ge(r_out, 16 * u.i)
                        nc.vector.reciprocal(recip[:, :], denom[:, :]).then_inc(rec_ok, 1)
                    if k == 13 and on[0]:
                        dve.wait_ge(rstd_ok, s.i + 1)
                        if past(s.i):
                            dve.wait_ge(xT_ps, s.i)
                        for t in range(NT):
                            last = nc.vector.tensor_scalar(xn[:, t, :], x[:, t, :], mv[:, t, 0:1], rstd[:, t:t + 1],
                                                           ALU.subtract, ALU.mult)
                        last.then_inc(xn_ok, 1)
                    if k == 18 and on[1]:
                        xa = resid[:, bass.ds(a.i * S, S)]
                        dve.wait_ge(ffn_ps, a.i + 1)
                        dve.wait_ge(biased_ok, a.i + 1)
                        nc.vector.tensor_tensor(xa, xa, X[:, :], ALU.add).then_inc(ffn_ok, 1)
                    if k == 19 and on[4]:
                        xu = resid[:, bass.ds(u.i * S, S)]
                        dve.wait_ge(wo_ps, u.i + 1)
                        dve.wait_ge(ffn_ok, u.i + 1)
                        nc.vector.tensor_tensor(xu, xu, G[0][:, :], ALU.add).then_inc(x2_ok, 1)
                if on[2]:
                    split_max(m)
            over_sequences(dve, turn, 3, LAG)


class Fields:

    def __init__(self, tile, dram, fields):
        self.tile, self.dram = tile, dram
        self.at, _ = offsets(fields)

    def __call__(self, name):
        a, w = self.at[name]
        return self.tile[:, a:a + w]


def program(nc, x_d, prm0_d, cst0_d, cst_d, prm1_d, cst1_d, out_d):
    passed = nc.alloc_semaphore("waits_passed")
    skew_d = nc.dram_tensor("bias_skew", (P, BIASW), F32)
    scratch = (nc.dram_tensor("qk_parts", (3, 2, 3, P, S), BF16).ap(), nc.dram_tensor("max_rows", (3, 3 * NH, S), BF16).ap(),
               nc.dram_tensor("head_rows", (3, NH * 32, S), F32).ap(), nc.dram_tensor("recip_rows", (3, NH, S), F32).ap())
    with ExitStack() as ctx:
        def fields(name, dram, table):
            _, w = offsets(table)
            return Fields(ctx.enter_context(nc.sbuf_tensor(name, [P, w], F32)), dram, table)

        resid = ctx.enter_context(nc.sbuf_tensor("resid", [P, NSEQ * S], F32))
        cst = fields("consts_sb", cst_d, CONSTS)
        prm1, cst1 = fields("params1_sb", prm1_d, PARAMS1), fields("consts1_sb", cst1_d, CONSTS1)
        layer0(nc, resid, x_d, prm0_d, cst0_d, cst, skew_d, (prm1, cst1), passed)
        layer1(nc, resid, cst, prm1, cst1, out_d, scratch, passed)


def pack(np, fields, values, rows=P):
    at, width = offsets(fields)
    out = np.zeros((rows, width), np.float32)
    for name, (a, w) in at.items():
        val = values[name]
        out[0:val.shape[0], a:a + w] = val
    return out


def layout0(np, v):
    col = lambda a: a.reshape(-1, 1)
    tiled = lambda a, n: np.broadcast_to(np.tile(a, n), (P, n * a.size))
    chunks = lambda a: a.reshape(NC, P, -1).transpose(1, 0, 2).reshape(P, -1)
    return pack(np, PARAMS0, {
        "wqk": v["L0_attn_wqk"], "wv": v["L0_attn_wv"], "bqk": col(v["L0_attn_bqk"]),
        "gamma0": col(v["L0_attn_gamma"][0]), "gamma1": col(v["L0_attn_gamma"][1]),
        "beta0": col(v["L0_attn_beta"][0]), "beta1": col(v["L0_attn_beta"][1]),
        "bv": tiled(v["L0_attn_bv"], NT), "gate": v["L0_ffn_gate"].T, "corr": tiled(v["L0_ffn_corr_bias"], NT),
        "up": v["L0_ffn_up_w"].T, "down": chunks(v["L0_ffn_down_w"].T),
        "fc1": v["L0_ffn_fc1_w"], "w1": v["L0_ffn_w1"].transpose(2, 0, 1).reshape(LAT, HID),
        "w2": v["L0_ffn_w2"].transpose(1, 0, 2).reshape(LAT, HID), "fc2": v["L0_ffn_fc2_w"].T,
        "table": col(v["L0_attn_rel_bias"]),
    })


def layout1(np, v):
    col = lambda a: a.reshape(-1, 1)
    tiled = lambda a, n: np.broadcast_to(np.tile(a, n), (P, n * a.size))
    chunks = lambda a: a.reshape(NC, P, -1).transpose(1, 0, 2).reshape(P, -1)
    swap = np.arange(D) ^ 1
    A = v["L1_ffn_lora_A"].reshape(E1 * RANK, D)
    B = v["L1_ffn_lora_B"].transpose(0, 2, 1).reshape(E1 * RANK, HID)
    return pack(np, PARAMS1, {
        "wq": v["L1_attn_Wq"].T, "wqs": v["L1_attn_Wq"][swap].T, "wk": v["L1_attn_Wk"].T, "wks": v["L1_attn_Wk"][swap].T,
        "wv": v["L1_attn_Wv"].T, "wo": v["L1_attn_Wo"].T,
        "ga": np.concatenate([v["L1_ffn_gate_W"], A]).T, "gate_b": tiled(v["L1_ffn_gate_b"], NT),
        "wi": v["L1_ffn_wi_W"].T, "wi_b": v["L1_ffn_wi_b"].reshape(NC, P).T, "wof": chunks(v["L1_ffn_wo_W"].T),
        "wo_b": tiled(v["L1_ffn_wo_b"], NT), "lora_b": B,
    })


def constants(np):
    exact = BUCKETS // 2
    n = np.maximum(np.arange(BIASW) - (P - 1), 0)
    far = exact + (np.log(np.maximum(n, 1).astype(np.float32) / exact) / np.log(P / exact) * (BUCKETS - exact)).astype(np.int32)
    bucket = np.where(n < exact, n, np.minimum(far, BUCKETS - 1))
    hot = (np.arange(BUCKETS)[:, None] == bucket[None, :]).astype(np.float32)
    r, h = np.arange(3 * E0)[:, None], np.arange(HID)[None, :]
    sel = (h // LAT == r % E0).astype(np.float32)
    e = np.arange(E0)
    before = np.broadcast_to(np.tile((e[None, :] < e[:, None]).reshape(-1), NT), (P, NT * E0 * E0))
    c0 = pack(np, CONSTS0, {"hot": hot, "sel": sel, "ones": np.ones((P, P), np.float32), "before": before})
    c = pack(np, CONSTS, {"ident": np.eye(P, dtype=np.float32),
                          "order": np.broadcast_to(np.tile(np.arange(E0, 0, -1), NT), (P, NT * E0))})
    freq = (1.0 / np.float32(10000.0) ** (np.arange(0, DH, 2, dtype=np.float32) / DH)).astype(np.float32)
    angle = np.tile(np.repeat(freq, 2), NH)[:, None] * np.arange(S, dtype=np.float32)[None, :]
    sign = np.tile(np.array([-1.0, 1.0], np.float32), D // 2)[:, None]
    i = np.arange(P)
    c1 = pack(np, CONSTS1, {"cos": np.cos(angle), "sin": np.sin(angle) * sign,
                            "mask_qk": np.where(i[None, :] > i[:, None], MASKED, 0.0),
                            "mask_kq": np.where(i[None, :] < i[:, None], MASKED, 0.0)})
    return c0, c, c1


def kernel(**inputs):
    import numpy as np
    import concourse.bacc as bacc
    from concourse.bass_utils import run_bass_kernel_spmd

    v = {n: np.asarray(a) for n, a in inputs.items()}
    c0, c, c1 = constants(np)
    arrays = {"x": np.ascontiguousarray(v["L0_attn_x"]), "params0": layout0(np, v), "consts0": c0, "consts": c,
              "params1": layout1(np, v), "consts1": c1}
    nc = bacc.Bacc("TRN2", target_bir_lowering=False, num_devices=1)
    args = [nc.dram_tensor(n, a.shape, F32, kind="ExternalInput").ap() for n, a in arrays.items()]
    out = nc.dram_tensor("out", (NSEQ, S, D), F32, kind="ExternalOutput").ap()
    program(nc, *args, out)
    r = run_bass_kernel_spmd(nc, [arrays], core_ids=[0])
    return r.results[0]["out"]
```

```python
from contextlib import ExitStack

import concourse.bass as bass
from concourse import mybir

F32 = mybir.dt.float32
BF16 = mybir.dt.bfloat16
ACT = mybir.ActivationFunctionType
ALU = mybir.AluOpType
AX = mybir.AxisListType

P = 128
NSEQ, S, D = 16, 512, 128
NT = S // P
EPS = 1e-5
MASKED = -1e30

E0 = 8
HID = 512
NC = HID // P
LAT = 64
BUCKETS = 32
BIASW = P + S
MU = 0.5 ** 0.5
STD2 = (0.25 * 3.141592653589793) ** 0.5 * 2.0 ** 0.5
ERF_LEAD = 1.589504771458711e-07
ERF_FACTORS = ((6.240601629142306, 19.10411456424337), (-5.013595302101354, 235.38095817050322),
               (-20.055374636116174, 67.20108358292511))
ERF_END = 4.3

NH, DH = 16, 8
E1, RANK = 8, 4
LOW_BPART = ((0, 1, 2), (0, 1, 0))

PARAMS0 = [
    ("fc1", D), ("w1", HID), ("w2", HID), ("fc2", D), ("table", 1),
    ("lora_b", HID),
    ("wqk", D), ("wv", D), ("bqk", 1), ("gamma0", 1), ("gamma1", 1), ("beta0", 1), ("beta1", 1),
    ("bv", S), ("gate", E0), ("corr", NT * E0), ("up", HID), ("down", HID),
]
PARAMS1 = [
    ("wq", D), ("wk", D), ("wv", D), ("wo", D),
    ("ga", E1 + E1 * RANK), ("gate_b", NT * E1), ("wi", HID), ("wi_b", NC), ("wof", HID),
    ("wo_b", S),
]
CONSTS0 = [("hot", BIASW), ("sel", HID), ("ones", P), ("before", NT * E0 * E0)]
CONSTS1 = [("cos", S), ("sin", S), ("mask_qk", P), ("mask_kq", P)]
CONSTS = [("ident", P), ("order", NT * E0)]


def offsets(fields):
    at, out = 0, {}
    for name, width in fields:
        out[name] = (at, width)
        at += width
    return out, at


def past(value):
    return not isinstance(value, int) or value > 0


class Seq:

    def __init__(self, quo, par, n):
        self.quo, self.par, self.n = quo, par, n
        self.i = quo * n + par

    def back(self, k):
        m = self.par - k
        return Seq(self.quo + m // self.n, m % self.n, self.n)


class Chain:

    def __init__(self, sem, steps, passed):
        self.sem, self.steps, self.passed = sem, steps, passed

    def begin(self, eng, s):
        self.eng, self.base, self.n = eng, s.i * self.steps, 0

    def step(self, ins):
        self.n += 1
        ins.then_inc(self.sem, 1)
        self.eng.wait_ge(self.sem, self.base + self.n)
        if not isinstance(self.base, int):
            self.eng.sem_inc(self.passed, 1)

    def last(self, ins):
        self.n += 1
        ins.then_inc(self.sem, 1)

    def end(self):
        assert self.n == self.steps, (self.n, self.steps)


def over_sequences(eng, turn, n, stages):
    last = NSEQ + stages - 1
    lead = stages - 1 + n
    loops = (NSEQ - lead) // n

    def peeled(i):
        turn(eng, Seq(i // n, i % n, n), [0 <= i - k < NSEQ for k in range(stages)])

    for i in range(lead):
        peeled(i)
    with eng.Fori(0, loops) as r:
        for j in range(lead, lead + n):
            turn(eng, Seq(r + j // n, j % n, n), [True] * stages)
    for i in range(lead + loops * n, last):
        peeled(i)


def layer0(nc, resid, x_d, prm0_d, cst0_d, cst, skew_d, for_layer1, lora_stack, passed):
    with ExitStack() as ctx:
        sem = lambda n: ctx.enter_context(nc.semaphore(n))
        sb = lambda n, shape, dt=F32: ctx.enter_context(nc.sbuf_tensor("l0_" + n, shape, dt))
        at0, w0 = offsets(PARAMS0)
        atc, wc = offsets(CONSTS0)
        prm_t, cst_t = sb("params0", [P, w0]), sb("consts0", [P, wc])
        prm = lambda n: prm_t[:, at0[n][0]:at0[n][0] + at0[n][1]]
        cst0 = lambda n: cst_t[:, atc[n][0]:atc[n][0] + atc[n][1]]
        identf = cst("ident")
        identb, selb = sb("identb0", [P, P], BF16), sb("selb", [64, HID], BF16)
        w1f, w2f = sb("w1f", [P, HID]), sb("w2f", [P, NC, D])
        bias, rows, tab = sb("bias", [P, S]), sb("bias_rows", [P, BIASW]), sb("table_cols", [BUCKETS, P])

        with ExitStack() as sctx:
            ssem = lambda n: sctx.enter_context(nc.semaphore(n))
            params_in, folded, scaled, tab_ok = ssem("params_in"), ssem("folded"), ssem("scaled"), ssem("tab_ok")
            later_in = ssem("later_in")
            skew_out, skew_in, made, bias_ok = ssem("skew_out"), ssem("skew_in"), ssem("made"), ssem("bias_ok")
            ps = sctx.enter_context(nc.psum_tensor("fold_ps", [P, 4, 512], F32))
            R3 = 3 * E1 * RANK
            lora_rest = sctx.enter_context(nc.sbuf_tensor("lora_rest", [R3, 2, HID], F32))
            lora_part = sctx.enter_context(nc.sbuf_tensor("lora_part", [R3, 3, HID], BF16))
            lora_ok, stacked = ssem("lora_ok"), ssem("stacked")
            block = sctx.enter_context(nc.Block())

            @block.sync
            def _(sp):
                sp.dma_start(cst_t[:, :], cst0_d).then_inc(params_in, 16)
                sp.wait_ge(scaled, 2)
                sp.dma_start(skew_d[:, :], rows[:, :]).then_inc(skew_out, 16)
                sp.wait_ge(skew_out, 16)
                sp.dma_start(bias[:, :], bass.AP(tensor=skew_d, offset=P - 1, ap=[[BIASW - 1, P], [1, S]])
                             ).then_inc(skew_in, 16)

            @block.scalar
            def _(act):
                setup = at0["wqk"][0]
                act.dma_start(prm_t[:, 0:setup], prm0_d[:, 0:setup]).then_inc(params_in, 16)
                act.dma_start(cst.tile[:, :], cst.dram).then_inc(params_in, 16)
                act.dma_start(prm_t[:, setup:w0], prm0_d[:, setup:w0]).then_inc(later_in, 16)
                for f in for_layer1:
                    act.dma_start(f.tile[:, :], f.dram).then_inc(later_in, 16)
                act.wait_ge(later_in, 16 * (1 + len(for_layer1)))

            @block.gpsimd
            def _(pool):
                pool.wait_ge(skew_in, 16)
                nc.gpsimd.affine_select(out=bias[:, :], in_=bias[:, :], compare_op=ALU.is_ge, fill=MASKED,
                                        base=0, pattern=[[1, S]], channel_multiplier=-1).then_inc(bias_ok, 1)
                pool.wait_ge(bias_ok, 1)

            @block.tensor
            def _(pe):
                pe.wait_ge(params_in, 48)
                pe.matmul(ps[:, 0, :], prm("fc1")[0:LAT], prm("w1")[0:LAT], start=True, stop=True).then_inc(folded, 1)
                for c in range(NC):
                    mm = pe.matmul(ps[:, 1, c * P:(c + 1) * P], prm("w2")[0:LAT, c * P:(c + 1) * P],
                                   prm("fc2")[0:LAT], start=True, stop=True)
                mm.then_inc(folded, 1)
                pe.wait_ge(tab_ok, 1)
                pe.matmul(ps[:, 2, :], tab[:, :], cst0("hot")[0:BUCKETS, 0:S], start=True, stop=True).then_inc(folded, 1)
                pe.matmul(ps[:, 3, 0:BIASW - S], tab[:, :], cst0("hot")[0:BUCKETS, S:BIASW],
                          start=True, stop=True).then_inc(folded, 1)

            @block.vector
            def _(dve):
                dve.wait_ge(params_in, 48)
                nc.vector.tensor_scalar(tab[:, :], cst0("ones")[0:BUCKETS], prm("table")[0:BUCKETS], None, ALU.mult
                                        ).then_inc(tab_ok, 1)
                nc.vector.tensor_copy(identb[:, :], identf).then_inc(made, 1)
                nc.vector.tensor_copy(selb[:, :], cst0("sel")[0:64]).then_inc(made, 1)
                tt, b = nc.vector.tensor_tensor, prm("lora_b")[0:R3]
                part, rest = lambda k: lora_part[:, k, :], lambda k: lora_rest[:, k, :]
                nc.vector.tensor_scalar(part(0), b, 1.0, None, ALU.mult).then_inc(lora_ok, 1)
                dve.wait_ge(lora_ok, 1)
                tt(part(1), b, part(0), ALU.subtract)
                tt(rest(0), b, part(0), ALU.subtract).then_inc(lora_ok, 1)
                dve.wait_ge(lora_ok, 2)
                tt(part(2), rest(0), part(1), ALU.subtract).then_inc(lora_ok, 1)
                dve.wait_ge(lora_ok, 3)
                for group in range(2):
                    for slot in range(3):
                        ranks = slice(slot * E1 * RANK, (slot + 1) * E1 * RANK)
                        nc.vector.tensor_copy(lora_stack[ranks, group, :], lora_part[ranks, LOW_BPART[group][slot], :]
                                              ).then_inc(stacked, 1)
                dve.wait_ge(stacked, 6)
                dve.wait_ge(folded, 4)
                nc.vector.tensor_scalar(rows[:, 0:S], ps[:, 2, :], float(D) ** 0.5 / STD2, -MU / STD2, ALU.mult, ALU.add
                                        ).then_inc(scaled, 1)
                nc.vector.tensor_scalar(rows[:, S:BIASW], ps[:, 3, 0:BIASW - S], float(D) ** 0.5 / STD2, -MU / STD2,
                                        ALU.mult, ALU.add).then_inc(scaled, 1)
                nc.vector.tensor_copy(w1f[:, :], ps[:, 0, :]).then_inc(made, 1)
                nc.vector.tensor_copy(w2f[:, :, :].rearrange("p c d -> p (c d)"), ps[:, 1, :]).then_inc(made, 1)
                dve.wait_ge(made, 4)

        xn, xnT = sb("xn", [P, 2, NT, D]), sb("xnT", [P, 2, S])
        sigq, uq, qT, kT = sb("sigq", [P, S]), sb("uq", [P, S]), sb("qT", [P, S]), sb("kT", [P, S])
        vt, sigv, v = sb("vt", [P, S]), sb("sigv", [P, S]), sb("v", [P, 2, NT, D])
        wsc, fac, att = sb("wsc", [P, 1280]), sb("fac", [P, 3, 1280]), sb("att", [P, 2, 1280])
        hr, hs = sb("hr", [P, 2, 512]), sb("hs", [P, 2, NC, S])
        rr, rw, rh = sb("rr", [P, 2, NC, S]), sb("rw", [P, 2, S]), sb("rh", [P, NC, S])
        st6, mv, rstd = sb("st6", [P, NT, 6]), sb("mv", [P, NT, 2]), sb("rstd", [P, NT])
        halfneg = sb("halfneg", [P, NT])
        gts = sb("gts", [P, 2, NT, E0])
        shift = sb("shift", [P, 3])
        sfc, top_s, in_group = sb("sfc", [P, NT, E0]), sb("top_s", [P, NT * 2]), sb("in_group", [P, NT, 2])
        pair_sums = sb("pair_sums", [P, NT * 2, 6])
        above, ties = sb("above", [P, NT, E0, E0]), sb("ties", [P, NT, E0, E0])
        rank, gsum, gate_w, gate_r = (sb("rank", [P, NT, E0]), sb("gsum", [P, NT]), sb("gate_w", [P, NT, E0]),
                                      sb("gate_r", [P, NT, E0]))
        picked = sb("picked", [P, NT, E0 + 1])
        w3 = sb("w3", [P, NT, 64], BF16)
        wT = sb("wT", [64, 2, S], BF16)

        psum = lambda n: ctx.enter_context(nc.psum_tensor(n, [P, 512], F32))
        X, Y = psum("X"), psum("Y")
        G = [psum("G0"), psum("G1")]
        Z = [psum("Z0"), psum("Z1")]
        BC = [psum("BC0"), psum("BC1")]

        x_in = [sem("x_in0"), sem("x_in1")]
        const_ok, rstd_ok, xn_ok = sem("const_ok"), sem("rstd_ok"), sem("xn_ok")
        xT_ps, xT_ok, qk_ps, sigq_ok, uq_ok = sem("xT_ps"), sem("xT_ok"), sem("qk_ps"), sem("sigq_ok"), sem("uq_ok")
        q_ok, k_ok, sim_ps, z_ok, erf_ok, p_ok = sem("q_ok"), sem("k_ok"), sem("sim_ps"), sem("z_ok"), sem("erf_ok"), sem("p_ok")
        v_ps, vt_ok, sigv_ok, v_ok = sem("v_ps"), sem("vt_ok"), sem("sigv_ok"), sem("v_ok")
        gate_ps, gate_ok, hid_ps, relu_ok, hs_ok = sem("gate_ps"), sem("gate_ok"), sem("hid_ps"), sem("relu_ok"), sem("hs_ok")
        wT_ps, wT_ok, bc_ps, rw_ok, rh_ok = sem("wT_ps"), sem("wT_ok"), sem("bc_ps"), sem("rw_ok"), sem("rh_ok")
        y_ps, x1_ok, clamp_ok, sq_ok = sem("y_ps"), sem("x1_ok"), sem("clamp_ok"), sem("sq_ok")
        poly_ok, gate_step, w3_ok = sem("poly_ok"), sem("gate_step"), sem("w3_ok")
        POLY, GATING = 9, 14
        ln_chain = Chain(sem("ln_chain"), 2, passed)
        pool_chain = Chain(sem("pool_chain"), 1, passed)

        KB = [(0, 0, 512), (1, 512, 384), (2, 1024, 256), (3, 896, 128)]
        UNITS = [(0, 512), (512, 512), (1024, 256)]
        block = ctx.enter_context(nc.Block())

        @block.sync
        def _(sp):
            def turn(sp, s, on):
                if past(2 * (s.i - 1)):
                    sp.wait_ge(ln_chain.sem, 2 * (s.i - 1))
                sp.dma_start(resid[:, bass.ds(s.i * S, S)].rearrange("p (t d) -> p t d", d=D),
                             x_d[bass.ds(s.i, 1), :, :].rearrange("s (t p) d -> p (s t) d", p=P)
                             ).then_inc(x_in[s.par], 16)
            over_sequences(sp, turn, 2, 1)

        @block.gpsimd
        def _(pool):
            nc.gpsimd.memset(halfneg[:, :], -0.5).then_inc(const_ok, 1)
            nc.gpsimd.memset(w3[:, :, :], 0.0).then_inc(const_ok, 1)
            nc.gpsimd.memset(picked[:, :, :], 1e-20).then_inc(const_ok, 1)
            for i in range(3):
                nc.gpsimd.memset(shift[:, i:i + 1], ERF_FACTORS[i][0]).then_inc(const_ok, 1)
            pool.wait_ge(const_ok, 6)

            def routed(b, c):
                pool.wait_ge(rw_ok, NC * b.i + c + 1)
                nc.gpsimd.tensor_tensor(rh[:, c, :], rw[:, c % 2, :], rr[:, b.par, c, :], ALU.mult).then_inc(rh_ok, 1)

            def turn(pool, s, on):
                a, b = s.back(1), s.back(2)
                if on[0]:
                    pool.wait_ge(ln_chain.sem, 2 * (s.i + 1))
                    pool.sem_inc(passed, 1)
                    pool_chain.begin(pool, s)
                    pool_chain.step(nc.gpsimd.tensor_scalar(rstd[:, :], mv[:, :, 1], EPS, None, ALU.add))
                    nc.gpsimd.tensor_tensor(rstd[:, :], rstd[:, :], halfneg[:, :], ALU.pow).then_inc(rstd_ok, 1)
                    pool_chain.end()
                if on[1]:
                    pool.wait_ge(uq_ok, a.i + 1)
                    pool.sem_inc(passed, 1)
                    if past(4 * a.i):
                        pool.wait_ge(sim_ps, 4 * a.i)
                        pool.sem_inc(passed, 1)
                    nc.gpsimd.tensor_scalar(kT[:, :], uq[:, :], prm("gamma1"), prm("beta1"), ALU.mult, ALU.add
                                            ).then_inc(k_ok, 1)
                if on[2]:
                    pool.wait_ge(erf_ok, b.i + 1)
                    pool.sem_inc(passed, 1)
                    nc.gpsimd.tensor_scalar(att[:, b.par, :], att[:, b.par, :], 0.5, 0.5, ALU.mult, ALU.add
                                            ).then_inc(p_ok, 1)
                    if past(b.i):
                        pool.wait_ge(y_ps, b.i)
                    routed(b, 0)
                if on[1]:
                    pool.wait_ge(sigv_ok, a.i + 1)
                    pool.sem_inc(passed, 1)
                    pool.wait_ge(vt_ok, a.i + 1)
                    pool.sem_inc(passed, 1)
                    if past(a.i - 1):
                        pool.wait_ge(y_ps, a.i - 1)
                    nc.gpsimd.tensor_tensor(v[:, a.par, :, :].rearrange("p t d -> p (t d)"), vt[:, :], sigv[:, :],
                                            ALU.mult).then_inc(v_ok, 1)
                if on[2]:
                    for c in range(1, NC):
                        routed(b, c)
            over_sequences(pool, turn, 2, 3)

        @block.scalar
        def _(act):
            def relu(a, g):
                act.wait_ge(hid_ps, 8 * a.i + g)
                src = G[(9 * a.par + g) % 2][:, :]
                if g <= NC:
                    if past(NC * a.i + g - 2):
                        act.wait_ge(hs_ok, NC * a.i + g - 2)
                    nc.scalar.activation(hr[:, g % 2, :], src, ACT.Relu).then_inc(relu_ok, 1)
                else:
                    if past(NC * (a.i - 1)):
                        act.wait_ge(rh_ok, NC * (a.i - 1))
                    nc.scalar.activation(rr[:, a.par, g - 5, :], src, ACT.Relu).then_inc(relu_ok, 1)

            def square(a, g):
                act.wait_ge(relu_ok, 8 * a.i + g)
                if g == 1:
                    if past(a.i - 1):
                        act.wait_ge(y_ps, a.i - 1)
                nc.scalar.activation(hs[:, a.par, g - 1, :], hr[:, g % 2, :], ACT.Square).then_inc(hs_ok, 1)

            act.wait_ge(const_ok, 6)

            def turn(act, s, on):
                a, b = s.back(1), s.back(2)
                if on[2]:
                    act.wait_ge(wT_ps, b.i + 1)
                    if past(NC * (b.i - 1)):
                        act.wait_ge(bc_ps, NC * (b.i - 1))
                    nc.scalar.activation(wT[:, b.par, :], BC[1][0:64, 0:S // 2].bitcast(BF16), ACT.Copy
                                         ).then_inc(wT_ok, 1)
                if on[1]:
                    act.wait_ge(qk_ps, a.i + 1)
                    if past(a.i):
                        act.wait_ge(uq_ok, a.i)
                    nc.scalar.activation(sigq[:, :], G[(9 * a.par) % 2][:, :], ACT.Sigmoid, bias=prm("bqk")
                                         ).then_inc(sigq_ok, 1)
                    relu(a, 1)
                if on[2]:
                    act.wait_ge(poly_ok, POLY * (b.i + 1))
                    nc.scalar.activation(att[:, b.par, :], att[:, b.par, :], ACT.Tanh, scale=ERF_LEAD
                                         ).then_inc(erf_ok, 1)
                if on[1]:
                    relu(a, 2)
                    act.wait_ge(vt_ok, a.i + 1)
                    if past(a.i):
                        act.wait_ge(v_ok, a.i)
                    nc.scalar.activation(sigv[:, :], vt[:, :], ACT.Sigmoid).then_inc(sigv_ok, 1)
                    square(a, 1)
                    square(a, 2)
                    act.wait_ge(gate_ps, a.i + 1)
                    nc.scalar.activation(gts[:, a.par, :, :], BC[0][:, 0:NT * E0].rearrange("p (t e) -> p t e", e=E0),
                                         ACT.Sigmoid).then_inc(gate_ok, 1)
                    relu(a, 3)
                    relu(a, 4)
                    square(a, 3)
                    square(a, 4)
                    for g in range(NC + 1, 2 * NC + 1):
                        relu(a, g)
                    for u, (c, w) in enumerate(UNITS):
                        act.wait_ge(clamp_ok, 3 * a.i + u + 1)
                        if past(POLY * a.i):
                            act.wait_ge(poly_ok, POLY * a.i)
                        nc.scalar.activation(fac[:, 2, c:c + w], wsc[:, c:c + w], ACT.Square).then_inc(sq_ok, 1)
                    for i in range(3):
                        if past(6 * a.i + (3, 3, 5)[i]):
                            act.wait_ge(sq_ok, 6 * a.i + (3, 3, 5)[i])
                        nc.scalar.activation(fac[:, i, :], fac[:, 2, :], ACT.Square, bias=shift[:, i:i + 1]
                                             ).then_inc(sq_ok, 1)
            over_sequences(act, turn, 2, 3)

        @block.tensor
        def _(pe):
            def hidden(a, g):
                bank = G[(9 * a.par + g) % 2]
                if g == 1:
                    if past(8 * a.i):
                        pe.wait_ge(relu_ok, 8 * a.i)
                elif g == 2:
                    pe.wait_ge(uq_ok, a.i + 1)
                else:
                    if past(8 * a.i + g - 2):
                        pe.wait_ge(relu_ok, 8 * a.i + g - 2)
                w = prm("up")[:, (g - 1) * P:g * P] if g <= NC else w1f[:, (g - 5) * P:(g - 4) * P]
                pe.matmul(bank[:, :], w, xnT[:, a.par, :], start=True, stop=True).then_inc(hid_ps, 1)

            def scores(a, kb, bank, lo):
                w = S - kb * P
                pe.matmul(bank[:, lo:lo + w], kT[:, kb * P:(kb + 1) * P], qT[:, kb * P:S], start=True, stop=True
                          ).then_inc(sim_ps, 1)

            def spread(b, c):
                if c < 2:
                    pe.wait_ge(wT_ok, b.i + 1)
                if past(NC * b.i + c - 1):
                    pe.wait_ge(rw_ok, NC * b.i + c - 1)
                pe.matmul(BC[c % 2][:, :], selb[:, c * P:(c + 1) * P], wT[:, b.par, :], start=True, stop=True
                          ).then_inc(bc_ps, 1)

            def output(b, t):
                if t == 0:
                    if past(b.i):
                        pe.wait_ge(x1_ok, b.i)
                    pe.wait_ge(p_ok, b.i + 1)
                    pe.wait_ge(v_ok, b.i + 1)
                    pe.wait_ge(hs_ok, NC * (b.i + 1))
                out, q = Y[:, t * P:(t + 1) * P], slice(t * P, (t + 1) * P)
                for kb, c, w in KB[:t + 1]:
                    lo = c + (t - kb) * P
                    pe.matmul(out, att[:, b.par, lo:lo + P], v[:, b.par, kb, :], start=(kb == 0), stop=False)
                for c in range(NC):
                    pe.matmul(out, hs[:, b.par, c, q], prm("down")[:, c * D:(c + 1) * D], start=False, stop=False)
                if t == 0:
                    pe.wait_ge(rh_ok, NC * (b.i + 1))
                for c in range(NC):
                    mm = pe.matmul(out, rh[:, c, q], w2f[:, c, :], start=False, stop=(c == NC - 1))
                if t == NT - 1:
                    mm.then_inc(y_ps, 1)

            def turn(pe, s, on):
                a, b = s.back(1), s.back(2)
                if on[2]:
                    pe.wait_ge(w3_ok, b.i + 1)
                    pe.sem_inc(passed, 1)
                    if past(NC * b.i):
                        pe.wait_ge(rw_ok, NC * b.i)
                        pe.sem_inc(passed, 1)
                    for t in range(NT):
                        mm = pe.transpose(BC[1][0:64, 0:S // 2].bitcast(BF16)[:, t * P:(t + 1) * P], w3[:, t, :],
                                          identb[:, :])
                    mm.then_inc(wT_ps, 1)
                if on[1]:
                    pe.wait_ge(xT_ok, a.i + 1)
                    if past(8 * a.i - 1):
                        pe.wait_ge(relu_ok, 8 * a.i - 1)
                    pe.matmul(G[(9 * a.par) % 2][:, :], prm("wqk"), xnT[:, a.par, :], start=True, stop=True
                              ).then_inc(qk_ps, 1)
                    hidden(a, 1)
                if on[2]:
                    spread(b, 0)
                if on[1]:
                    for t in range(NT):
                        mm = pe.matmul(X[:, t * P:(t + 1) * P], xnT[:, a.par, t * P:(t + 1) * P], prm("wv"),
                                       start=True, stop=True)
                    mm.then_inc(v_ps, 1)
                    hidden(a, 2)
                if on[2]:
                    spread(b, 1)
                if on[1]:
                    if past(NC * (a.i - 1) + 1):
                        pe.wait_ge(rw_ok, NC * (a.i - 1) + 1)
                    for t in range(NT):
                        mm = pe.matmul(BC[0][:, t * E0:(t + 1) * E0], xnT[:, a.par, t * P:(t + 1) * P], prm("gate"),
                                       start=True, stop=True)
                    mm.then_inc(gate_ps, 1)
                    hidden(a, 3)
                    pe.wait_ge(q_ok, a.i + 1)
                    pe.wait_ge(k_ok, a.i + 1)
                    if past(3 * a.i):
                        pe.wait_ge(z_ok, 3 * a.i)
                    scores(a, 0, Z[0], 0)
                if on[2]:
                    if on[1]:
                        pe.wait_ge(gate_ok, a.i + 1)
                    spread(b, 2)
                if on[1]:
                    scores(a, 1, Z[1], 0)
                    scores(a, 3, Z[1], 384)
                    hidden(a, 4)
                if on[2]:
                    spread(b, 3)
                if on[1]:
                    pe.wait_ge(z_ok, 3 * a.i + 1)
                    scores(a, 2, Z[0], 0)
                    for g in range(NC + 1, 2 * NC + 1):
                        hidden(a, g)
                for t in range(NT):
                    if on[2]:
                        output(b, t)
                    if t == 0 and on[0]:
                        pe.wait_ge(xn_ok, s.i + 1)
                        if past(s.i):
                            pe.wait_ge(vt_ok, s.i)
                        for i in range(NT):
                            mm = pe.transpose(X[:, i * P:(i + 1) * P], xn[:, s.par, i, :], identf)
                        mm.then_inc(xT_ps, 1)
            over_sequences(pe, turn, 2, 3)

        @block.vector
        def _(dve):
            dve.wait_ge(const_ok, 6)

            def gating(a, k):
                tt, red = nc.vector.tensor_tensor, nc.vector.tensor_reduce
                score, parts = gts[:, a.par, :, :], lambda m: w3[:, :, m * E0:(m + 1) * E0]
                grp = sfc[:, :, :].rearrange("p t (g e) -> p (t g) e", e=E0 // 2)
                if k == 0:
                    dve.wait_ge(gate_ok, a.i + 1)
                    last = tt(sfc[:, :, :], score, prm("corr").rearrange("p (t e) -> p t e", e=E0), ALU.add)
                else:
                    dve.wait_ge(gate_step, GATING * a.i + k)
                if k == 1:
                    tt(pair_sums[:, :, 0:3], grp[:, :, 0:3], grp[:, :, 1:4], ALU.add)
                    tt(pair_sums[:, :, 3:5], grp[:, :, 0:2], grp[:, :, 2:4], ALU.add)
                    last = tt(pair_sums[:, :, 5:6], grp[:, :, 0:1], grp[:, :, 3:4], ALU.add)
                if k == 2:
                    last = red(top_s[:, :], pair_sums[:, :, :], AX.X, ALU.max)
                if k == 3:
                    ts = top_s[:, :].rearrange("p (t g) -> p t g", g=2)
                    tt(in_group[:, :, 0:1], ts[:, :, 0:1], ts[:, :, 1:2], ALU.is_ge)
                    last = tt(in_group[:, :, 1:2], ts[:, :, 0:1], ts[:, :, 1:2], ALU.is_lt)
                if k == 4:
                    last = tt(grp, grp, in_group[:, :, :].rearrange("p t g -> p (t g)").unsqueeze(2)
                              .to_broadcast([P, 2 * NT, E0 // 2]), ALU.mult)
                if k == 5:
                    other = sfc[:, :, :].unsqueeze(2).to_broadcast([P, NT, E0, E0])
                    own = sfc[:, :, :].unsqueeze(3).to_broadcast([P, NT, E0, E0])
                    tt(above[:, :, :, :], other, own, ALU.is_gt)
                    last = tt(ties[:, :, :, :], other, own, ALU.is_ge)
                flat = lambda m: m[:, :, :, :].rearrange("p t e f -> p (t e f)")
                if k == 6:
                    last = tt(flat(ties), flat(ties), cst0("before"), ALU.mult)
                if k == 7:
                    last = tt(flat(above), flat(above), flat(ties), ALU.max)
                if k == 8:
                    last = red(rank[:, :, :], above[:, :, :, :], AX.X, ALU.add)
                if k == 9:
                    last = nc.vector.scalar_tensor_tensor(out=picked[:, :, 0:E0], in0=rank[:, :, :], scalar=1.5,
                                                          in1=score, op0=ALU.is_lt, op1=ALU.mult)
                if k == 10:
                    last = red(gsum[:, :], picked[:, :, :], AX.X, ALU.add)
                if k == 11:
                    last = nc.vector.reciprocal(gsum[:, :], gsum[:, :])
                if k == 12:
                    inverse = gsum[:, :].unsqueeze(2).to_broadcast([P, NT, E0])
                    tt(gate_w[:, :, :], picked[:, :, 0:E0], inverse, ALU.mult)
                    if past(a.i):
                        dve.wait_ge(wT_ps, a.i)
                    last = tt(parts(0), picked[:, :, 0:E0], inverse, ALU.mult)
                if k == 13:
                    tt(gate_r[:, :, :], gate_w[:, :, :], parts(0), ALU.subtract)
                    last = tt(parts(1), gate_w[:, :, :], parts(0), ALU.subtract)
                last.then_inc(gate_step, 1)

            def gating_end(a):
                dve.wait_ge(gate_step, GATING * (a.i + 1))
                nc.vector.tensor_tensor(w3[:, :, 2 * E0:3 * E0], gate_r[:, :, :], w3[:, :, E0:2 * E0], ALU.subtract
                                        ).then_inc(w3_ok, 1)

            def polynomial(a, i, u):
                c, w = UNITS[u]
                t = att[:, a.par, c:c + w]
                dve.wait_ge(sq_ok, 6 * a.i + 4 + i)
                if i == 0:
                    if past(a.i - 1):
                        dve.wait_ge(y_ps, a.i - 1)
                else:
                    dve.wait_ge(poly_ok, POLY * a.i + 3 * (i - 1) + u + 1)
                nc.vector.scalar_tensor_tensor(out=t, in0=fac[:, i, c:c + w], scalar=ERF_FACTORS[i][1],
                                               in1=(t if i else wsc[:, c:c + w]), op0=ALU.add, op1=ALU.mult
                                               ).then_inc(poly_ok, 1)

            def scaled(b, c):
                dve.wait_ge(bc_ps, NC * b.i + c + 1)
                if past(NC * b.i + c - 1):
                    dve.wait_ge(rh_ok, NC * b.i + c - 1)
                nc.vector.tensor_tensor(rw[:, c % 2, :], rr[:, b.par, c, :], BC[c % 2][:, :], ALU.mult
                                        ).then_inc(rw_ok, 1)

            def biased(a, u):
                for kb, c, w in KB:
                    if UNITS[u][0] <= c < UNITS[u][0] + UNITS[u][1]:
                        dve.wait_ge(sim_ps, 4 * a.i + (1, 3, 4)[u])
                        last = nc.vector.scalar_tensor_tensor(
                            out=wsc[:, c:c + w], in0=Z[u % 2][:, c - UNITS[u][0]:c - UNITS[u][0] + w],
                            scalar=1.0 / (S * STD2), in1=bias[:, 0:w], op0=ALU.mult, op1=ALU.add)
                last.then_inc(z_ok, 1)

            def clamp(a, u):
                c, w = UNITS[u]
                dve.wait_ge(z_ok, 3 * a.i + u + 1)
                nc.vector.tensor_scalar(wsc[:, c:c + w], wsc[:, c:c + w], ERF_END, -ERF_END, ALU.min, ALU.max
                                        ).then_inc(clamp_ok, 1)

            def normalise(s, x, tiles):
                dve.wait_ge(rstd_ok, s.i + 1)
                if past(s.i - 1):
                    dve.wait_ge(xT_ps, s.i - 1)
                for t in tiles:
                    last = nc.vector.tensor_scalar(xn[:, s.par, t, :], x[:, t, :], mv[:, t, 0:1], rstd[:, t:t + 1],
                                                   ALU.subtract, ALU.mult)
                if t == NT - 1:
                    last.then_inc(xn_ok, 1)

            def turn(dve, s, on):
                a, b = s.back(1), s.back(2)
                if on[0]:
                    x = resid[:, bass.ds(s.i * S, S)].rearrange("p (t d) -> p t d", d=D)
                    dve.wait_ge(x_in[s.par], 16 * (s.quo + 1))
                    ln_chain.begin(dve, s)
                    for t in range(NT):
                        last = nc.vector.bn_stats(st6[:, t, :], x[:, t, :])
                    ln_chain.step(last)
                    if past(s.i):
                        dve.wait_ge(rstd_ok, s.i)
                        dve.sem_inc(passed, 1)
                    for t in range(NT):
                        last = nc.vector.bn_aggr(mv[:, t, :], st6[:, t, :])
                    ln_chain.last(last)
                    ln_chain.end()
                if on[1]:
                    dve.wait_ge(sigq_ok, a.i + 1)
                    if past(a.i):
                        dve.wait_ge(k_ok, a.i)
                    nc.vector.scalar_tensor_tensor(out=uq[:, :], in0=G[(9 * a.par) % 2][:, :], scalar=prm("bqk"),
                                                   in1=sigq[:, :], op0=ALU.add, op1=ALU.mult).then_inc(uq_ok, 1)
                if on[2]:
                    scaled(b, 0)
                if on[1]:
                    dve.wait_ge(uq_ok, a.i + 1)
                    if past(4 * a.i):
                        dve.wait_ge(sim_ps, 4 * a.i)
                    nc.vector.tensor_scalar(qT[:, :], uq[:, :], prm("gamma0"), prm("beta0"), ALU.mult, ALU.add
                                            ).then_inc(q_ok, 1)
                    dve.wait_ge(v_ps, a.i + 1)
                    if past(a.i):
                        dve.wait_ge(v_ok, a.i)
                    nc.vector.tensor_tensor(vt[:, :], X[:, :], prm("bv"), ALU.add).then_inc(vt_ok, 1)
                if on[2]:
                    scaled(b, 1)
                if on[1]:
                    gating(a, 0)
                if on[0]:
                    normalise(s, x, (0, 1))
                if on[1]:
                    gating(a, 1)
                if on[0]:
                    normalise(s, x, (2, 3))
                if on[1]:
                    gating(a, 2)
                    biased(a, 0)
                    gating(a, 3)
                if on[2]:
                    scaled(b, 2)
                if on[1]:
                    gating(a, 4)
                    biased(a, 1)
                    gating(a, 5)
                if on[2]:
                    scaled(b, 3)
                if on[1]:
                    clamp(a, 0)
                    gating(a, 6)
                    biased(a, 2)
                    gating(a, 7)
                    clamp(a, 1)
                    gating(a, 8)
                    clamp(a, 2)
                    for k in range(9, GATING):
                        gating(a, k)
                    gating_end(a)
                    for u in range(3):
                        polynomial(a, 0, u)
                if on[0]:
                    dve.wait_ge(xT_ps, s.i + 1)
                    if past(8 * (s.i - 1)):
                        dve.wait_ge(hid_ps, 8 * (s.i - 1))
                    nc.vector.tensor_copy(xnT[:, s.par, :], X[:, :]).then_inc(xT_ok, 1)
                if on[1]:
                    for i in (1, 2):
                        for u in range(3):
                            polynomial(a, i, u)
                if on[2]:
                    dve.wait_ge(y_ps, b.i + 1)
                    xb = resid[:, bass.ds(b.i * S, S)]
                    nc.vector.tensor_tensor(xb, xb, Y[:, :], ALU.add).then_inc(x1_ok, 1)
            over_sequences(dve, turn, 2, 3)
            dve.wait_ge(x1_ok, NSEQ)


def layer1(nc, resid, cst, prm, cst1, out_d, scratch, lora_stack, passed):
    QPART, KPART = (0, 0, 0, 1, 1, 2), (0, 1, 2, 0, 1, 0)
    ROWS = 6 * DH
    SCALE = DH ** -0.5
    qk_d, o_d, r_d, ones_d = scratch
    with ExitStack() as ctx:
        sem = lambda n: ctx.enter_context(nc.semaphore("b_" + n))
        sb = lambda n, shape, dt=F32: ctx.enter_context(nc.sbuf_tensor("l1_" + n, shape, dt))
        identf = cst("ident")
        identb = sb("identb", [P, P], BF16)
        mask_qk, mask_kq = sb("mask_qk", [P, P], BF16), sb("mask_kq", [P, P], BF16)
        Q, K = sb("Q", [P, 3, NH // 2, S], BF16), sb("K", [P, 3, NH // 2, S], BF16)
        V = sb("V", [P, 3, NT, NH, 32])
        E = sb("E", [P, 2, 5120])
        xn, xnT = sb("xn", [P, NT, D]), sb("xnT", [P, S])
        rope = sb("rope", [P, 2, 2, S])
        parts, rest = sb("parts", [P, 2, 3, S], BF16), sb("rest", [P, 2, S])
        hid = sb("hid", [P, NC, S])
        LR = E1 * RANK
        low, low_rest = sb("low", [P, NT, LR]), sb("low_rest", [P, NT, LR])
        low_parts, lowT = sb("low_parts", [P, NT, 2, 3, LR], BF16), sb("lowT", [3 * LR, 2, S], BF16)
        gl = sb("gl", [P, 4, NT * E1])
        st6, mv, rstd, halfneg = sb("st6", [P, NT, 6]), sb("mv", [P, NT, 2]), sb("rstd", [P, NT]), sb("halfneg", [P, NT])
        negmax, maxrest = sb("negmax", [P, 3, NT, NH]), sb("maxrest", [P, NT, NH])
        mparts, mT = sb("mparts", [P, NT, 3 * NH], BF16), sb("mT", [3 * NH, S], BF16)
        avs = sb("avs", [P, 2, S])
        heads, denom, recip, normed = (sb("heads", [P, S]), sb("denom", [P, S // 8]), sb("recip", [P, S // 8]),
                                       sb("normed", [P, S]))

        psum = lambda n, shape: ctx.enter_context(nc.psum_tensor("l1_" + n, shape, F32))
        MB, TB = psum("MB", [P, 2, 512]), psum("TB", [P, 2, 512])
        AVB, X, G = psum("AVB", [P, 512]), psum("X", [P, 512]), [psum("G0", [P, 512]), psum("G1", [P, 512])]

        set_ok, dset_ok, rstd_ok, xn_ok = sem("set_ok"), sem("dset_ok"), sem("rstd_ok"), sem("xn_ok")
        xT_ps, xT_ok, q_ps, k_ps, rope_ok, v_ps, v_ok = (sem("xT_ps"), sem("xT_ok"), sem("q_ps"), sem("k_ps"),
                                                         sem("rope_ok"), sem("v_ps"), sem("v_ok"))
        raw_ok, swap_in = sem("raw_ok"), [sem("q_swap_in"), sem("k_swap_in")]
        ga_ps, low_ps, lowT_ok, hid_ps, hid_ok, ffn_ps, ffn_ok = (sem("ga_ps"), sem("low_ps"), sem("lowT_ok"), sem("hid_ps"),
                                                                  sem("hid_ok"), sem("ffn_ps"), sem("ffn_ok"))
        biased_ok = sem("biased_ok")
        mT_ps, mT_ok, m_in = sem("mT_ps"), sem("mT_ok"), sem("m_in")
        m_ps, max_ok = [sem("m_ps0"), sem("m_ps1")], [sem("max_ok0"), sem("max_ok1")]
        t_ps, exp_ok = [sem("t_ps0"), sem("t_ps1")], [sem("exp_ok0"), sem("exp_ok1")]
        av_ps, avs_ok = sem("av_ps"), sem("avs_ok")
        parts_out, stack_in = [sem("q_parts_out"), sem("k_parts_out")], [sem("q_stack_in"), sem("k_stack_in")]
        o_out, o_in, rec_ok, r_out, r_in, normed_ok, wo_ps, x2_ok, stored = (
            [sem("even_o_out"), sem("odd_o_out")], sem("o_in"), sem("rec_ok"), sem("r_out"), sem("r_in"), sem("normed_ok"), sem("wo_ps"),
            sem("x2_ok"), sem("stored"))
        ln_chain, pool_chain = Chain(sem("ln_chain"), 2, passed), Chain(sem("pool_chain"), 1, passed)
        part_chain, top_chain = Chain(sem("part_chain"), 6, passed), Chain(sem("top_chain"), 10, passed)
        max_chain = Chain(sem("max_chain"), 3, passed)
        ones_out, ones_in = sem("ones_out"), sem("ones_in")

        def head(h):
            return slice(64 * (h % 2), 64 * (h % 2) + ROWS), slice(64 * (h % 2), 64 * (h % 2) + ROWS + 3), h // 2

        MUNITS = [[(0, 3, 0, 0), (1, 3, 1, 0)], [(2, 3, 0, 0), (3, 3, 1, 0)],
                  [(0, 2, 0, 0), (0, 0, 0, 384), (1, 2, 1, 0), (1, 0, 1, 384)],
                  [(2, 2, 0, 0), (2, 0, 0, 384), (3, 2, 1, 0), (3, 0, 1, 384)],
                  [(h, 1, h % 2, 256 * (h // 2)) for h in range(4)]]
        TUNITS = [[(h, 0, 0, 0), (h, 1, 1, 0), (h, 3, 1, 384)] for h in range(4)]
        TUNITS.append([(h, 2, h % 2, 256 * (h // 2)) for h in range(4)])
        UN = len(TUNITS)
        ECOL = {(h, kb): unit * 1024 + bank * 512 + col
                for unit, blocks in enumerate(TUNITS) for h, kb, bank, col in blocks}

        LAG = 5
        BEGUN_AT, HIDDEN_AT = {5: 0, 6: 1, 13: 2, 14: 3}, {12: (0, 1), 13: (2,), 14: (3,)}

        def quad_of(j, t, u, on):
            return (t, j - 1, on[3]) if j else (u, 3, on[4])

        def value_quad_of(j, t, u, on):
            return [(u, 2, on[4]), (u, 3, on[4]), (t, 0, on[3]), (t, 1, on[3])][j]

        block = ctx.enter_context(nc.Block())

        @block.sync
        def _(sp):
            sp.wait_ge(dset_ok, 4)
            sp.dma_start(ones_d, parts[0:1, 0, 0, :]).then_inc(ones_out, 16)
            sp.wait_ge(ones_out, 16)
            for half in range(2):
                lo = 64 * half + ROWS
                sp.dma_start(K[lo:lo + 3, :, :, :].rearrange("p b g n -> p (b g) n"),
                             bass.AP(tensor=ones_d.tensor, offset=0, ap=[[0, 3], [0, 3 * NH // 2], [1, S]])
                             ).then_inc(ones_in, 16)

            def turn(sp, s, on):
                a, t, u, v = s.back(1), s.back(3), s.back(4), s.back(5)
                if on[5]:
                    sp.wait_ge(x2_ok, v.i + 1)
                    sp.sem_inc(passed, 1)
                    sp.dma_start(out_d[bass.ds(v.i, 1), :, :].rearrange("s (t p) d -> p (s t) d", p=P),
                                 resid[:, bass.ds(v.i * S, S)].rearrange("p (t d) -> p t d", d=D)).then_inc(stored, 16)
                if on[1]:
                    swap_pairs(sp, a, 0)
                if on[3]:
                    sp.wait_ge(mT_ok, t.i + 1)
                    sp.sem_inc(passed, 1)
                    for half in range(2):
                        lo = 64 * half + ROWS
                        sp.dma_start(Q[lo:lo + 3, t.par, :, :], mT[half:3 * NH:2, :]).then_inc(m_in, 16)
                if on[1]:
                    swap_pairs(sp, a, 1)
                if on[4]:
                    store_heads(sp, u, 2)
                if on[1]:
                    store_parts(sp, a, 0)
                    load_stack(sp, a, 0)
                if on[4]:
                    store_heads(sp, u, 3)
                    for r in range(2):
                        sp.wait_ge(o_out[r], 16 * 2 * (u.i + 1))
                        sp.sem_inc(passed, 1)
                    if past(u.i):
                        sp.wait_ge(normed_ok, u.i)
                        sp.sem_inc(passed, 1)
                    if past(u.i):
                        sp.wait_ge(rec_ok, u.i)
                        sp.sem_inc(passed, 1)
                    o = o_d[u.par].rearrange("(h r) n -> h r n", r=32)
                    sp.dma_start(denom[:, :], o[:, DH, :].rearrange("h (b n) -> h b n", b=8)).then_inc(o_in, 16)
                    sp.dma_start(heads[:, :], o[:, 0:DH, :]).then_inc(o_in, 16)
                if on[1]:
                    store_parts(sp, a, 1)
                if on[4]:
                    sp.wait_ge(rec_ok, u.i + 1)
                    sp.sem_inc(passed, 1)
                    sp.dma_start(r_d[u.par].rearrange("h (b n) -> (h b) n", b=8), recip[:, :]).then_inc(r_out, 16)
                    sp.wait_ge(r_out, 16 * (u.i + 1))
                    sp.sem_inc(passed, 1)
                    if past(u.i):
                        sp.wait_ge(wo_ps, u.i)
                        sp.sem_inc(passed, 1)
                    sp.dma_start(normed[:, :], bass.AP(tensor=r_d.tensor, offset=u.par * NH * S,
                                                       ap=[[S, NH], [0, DH], [1, S]])).then_inc(r_in, 16)
                if on[1]:
                    load_stack(sp, a, 1)
                if on[3]:
                    store_heads(sp, t, 0)
                    store_heads(sp, t, 1)

            def swap_pairs(sp, a, side):
                sp.wait_ge(raw_ok, 2 * a.i + side + 1)
                sp.sem_inc(passed, 1)
                for r in range(2):
                    sp.dma_start(rope[r:P:2, side, 1, :], rope[1 - r:P:2, side, 0, :]).then_inc(swap_in[side], 16)

            def store_parts(sp, a, side):
                sp.wait_ge(part_chain.sem, part_chain.steps * a.i + 3 * (side + 1))
                sp.sem_inc(passed, 1)
                sp.dma_start(qk_d[a.par, side].rearrange("m p n -> p m n"), parts[:, side, :, :]
                             ).then_inc(parts_out[side], 16)

            def load_stack(sp, a, side):
                stack, order = ((Q, QPART), (K, KPART))[side]
                sp.wait_ge(parts_out[side], 16 * (a.i + 1))
                sp.sem_inc(passed, 1)
                if past(UN * 4 * (a.i - 2)):
                    sp.wait_ge(t_ps[1], UN * 4 * (a.i - 2))
                    sp.sem_inc(passed, 1)
                if past(16 * 12 * a.i):
                    sp.wait_ge(stack_in[side], 16 * 12 * a.i)
                    sp.sem_inc(passed, 1)
                for slot, part in enumerate(order):
                    for half in range(2):
                        lo = 64 * half + slot * DH
                        rows = qk_d[a.par, side, part].rearrange("(g f d) n -> f d g n", f=2, d=DH)[half]
                        sp.dma_start(stack[lo:lo + DH, a.par, :, :], rows).then_inc(stack_in[side], 16)

            def store_heads(sp, seq, q):
                sp.wait_ge(avs_ok, 4 * seq.i + q + 1)
                sp.sem_inc(passed, 1)
                sp.dma_start(o_d[seq.par, q * P:(q + 1) * P, :], avs[:, q % 2, :]).then_inc(o_out[q % 2], 16)

            over_sequences(sp, turn, 3, LAG + 1)
            sp.wait_ge(stored, 16 * NSEQ)

        @block.gpsimd
        def _(pool):
            nc.gpsimd.memset(halfneg[:, :], -0.5).then_inc(set_ok, 1)
            nc.gpsimd.memset(V[:, :, :, :, :], 0.0).then_inc(set_ok, 1)
            pool.wait_ge(set_ok, 2)
            nc.gpsimd.memset(V[:, :, :, :, DH:DH + 1], 1.0).then_inc(set_ok, 1)
            pool.wait_ge(set_ok, 3)
            pool.wait_ge(ones_out, 16)

            def split(a, side):
                r0, r1, part = rope[:, side, 0, :], rope[:, side, 1, :], lambda k: parts[:, side, k, :]
                pool.wait_ge(swap_in[side], 32 * (a.i + 1))
                pool.sem_inc(passed, 1)
                x = rope[:, side, :, :].rearrange("p c n -> p (c n)")
                nc.gpsimd.tensor_tensor(x, x, cst1.tile[:, 0:2 * S], ALU.mult).then_inc(rope_ok, 1)
                pool.wait_ge(rope_ok, 2 * a.i + side + 1)
                pool.sem_inc(passed, 1)
                if past(16 * a.i):
                    pool.wait_ge(parts_out[side], 16 * a.i)
                ch, tt = part_chain, nc.gpsimd.tensor_tensor
                tt(part(0), r0, r1, ALU.add)
                ch.step(tt(rest[:, 0, :], r0, r1, ALU.add))
                tt(part(1), rest[:, 0, :], part(0), ALU.subtract)
                ch.step(tt(rest[:, 1, :], rest[:, 0, :], part(0), ALU.subtract))
                ch.last(tt(part(2), rest[:, 1, :], part(1), ALU.subtract))

            def split_max(t):
                ch, nm, tt = max_chain, negmax[:, t.par, :, :], nc.gpsimd.tensor_tensor
                ch.begin(pool, t)
                pool.wait_ge(max_ok[1], UN * 4 * (t.i + 1))
                pool.sem_inc(passed, 1)
                if past(t.i):
                    pool.wait_ge(mT_ps, t.i)
                    pool.sem_inc(passed, 1)
                ch.step(nc.gpsimd.tensor_scalar(mparts[:, :, 0:NH], nm, 1.0, None, ALU.mult))
                tt(mparts[:, :, NH:2 * NH], nm, mparts[:, :, 0:NH], ALU.subtract)
                ch.step(tt(maxrest[:, :, :], nm, mparts[:, :, 0:NH], ALU.subtract))
                ch.last(tt(mparts[:, :, 2 * NH:3 * NH], maxrest[:, :, :], mparts[:, :, NH:2 * NH], ALU.subtract))
                ch.end()

            def turn(pool, s, on):
                a, t, u = s.back(1), s.back(3), s.back(4)
                if on[3]:
                    split_max(t)
                if on[1]:
                    part_chain.begin(pool, a)
                    split(a, 0)
                if on[1]:
                    split(a, 1)
                    part_chain.end()
                    x = resid[:, bass.ds(a.i * S, S)]
                    pool.wait_ge(xn_ok, a.i + 1)
                    nc.gpsimd.tensor_tensor(x, x, prm("wo_b"), ALU.add).then_inc(biased_ok, 1)
                if on[0]:
                    pool.wait_ge(ln_chain.sem, 2 * (s.i + 1))
                    pool.sem_inc(passed, 1)
                    pool_chain.begin(pool, s)
                    pool_chain.step(nc.gpsimd.tensor_scalar(rstd[:, :], mv[:, :, 1], EPS, None, ALU.add))
                    nc.gpsimd.tensor_tensor(rstd[:, :], rstd[:, :], halfneg[:, :], ALU.pow).then_inc(rstd_ok, 1)
                    pool_chain.end()
                if on[4]:
                    pool.wait_ge(o_in, 32 * (u.i + 1))
                    pool.wait_ge(r_in, 16 * (u.i + 1))
                    nc.gpsimd.tensor_tensor(normed[:, :], heads[:, :], normed[:, :], ALU.mult).then_inc(normed_ok, 1)
            over_sequences(pool, turn, 3, LAG)

        @block.scalar
        def _(act):
            def turn(act, s, on):
                a, t, u = s.back(1), s.back(3), s.back(4)
                for k in range(4 * UN):
                    j, n = divmod(k, UN)
                    seq, q, live = quad_of(j, t, u, on)
                    if live:
                        for bank in range(2):
                            act.wait_ge(t_ps[bank], UN * (4 * seq.i + q) + n + 1)
                            if n == 0 and bank == 0:
                                if past(4 * seq.i + q - 1):
                                    act.wait_ge(av_ps, 4 * seq.i + q - 1)
                            lo = 1024 * n + 512 * bank
                            nc.scalar.activation(E[:, j % 2, lo:lo + 512], TB[:, bank, :], ACT.Exp, scale=SCALE
                                                 ).then_inc(exp_ok[bank], 1)
                    if k == 0 and on[1]:
                        act.wait_ge(xT_ps, a.i + 1)
                        if past(NC * a.i):
                            act.wait_ge(hid_ps, NC * a.i)
                        nc.scalar.activation(xnT[:, :], X[:, :], ACT.Copy).then_inc(xT_ok, 1)
                    if k == 2 and on[3]:
                        act.wait_ge(mT_ps, t.i + 1)
                        if past(32 * t.i):
                            act.wait_ge(m_in, 32 * t.i)
                        nc.scalar.activation(mT[:, :], X[0:3 * NH, 0:S // 2].bitcast(BF16), ACT.Copy).then_inc(mT_ok, 1)
                    if k in (2, 3) and on[1]:
                        side = k - 2
                        act.wait_ge((q_ps, k_ps)[side], a.i + 1)
                        if past(part_chain.steps * a.i):
                            act.wait_ge(part_chain.sem, part_chain.steps * a.i)
                        nc.scalar.activation(rope[:, side, 0, :], G[side][:, :], ACT.Copy).then_inc(raw_ok, 1)
                    if k == 10 and on[1]:
                        act.wait_ge(low_ps, a.i + 1)
                        nc.scalar.activation(lowT[:, :, :].rearrange("p g n -> p (g n)"), X[0:3 * LR, :].bitcast(BF16),
                                             ACT.Copy).then_inc(lowT_ok, 1)
                    for c in HIDDEN_AT.get(k, ()) if on[1] else ():
                        act.wait_ge(hid_ps, NC * a.i + c + 1)
                        if past(a.i):
                            act.wait_ge(ffn_ps, a.i)
                        nc.scalar.activation(hid[:, c, :], G[c % 2][:, :], ACT.Relu, bias=prm("wi_b")[:, c:c + 1]
                                             ).then_inc(hid_ok, 1)
                    if n == 4:
                        seq, q, live = value_quad_of(j, t, u, on)
                        if live:
                            act.wait_ge(av_ps, 4 * seq.i + q + 1)
                            if past(16 * (2 * seq.i + q // 2)):
                                act.wait_ge(o_out[q % 2], 16 * (2 * seq.i + q // 2))
                            nc.scalar.activation(avs[:, q % 2, :], AVB[:, :], ACT.Copy).then_inc(avs_ok, 1)
            over_sequences(act, turn, 3, LAG)

        @block.tensor
        def _(pe):
            pe.wait_ge(set_ok, 3)
            pe.wait_ge(dset_ok, 4)
            pe.wait_ge(ones_in, 32)

            def maxima(m, j, n, bank):
                if j == 0 and n == 0 and bank == 0:
                    pe.wait_ge(stack_in[0], 16 * 12 * (m.i + 1))
                    pe.wait_ge(stack_in[1], 16 * 12 * (m.i + 1))
                if past(UN * (4 * m.i + j) + n):
                    pe.wait_ge(max_ok[bank], UN * (4 * m.i + j) + n)
                for h, qt, b, lo in MUNITS[n]:
                    if b == bank:
                        rows, _, g = head(4 * j + h)
                        w = (qt + 1) * P
                        pe.matmul(MB[:, bank, lo:lo + w], Q[rows, m.par, g, qt * P:w], K[rows, m.par, g, 0:w],
                                  start=True, stop=False)
                        mm = pe.matmul(MB[:, bank, lo + qt * P:lo + w], identb[:, :], mask_qk[:, :], start=False, stop=True)
                mm.then_inc(m_ps[bank], 1)

            def scores(t, q, n, bank):
                if n == 0 and bank == 0:
                    pe.wait_ge(m_in, 32 * (t.i + 1))
                if past(UN * (4 * t.i + q) + n):
                    pe.wait_ge(exp_ok[bank], UN * (4 * t.i + q) + n)
                for h, kb, b, lo in TUNITS[n]:
                    if b == bank:
                        _, rows, g = head(4 * q + h)
                        w = S - kb * P
                        pe.matmul(TB[:, bank, lo:lo + w], K[rows, t.par, g, kb * P:(kb + 1) * P],
                                  Q[rows, t.par, g, kb * P:S], start=True, stop=False)
                        mm = pe.matmul(TB[:, bank, lo:lo + P], identb[:, :], mask_kq[:, :], start=False, stop=True)
                mm.then_inc(t_ps[bank], 1)

            def values(t, q, kb, buf):
                if kb == 0:
                    if past(UN * (4 * t.i + q + 1)):
                        pe.wait_ge(exp_ok[1], UN * (4 * t.i + q + 1))
                    if past(4 * t.i + q):
                        pe.wait_ge(avs_ok, 4 * t.i + q)
                    pe.wait_ge(v_ok, t.i + 1)
                w = S - kb * P
                for h in range(4):
                    c = ECOL[(h, kb)]
                    mm = pe.matmul(AVB[32 * h:32 * h + 32, kb * P:S], V[:, t.par, kb, 4 * q + h, :], E[:, buf, c:c + w],
                                   start=(kb == 0), stop=(kb == NT - 1))
                if kb == NT - 1:
                    mm.then_inc(av_ps, 1)

            def general(k, a, t, u, on):
                if k == 0 and on[1]:
                    pe.wait_ge(xn_ok, a.i + 1)
                    if past(a.i):
                        pe.wait_ge(ffn_ok, a.i)
                    for i in range(NT):
                        mm = pe.transpose(X[:, i * P:(i + 1) * P], xn[:, i, :], identf)
                    mm.then_inc(xT_ps, 1)
                if k == 2 and on[3]:
                    pe.wait_ge(max_chain.sem, max_chain.steps * (t.i + 1))
                    pe.sem_inc(passed, 1)
                    if on[1]:
                        pe.wait_ge(xT_ok, a.i + 1)
                        pe.sem_inc(passed, 1)
                    pe.wait_ge(ffn_ok, 1)
                    pe.sem_inc(passed, 1)
                    for i in range(NT):
                        mm = pe.transpose(X[0:3 * NH, 0:S // 2].bitcast(BF16)[:, i * P:(i + 1) * P], mparts[:, i, :],
                                          identb[:, :])
                    mm.then_inc(mT_ps, 1)
                if k == 2 and on[1]:
                    pe.wait_ge(xT_ok, a.i + 1)
                    if past(NC * a.i):
                        pe.wait_ge(hid_ok, NC * a.i)
                    if past(a.i - 3):
                        pe.wait_ge(x2_ok, a.i - 3)
                    pe.matmul(G[0][:, :], prm("wq"), xnT[:, :], start=True, stop=True).then_inc(q_ps, 1)
                if k == 3 and on[1]:
                    pe.matmul(G[1][:, :], prm("wk"), xnT[:, :], start=True, stop=True).then_inc(k_ps, 1)
                if k == 4 and on[1]:
                    if on[3]:
                        pe.wait_ge(mT_ok, t.i + 1)
                    for i in range(NT):
                        mm = pe.matmul(X[:, i * 40:(i + 1) * 40], xnT[:, i * P:(i + 1) * P], prm("ga"),
                                       start=True, stop=True)
                    mm.then_inc(ga_ps, 1)
                if k == 10 and on[1]:
                    pe.wait_ge(top_chain.sem, top_chain.steps * (a.i + 1))
                    pe.sem_inc(passed, 1)
                    for i in range(NT):
                        for group in range(2):
                            lo = group * S + i * P
                            mm = pe.transpose(X[0:3 * LR, :].bitcast(BF16)[:, lo:lo + P],
                                              low_parts[:, i, group, :, :].rearrange("p s r -> p (s r)"), identb[:, :])
                    mm.then_inc(low_ps, 1)
                if k in BEGUN_AT and on[1]:
                    c = BEGUN_AT[k]
                    if c < 2:
                        pe.wait_ge(raw_ok, 2 * a.i + c + 1)
                    else:
                        if past(NC * a.i + c - 1):
                            pe.wait_ge(hid_ok, NC * a.i + c - 1)
                    pe.matmul(G[c % 2][:, :], prm("wi")[:, c * P:(c + 1) * P], xnT[:, :], start=True, stop=False)
                for c in HIDDEN_AT.get(k, ()) if on[1] else ():
                    if c == 0:
                        pe.wait_ge(lowT_ok, a.i + 1)
                    for group in range(2):
                        mm = pe.matmul(G[c % 2][:, :], lora_stack[:, group, c * P:(c + 1) * P], lowT[:, group, :],
                                       start=False, stop=(group == 1))
                    mm.then_inc(hid_ps, 1)
                if k == 15 and on[1]:
                    pe.wait_ge(lowT_ok, a.i + 1)
                    for i in range(NT):
                        mm = pe.matmul(X[:, i * P:(i + 1) * P], xnT[:, i * P:(i + 1) * P], prm("wv"),
                                       start=True, stop=True)
                    mm.then_inc(v_ps, 1)
                for i in {17: (0, 1), 18: (2, 3)}.get(k, ()) if on[1] else ():
                    if i == 0:
                        pe.wait_ge(hid_ok, NC * (a.i + 1))
                        pe.wait_ge(v_ok, a.i + 1)
                    for c in range(NC):
                        mm = pe.matmul(X[:, i * P:(i + 1) * P], hid[:, c, i * P:(i + 1) * P],
                                       prm("wof")[:, c * D:(c + 1) * D], start=(c == 0), stop=(c == NC - 1))
                    if i == NT - 1:
                        mm.then_inc(ffn_ps, 1)
                if k == 19 and on[4]:
                    pe.wait_ge(normed_ok, u.i + 1)
                    if on[1]:
                        pe.wait_ge(hid_ok, NC * (a.i + 1))
                    for i in range(NT):
                        mm = pe.matmul(G[0][:, i * P:(i + 1) * P], normed[:, i * P:(i + 1) * P], prm("wo"),
                                       start=True, stop=True)
                    mm.then_inc(wo_ps, 1)

            def turn(pe, s, on):
                a, m, t, u = s.back(1), s.back(2), s.back(3), s.back(4)
                for k in range(4 * UN):
                    j, n = divmod(k, UN)
                    seq, q, live = quad_of(j, t, u, on)
                    if on[2]:
                        maxima(m, j, n, 0)
                    if live:
                        scores(seq, q, n, 0)
                    general(k, a, t, u, on)
                    if on[2]:
                        maxima(m, j, n, 1)
                    if live:
                        scores(seq, q, n, 1)
                    if n > 0:
                        seq, q, live = value_quad_of(j, t, u, on)
                        if live:
                            values(seq, q, n - 1, (j + 1) % 2)
            over_sequences(pe, turn, 3, LAG)

        @block.vector
        def _(dve):
            nc.vector.memset(parts[0:1, 0, 0, :], 1.0).then_inc(dset_ok, 1)
            nc.vector.tensor_copy(identb[:, :], identf).then_inc(dset_ok, 1)
            nc.vector.tensor_copy(mask_qk[:, :], cst1("mask_qk")).then_inc(dset_ok, 1)
            nc.vector.tensor_copy(mask_kq[:, :], cst1("mask_kq")).then_inc(dset_ok, 1)
            dve.wait_ge(set_ok, 3)

            def rowmax(m, j, n, bank):
                dve.wait_ge(m_ps[bank], UN * (4 * m.i + j) + n + 1)
                if j == 0 and n == 0:
                    if past(max_chain.steps * (m.i - 2)):
                        dve.wait_ge(max_chain.sem, max_chain.steps * (m.i - 2))
                red = nc.vector.tensor_reduce
                h = 4 * j + 2 * (n % 2) + bank
                if n < 2:
                    last = red(negmax[:, m.par, 3, h:h + 1], MB[:, bank, :], AX.X, ALU.max, negate=True)
                elif n < 4:
                    red(negmax[:, m.par, 2, h:h + 1], MB[:, bank, 0:384], AX.X, ALU.max, negate=True)
                    last = red(negmax[:, m.par, 0, h:h + 1], MB[:, bank, 384:512], AX.X, ALU.max, negate=True)
                else:
                    last = red(negmax[:, m.par, 1, 4 * j:4 * j + 4].rearrange("p (h b) -> p b h", b=2)[:, bank, :],
                               MB[:, bank, :].rearrange("p (h n) -> p h n", n=256), AX.X, ALU.max, negate=True)
                last.then_inc(max_ok[bank], 1)

            def top1(a, stage):
                ch, tt = top_chain, nc.vector.tensor_tensor
                te = lambda k: gl[:, k, :].rearrange("p (t e) -> p t e", e=E1)
                per_t = gl[:, 3, 0:NT].unsqueeze(2).to_broadcast([P, NT, E1])
                ga = X[:, 0:NT * 40].rearrange("p (t c) -> p t c", c=40)
                if stage == 0:
                    ch.begin(dve, a)
                    dve.wait_ge(ga_ps, a.i + 1)
                    ch.step(tt(te(0), ga[:, :, 0:E1], prm("gate_b").rearrange("p (t e) -> p t e", e=E1), ALU.add))
                    ch.step(nc.vector.tensor_reduce(gl[:, 3, 0:NT], te(0), AX.X, ALU.max))
                    ch.step(tt(te(1), te(0), per_t, ALU.is_equal))
                if stage == 1:
                    ch.step(tt(te(1), te(1), cst("order").rearrange("p (t e) -> p t e", e=E1), ALU.mult))
                    ch.step(nc.vector.tensor_reduce(gl[:, 3, 0:NT], te(1), AX.X, ALU.max))
                if stage == 2:
                    ch.step(tt(te(2), te(1), per_t, ALU.is_equal))
                    ch.step(tt(low[:, :, :].rearrange("p t (e r) -> p t e r", r=RANK),
                               ga[:, :, E1:40].rearrange("p t (e r) -> p t e r", r=RANK),
                               te(2).unsqueeze(3).to_broadcast([P, NT, E1, RANK]), ALU.mult))
                if stage == 3:
                    if past(a.i):
                        dve.wait_ge(low_ps, a.i)
                    part = lambda group, slot: low_parts[:, :, group, slot, :]
                    for slot in range(1, 3):
                        nc.vector.tensor_copy(part(0, slot), low[:, :, :])
                    ch.step(nc.vector.tensor_copy(part(0, 0), low[:, :, :]))
                if stage == 4:
                    part = lambda group, slot: low_parts[:, :, group, slot, :]
                    for slot in range(2):
                        tt(part(1, slot), low[:, :, :], part(0, 0), ALU.subtract)
                    ch.step(tt(low_rest[:, :, :], low[:, :, :], part(0, 0), ALU.subtract))
                    ch.last(tt(part(1, 2), low_rest[:, :, :], part(1, 0), ALU.subtract))
                    ch.end()

            def turn(dve, s, on):
                a, m, u = s.back(1), s.back(2), s.back(4)
                if on[0]:
                    x = resid[:, bass.ds(s.i * S, S)].rearrange("p (t d) -> p t d", d=D)
                for k in range(4 * UN):
                    if on[2]:
                        rowmax(m, *divmod(k, UN), 0)
                        rowmax(m, *divmod(k, UN), 1)
                    if k == 10 and on[0]:
                        ln_chain.begin(dve, s)
                        for t in range(NT):
                            last = nc.vector.bn_stats(st6[:, t, :], x[:, t, :])
                        ln_chain.step(last)
                    if k == 11 and on[0]:
                        if past(s.i):
                            dve.wait_ge(rstd_ok, s.i)
                            dve.sem_inc(passed, 1)
                        for t in range(NT):
                            last = nc.vector.bn_aggr(mv[:, t, :], st6[:, t, :])
                        ln_chain.last(last)
                        ln_chain.end()
                    if k == 15 and on[1]:
                        dve.wait_ge(v_ps, a.i + 1)
                        if past(4 * (a.i - 2)):
                            dve.wait_ge(av_ps, 4 * (a.i - 2))
                        nc.vector.tensor_copy(V[:, a.par, :, :, 0:DH],
                                              X[:, :].rearrange("p (t h d) -> p t h d", t=NT, d=DH)).then_inc(v_ok, 1)
                    if 4 <= k < 9 and on[1]:
                        top1(a, k - 4)
                    if k == 14 and on[4]:
                        dve.wait_ge(o_in, 32 * (u.i + 1))
                        if past(16 * u.i):
                            dve.wait_ge(r_out, 16 * u.i)
                        nc.vector.reciprocal(recip[:, :], denom[:, :]).then_inc(rec_ok, 1)
                    if k in (16, 17) and on[0]:
                        dve.wait_ge(rstd_ok, s.i + 1)
                        if past(s.i):
                            dve.wait_ge(xT_ps, s.i)
                        for t in ((0, 1), (2, 3))[k - 16]:
                            last = nc.vector.tensor_scalar(xn[:, t, :], x[:, t, :], mv[:, t, 0:1], rstd[:, t:t + 1],
                                                           ALU.subtract, ALU.mult)
                        if k == 17:
                            last.then_inc(xn_ok, 1)
                    if k == 18 and on[1]:
                        xa = resid[:, bass.ds(a.i * S, S)]
                        dve.wait_ge(ffn_ps, a.i + 1)
                        dve.wait_ge(biased_ok, a.i + 1)
                        nc.vector.tensor_tensor(xa, xa, X[:, :], ALU.add).then_inc(ffn_ok, 1)
                    if k == 19 and on[4]:
                        xu = resid[:, bass.ds(u.i * S, S)]
                        dve.wait_ge(wo_ps, u.i + 1)
                        dve.wait_ge(ffn_ok, u.i + 1)
                        nc.vector.tensor_tensor(xu, xu, G[0][:, :], ALU.add).then_inc(x2_ok, 1)
            over_sequences(dve, turn, 3, LAG)


class Fields:

    def __init__(self, tile, dram, fields):
        self.tile, self.dram = tile, dram
        self.at, _ = offsets(fields)

    def __call__(self, name):
        a, w = self.at[name]
        return self.tile[:, a:a + w]


def program(nc, x_d, prm0_d, cst0_d, cst_d, prm1_d, cst1_d, out_d):
    passed = nc.alloc_semaphore("waits_passed")
    skew_d = nc.dram_tensor("bias_skew", (P, BIASW), F32)
    scratch = (nc.dram_tensor("qk_parts", (3, 2, 3, P, S), BF16).ap(), nc.dram_tensor("head_rows", (3, NH * 32, S), F32).ap(), nc.dram_tensor("recip_rows", (3, NH, S), F32).ap(),
               nc.dram_tensor("ones_row", (1, S), BF16).ap())
    with ExitStack() as ctx:
        def fields(name, dram, table):
            _, w = offsets(table)
            return Fields(ctx.enter_context(nc.sbuf_tensor(name, [P, w], F32)), dram, table)

        resid = ctx.enter_context(nc.sbuf_tensor("resid", [P, NSEQ * S], F32))
        cst = fields("consts_sb", cst_d, CONSTS)
        prm1, cst1 = fields("params1_sb", prm1_d, PARAMS1), fields("consts1_sb", cst1_d, CONSTS1)
        lora_stack = ctx.enter_context(nc.sbuf_tensor("lora_stack", [3 * E1 * RANK, 2, HID], BF16))
        layer0(nc, resid, x_d, prm0_d, cst0_d, cst, skew_d, (prm1, cst1), lora_stack, passed)
        layer1(nc, resid, cst, prm1, cst1, out_d, scratch, lora_stack, passed)


def pack(np, fields, values, rows=P):
    at, width = offsets(fields)
    out = np.zeros((rows, width), np.float32)
    for name, (a, w) in at.items():
        val = values[name]
        out[0:val.shape[0], a:a + w] = val
    return out


def layout0(np, v):
    col = lambda a: a.reshape(-1, 1)
    tiled = lambda a, n: np.broadcast_to(np.tile(a, n), (P, n * a.size))
    chunks = lambda a: a.reshape(NC, P, -1).transpose(1, 0, 2).reshape(P, -1)
    return pack(np, PARAMS0, {
        "wqk": v["L0_attn_wqk"], "wv": v["L0_attn_wv"], "bqk": col(v["L0_attn_bqk"]),
        "gamma0": col(v["L0_attn_gamma"][0]), "gamma1": col(v["L0_attn_gamma"][1]),
        "beta0": col(v["L0_attn_beta"][0]), "beta1": col(v["L0_attn_beta"][1]),
        "bv": tiled(v["L0_attn_bv"], NT), "gate": v["L0_ffn_gate"].T, "corr": tiled(v["L0_ffn_corr_bias"], NT),
        "up": v["L0_ffn_up_w"].T, "down": chunks(v["L0_ffn_down_w"].T),
        "fc1": v["L0_ffn_fc1_w"], "w1": v["L0_ffn_w1"].transpose(2, 0, 1).reshape(LAT, HID),
        "w2": v["L0_ffn_w2"].transpose(1, 0, 2).reshape(LAT, HID), "fc2": v["L0_ffn_fc2_w"].T,
        "table": col(v["L0_attn_rel_bias"]),
        "lora_b": np.tile(v["L1_ffn_lora_B"].transpose(0, 2, 1).reshape(E1 * RANK, HID), (3, 1)),
    })


def layout1(np, v):
    col = lambda a: a.reshape(-1, 1)
    tiled = lambda a, n: np.broadcast_to(np.tile(a, n), (P, n * a.size))
    chunks = lambda a: a.reshape(NC, P, -1).transpose(1, 0, 2).reshape(P, -1)
    A = v["L1_ffn_lora_A"].reshape(E1 * RANK, D)
    return pack(np, PARAMS1, {
        "wq": v["L1_attn_Wq"].T, "wk": v["L1_attn_Wk"].T,
        "wv": v["L1_attn_Wv"].T, "wo": v["L1_attn_Wo"].T,
        "ga": np.concatenate([v["L1_ffn_gate_W"], A]).T, "gate_b": tiled(v["L1_ffn_gate_b"], NT),
        "wi": v["L1_ffn_wi_W"].T, "wi_b": v["L1_ffn_wi_b"].reshape(NC, P).T, "wof": chunks(v["L1_ffn_wo_W"].T),
        "wo_b": tiled(v["L1_ffn_wo_b"], NT),
    })


def constants(np):
    exact = BUCKETS // 2
    n = np.maximum(np.arange(BIASW) - (P - 1), 0)
    far = exact + (np.log(np.maximum(n, 1).astype(np.float32) / exact) / np.log(P / exact) * (BUCKETS - exact)).astype(np.int32)
    bucket = np.where(n < exact, n, np.minimum(far, BUCKETS - 1))
    hot = (np.arange(BUCKETS)[:, None] == bucket[None, :]).astype(np.float32)
    r, h = np.arange(3 * E0)[:, None], np.arange(HID)[None, :]
    sel = (h // LAT == r % E0).astype(np.float32)
    e = np.arange(E0)
    before = np.broadcast_to(np.tile((e[None, :] < e[:, None]).reshape(-1), NT), (P, NT * E0 * E0))
    c0 = pack(np, CONSTS0, {"hot": hot, "sel": sel, "ones": np.ones((P, P), np.float32), "before": before})
    c = pack(np, CONSTS, {"ident": np.eye(P, dtype=np.float32),
                          "order": np.broadcast_to(np.tile(np.arange(E0, 0, -1), NT), (P, NT * E0))})
    freq = (1.0 / np.float32(10000.0) ** (np.arange(0, DH, 2, dtype=np.float32) / DH)).astype(np.float32)
    angle = np.tile(np.repeat(freq, 2), NH)[:, None] * np.arange(S, dtype=np.float32)[None, :]
    sign = np.tile(np.array([-1.0, 1.0], np.float32), D // 2)[:, None]
    i = np.arange(P)
    c1 = pack(np, CONSTS1, {"cos": np.cos(angle), "sin": np.sin(angle) * sign,
                            "mask_qk": np.where(i[None, :] > i[:, None], MASKED, 0.0),
                            "mask_kq": np.where(i[None, :] < i[:, None], MASKED, 0.0)})
    return c0, c, c1


def kernel(**inputs):
    import numpy as np
    import concourse.bacc as bacc
    from concourse.bass_utils import run_bass_kernel_spmd

    v = {n: np.asarray(a) for n, a in inputs.items()}
    c0, c, c1 = constants(np)
    arrays = {"x": np.ascontiguousarray(v["L0_attn_x"]), "params0": layout0(np, v), "consts0": c0, "consts": c,
              "params1": layout1(np, v), "consts1": c1}
    nc = bacc.Bacc("TRN2", target_bir_lowering=False, num_devices=1)
    args = [nc.dram_tensor(n, a.shape, F32, kind="ExternalInput").ap() for n, a in arrays.items()]
    out = nc.dram_tensor("out", (NSEQ, S, D), F32, kind="ExternalOutput").ap()
    program(nc, *args, out)
    r = run_bass_kernel_spmd(nc, [arrays], core_ids=[0])
    return r.results[0]["out"]
```
